# Optimizing a Trainium2 kernel written in Bass

```python
import numpy as np
import jax
import jax.numpy as jnp

def _softmax(x, axis=-1):
    return jax.nn.softmax(x, axis=axis)

def _gelu(x):
    return jax.nn.gelu(x, approximate=True)

def _silu(x):
    return jax.nn.silu(x)

def _sigmoid(x):
    return jax.nn.sigmoid(x)

def _layernorm(x, axis=-1, eps=1e-05):
    m = jnp.mean(x, axis=axis, keepdims=True)
    v = jnp.var(x, axis=axis, keepdims=True)
    return (x - m) / jnp.sqrt(v + eps)

def _scatter_add(tgt, idx, src, axis=0):
    return tgt.at[idx].add(src)

def _segment_sum(src, seg, n):
    return jax.ops.segment_sum(src, seg, n)
kernel_name = 'mk_gnn_resnorm_d2_gnn_r8_7307f8'

def setup_inputs(seed: int=0):
    np.random.seed(seed)
    _w = jnp.asarray

    def _rec_inputs():
        import jax
        import jax.numpy as jnp
        _gk = jax.random.key(seed)
        x = -0.0005121 + 1.001 * jax.random.normal(jax.random.fold_in(_gk, 1), (12500, 160), jnp.float32)
        src = jax.random.randint(jax.random.fold_in(_gk, 2), (200000,), 0, 12500, jnp.int32)
        dst = jnp.minimum((12500 * jax.random.uniform(jax.random.fold_in(_gk, 3), (200000,)) ** 2.0).astype(jnp.int32), 99999)
        _o = jnp.argsort(dst, stable=True)
        src = src[_o]
        dst = dst[_o]
        edge_attr_16 = jax.random.uniform(jax.random.fold_in(_gk, 12), (200000, 16), jnp.float32, 0.0, 1)
        edge_attr_4 = 0.000898722 + 1.00012 * jax.random.normal(jax.random.fold_in(_gk, 13), (200000, 4), jnp.float32)
        node_vec1 = jax.random.uniform(jax.random.fold_in(_gk, 15), (12500, 1), jnp.float32, 0.0, 1)
        return (x, src, dst, edge_attr_16, edge_attr_4, node_vec1)
    x, src, dst, edge_attr_16, edge_attr_4, node_vec1 = _rec_inputs()

    def _L0_gnn_setup():
        import jax, jax.numpy as jnp
        import numpy as np
        N, E = (2500, 40000)
        CS, CV = (64, 32)
        AS_, AV, H = (16, 8, 4)
        NB = 16
        SQRT3 = 1.7320508075688772
        SQRT2 = 1.4142135623730951
        EPS = 1e-05

        def _cg_tp(s, v, y0, y1, w_ss, w_sv, w_vs, w_vv0, w_vv1):
            out_s = jnp.concatenate([w_ss * s * y0[:, None], w_vv0 * (jnp.einsum('eci,ei->ec', v, y1) / SQRT3)], axis=-1)
            out_v = jnp.concatenate([(w_sv * s)[:, :, None] * y1[:, None, :], (w_vs * jnp.ones_like(v[..., 0]))[..., None] * v * y0[:, None, None], (w_vv1 * jnp.ones_like(v[..., 0]))[..., None] * (jnp.cross(v, y1[:, None, :]) / SQRT2)], axis=1)
            return (out_s, out_v)

        def _equiv_layernorm(s, v, gamma_s, beta_s, gamma_v):
            mu = jnp.mean(s, axis=-1, keepdims=True)
            var = jnp.var(s, axis=-1, keepdims=True)
            s_n = (s - mu) * jax.lax.rsqrt(var + EPS) * gamma_s + beta_s
            rms = jnp.sqrt(jnp.mean(jnp.sum(v * v, axis=-1), axis=-1, keepdims=True) + EPS)
            v_n = v / rms[..., None] * gamma_v[None, :, None]
            return (s_n, v_n)
        key = jax.random.key(seed)
        ks = jax.random.split(key, 26)

        def rn(k, shape, fan):
            return jax.random.normal(k, shape, jnp.float32) / np.sqrt(fan)
        D1S, D1V = (CS + CV, CS + 2 * CV)
        WN = 2 * CS + 3 * CV
        inp = {'node': jax.random.normal(ks[0], (N, CS + 3 * CV), jnp.float32), 'edge_index': jax.random.randint(ks[1], (2, E), 0, N, jnp.int64 if jax.config.jax_enable_x64 else jnp.int32), 'rbf': jax.random.uniform(ks[2], (E, NB), jnp.float32), 'rsh': jax.random.normal(ks[3], (E, 4), jnp.float32), 'gamma_s': jnp.ones((CS,), jnp.float32), 'beta_s': jnp.zeros((CS,), jnp.float32), 'gamma_v': jnp.ones((CV,), jnp.float32), 'Ws_src': rn(ks[4], (CS, CS), CS), 'Wv_src': rn(ks[5], (CV, CV), CV), 'Ws_dst': rn(ks[6], (CS, CS), CS), 'Wv_dst': rn(ks[7], (CV, CV), CV), 'W_rbf': rn(ks[8], (NB, WN), NB), 'W_alpha': rn(ks[9], (D1S, H * AS_), D1S), 'alpha_dot': rn(ks[10], (1, H, AS_), AS_), 'Ws_val': rn(ks[11], (D1S, CS), D1S), 'Wv_val': rn(ks[12], (D1V, CV), D1V), 'Wg': rn(ks[13], (CS, CV), CS), 'w2_ss': rn(ks[14], (CS,), 1), 'w2_sv': rn(ks[15], (CS,), 1), 'w2_vs': rn(ks[16], (CV,), 1), 'w2_vv0': rn(ks[17], (CV,), 1), 'w2_vv1': rn(ks[18], (CV,), 1), 'Ws_vlin': rn(ks[19], (D1S, H * AS_), D1S), 'Wv_vlin': rn(ks[20], (D1V, H * AV), D1V), 'Wps': rn(ks[21], (H * AS_, CS), H * AS_), 'Wpv': rn(ks[22], (H * AV, CV), H * AV)}
        return inp
    _L0_gnn_all = _L0_gnn_setup()
    _L0_gnn_in = {k: v for k, v in _L0_gnn_all.items() if k in ('gamma_s', 'beta_s', 'gamma_v', 'Ws_src', 'Wv_src', 'Ws_dst', 'Wv_dst', 'W_rbf', 'W_alpha', 'alpha_dot', 'Ws_val', 'Wv_val', 'Wg', 'w2_ss', 'w2_sv', 'w2_vs', 'w2_vv0', 'w2_vv1', 'Ws_vlin', 'Wv_vlin', 'Wps', 'Wpv')}
    del _L0_gnn_all

    def _L1_gnn_setup():
        import jax, jax.numpy as jnp
        import numpy as np
        N = 2500
        E = 40000
        MUL0 = 64
        MUL1 = 32
        FC_IN = 16
        FC_H = 64
        WNUM = 192
        key = jax.random.key(seed)
        ks = jax.random.split(key, 16)
        return {'x': jax.random.normal(ks[0], (N, MUL0 + 3 * MUL1), jnp.float32), 'node_attr': jnp.ones((N, 1), jnp.float32), 'edge_scalars': jax.random.normal(ks[1], (E, FC_IN), jnp.float32), 'edge_attr_sh': jax.random.normal(ks[2], (E, 4), jnp.float32), 'edge_src': jax.random.randint(ks[3], (E,), 0, N), 'edge_dst': jax.random.randint(ks[4], (E,), 0, N), 'Wfc1': jax.random.normal(ks[5], (FC_IN, FC_H), jnp.float32), 'Wfc2': jax.random.normal(ks[6], (FC_H, WNUM), jnp.float32), 'Wsc0': jax.random.normal(ks[7], (MUL0, MUL0), jnp.float32), 'Wsc1': jax.random.normal(ks[8], (MUL1, MUL1), jnp.float32), 'Wl1_0': jax.random.normal(ks[9], (MUL0, MUL0), jnp.float32), 'Wl1_1': jax.random.normal(ks[10], (MUL1, MUL1), jnp.float32), 'Wl2_s': jax.random.normal(ks[11], (MUL0 + MUL1, MUL0), jnp.float32), 'Wl2_v': jax.random.normal(ks[12], (MUL0 + MUL1, MUL1), jnp.float32), 'Wa': 0.1 * jax.random.normal(ks[13], (MUL0 + MUL1, 1), jnp.float32)}
    _L1_gnn_all = _L1_gnn_setup()
    _L1_gnn_in = {k: v for k, v in _L1_gnn_all.items() if k in ('Wfc1', 'Wfc2', 'Wsc0', 'Wsc1', 'Wl1_0', 'Wl1_1', 'Wl2_s', 'Wl2_v', 'Wa')}
    del _L1_gnn_all
    return {'x': x, 'src': src, 'dst': dst, 'edge_attr_16': edge_attr_16, 'edge_attr_4': edge_attr_4, 'node_vec1': node_vec1, 'L0_gnn_gamma_s': _L0_gnn_in['gamma_s'], 'L0_gnn_beta_s': _L0_gnn_in['beta_s'], 'L0_gnn_gamma_v': _L0_gnn_in['gamma_v'], 'L0_gnn_Ws_src': _L0_gnn_in['Ws_src'], 'L0_gnn_Wv_src': _L0_gnn_in['Wv_src'], 'L0_gnn_Ws_dst': _L0_gnn_in['Ws_dst'], 'L0_gnn_Wv_dst': _L0_gnn_in['Wv_dst'], 'L0_gnn_W_rbf': _L0_gnn_in['W_rbf'], 'L0_gnn_W_alpha': _L0_gnn_in['W_alpha'], 'L0_gnn_alpha_dot': _L0_gnn_in['alpha_dot'], 'L0_gnn_Ws_val': _L0_gnn_in['Ws_val'], 'L0_gnn_Wv_val': _L0_gnn_in['Wv_val'], 'L0_gnn_Wg': _L0_gnn_in['Wg'], 'L0_gnn_w2_ss': _L0_gnn_in['w2_ss'], 'L0_gnn_w2_sv': _L0_gnn_in['w2_sv'], 'L0_gnn_w2_vs': _L0_gnn_in['w2_vs'], 'L0_gnn_w2_vv0': _L0_gnn_in['w2_vv0'], 'L0_gnn_w2_vv1': _L0_gnn_in['w2_vv1'], 'L0_gnn_Ws_vlin': _L0_gnn_in['Ws_vlin'], 'L0_gnn_Wv_vlin': _L0_gnn_in['Wv_vlin'], 'L0_gnn_Wps': _L0_gnn_in['Wps'], 'L0_gnn_Wpv': _L0_gnn_in['Wpv'], 'L1_gnn_Wfc1': _L1_gnn_in['Wfc1'], 'L1_gnn_Wfc2': _L1_gnn_in['Wfc2'], 'L1_gnn_Wsc0': _L1_gnn_in['Wsc0'], 'L1_gnn_Wsc1': _L1_gnn_in['Wsc1'], 'L1_gnn_Wl1_0': _L1_gnn_in['Wl1_0'], 'L1_gnn_Wl1_1': _L1_gnn_in['Wl1_1'], 'L1_gnn_Wl2_s': _L1_gnn_in['Wl2_s'], 'L1_gnn_Wl2_v': _L1_gnn_in['Wl2_v'], 'L1_gnn_Wa': _L1_gnn_in['Wa']}

def reference(x, src, dst, edge_attr_16, edge_attr_4, node_vec1, L0_gnn_gamma_s, L0_gnn_beta_s, L0_gnn_gamma_v, L0_gnn_Ws_src, L0_gnn_Wv_src, L0_gnn_Ws_dst, L0_gnn_Wv_dst, L0_gnn_W_rbf, L0_gnn_W_alpha, L0_gnn_alpha_dot, L0_gnn_Ws_val, L0_gnn_Wv_val, L0_gnn_Wg, L0_gnn_w2_ss, L0_gnn_w2_sv, L0_gnn_w2_vs, L0_gnn_w2_vv0, L0_gnn_w2_vv1, L0_gnn_Ws_vlin, L0_gnn_Wv_vlin, L0_gnn_Wps, L0_gnn_Wpv, L1_gnn_Wfc1, L1_gnn_Wfc2, L1_gnn_Wsc0, L1_gnn_Wsc1, L1_gnn_Wl1_0, L1_gnn_Wl1_1, L1_gnn_Wl2_s, L1_gnn_Wl2_v, L1_gnn_Wa):
    import jax
    import jax.numpy as jnp

    def _L0_gnn_ref(node, rbf, rsh, gamma_s, beta_s, gamma_v, Ws_src, Wv_src, Ws_dst, Wv_dst, W_rbf, W_alpha, alpha_dot, Ws_val, Wv_val, Wg, w2_ss, w2_sv, w2_vs, w2_vv0, w2_vv1, Ws_vlin, Wv_vlin, Wps, Wpv, edge_index):
        import jax, jax.numpy as jnp
        import numpy as np
        N, E = (2500, 40000)
        CS, CV = (64, 32)
        AS_, AV, H = (16, 8, 4)
        NB = 16
        SQRT3 = 1.7320508075688772
        SQRT2 = 1.4142135623730951
        EPS = 1e-05

        def _cg_tp(s, v, y0, y1, w_ss, w_sv, w_vs, w_vv0, w_vv1):
            out_s = jnp.concatenate([w_ss * s * y0[:, None], w_vv0 * (jnp.einsum('eci,ei->ec', v, y1) / SQRT3)], axis=-1)
            out_v = jnp.concatenate([(w_sv * s)[:, :, None] * y1[:, None, :], (w_vs * jnp.ones_like(v[..., 0]))[..., None] * v * y0[:, None, None], (w_vv1 * jnp.ones_like(v[..., 0]))[..., None] * (jnp.cross(v, y1[:, None, :]) / SQRT2)], axis=1)
            return (out_s, out_v)

        def _equiv_layernorm(s, v, gamma_s, beta_s, gamma_v):
            mu = jnp.mean(s, axis=-1, keepdims=True)
            var = jnp.var(s, axis=-1, keepdims=True)
            s_n = (s - mu) * jax.lax.rsqrt(var + EPS) * gamma_s + beta_s
            rms = jnp.sqrt(jnp.mean(jnp.sum(v * v, axis=-1), axis=-1, keepdims=True) + EPS)
            v_n = v / rms[..., None] * gamma_v[None, :, None]
            return (s_n, v_n)
        n = node.shape[0]
        e = rsh.shape[0]
        s = node[:, :CS]
        v = node[:, CS:].reshape(n, CV, 3)
        s_n, v_n = _equiv_layernorm(s, v, gamma_s, beta_s, gamma_v)
        src, dst = (edge_index[0], edge_index[1])
        msg_s = (s_n @ Ws_src)[src] + (s_n @ Ws_dst)[dst]
        msg_v = jnp.einsum('ncx,cd->ndx', v_n, Wv_src)[src] + jnp.einsum('ncx,cd->ndx', v_n, Wv_dst)[dst]
        y0, y1 = (rsh[:, 0], rsh[:, 1:4])
        w1 = rbf @ W_rbf
        m1_s, m1_v = _cg_tp(msg_s, msg_v, y0, y1, w1[:, :CS], w1[:, CS:2 * CS], w1[:, 2 * CS:2 * CS + CV], w1[:, 2 * CS + CV:2 * CS + 2 * CV], w1[:, 2 * CS + 2 * CV:])
        a = (m1_s @ W_alpha).reshape(e, H, AS_)
        a = jnp.where(a > 0, a, 0.2 * a)
        a = jnp.sum(a * alpha_dot, axis=-1, keepdims=True)
        amax = jax.ops.segment_max(a, dst, num_segments=n)
        amax = jnp.where(jnp.isfinite(amax), amax, 0.0)
        ex = jnp.exp(a - amax[dst])
        den = jax.ops.segment_sum(ex, dst, num_segments=n)
        alpha = ex / (den[dst] + 1e-16)
        val_s = m1_s @ Ws_val
        val_v = jnp.einsum('ecx,cd->edx', m1_v, Wv_val)
        val_v = val_v * jax.nn.sigmoid(val_s @ Wg)[..., None]
        val_s = jax.nn.sigmoid(val_s)
        m2_s, m2_v = _cg_tp(val_s, val_v, y0, y1, w2_ss, w2_sv, w2_vs, w2_vv0, w2_vv1)
        hs = (m2_s @ Ws_vlin).reshape(e, H, AS_)
        hv = jnp.einsum('ecx,cd->edx', m2_v, Wv_vlin).reshape(e, H, AV, 3)
        h = jnp.concatenate([hs, hv.reshape(e, H, AV * 3)], axis=-1)
        agg = jax.ops.segment_sum(alpha * h, dst, num_segments=n)
        agg_s = agg[:, :, :AS_].reshape(n, H * AS_)
        agg_v = agg[:, :, AS_:].reshape(n, H * AV, 3)
        out = node + jnp.concatenate([agg_s @ Wps, jnp.einsum('ncx,cd->ndx', agg_v, Wpv).reshape(n, CV * 3)], axis=-1)
        return out

    def _L1_gnn_ref(x, node_attr, edge_scalars, edge_attr_sh, edge_src, edge_dst, Wfc1, Wfc2, Wsc0, Wsc1, Wl1_0, Wl1_1, Wl2_s, Wl2_v, Wa):
        import jax, jax.numpy as jnp
        import numpy as np
        N = 2500
        E = 40000
        MUL0 = 64
        MUL1 = 32
        FC_IN = 16
        FC_H = 64
        WNUM = 192
        n = x.shape[0]
        x0 = x[:, :MUL0]
        x1 = x[:, MUL0:].reshape(n, MUL1, 3)
        a = node_attr
        h = jax.nn.silu(edge_scalars @ (Wfc1 / jnp.sqrt(jnp.float32(FC_IN))))
        w = h @ (Wfc2 / jnp.sqrt(jnp.float32(FC_H)))
        w0 = w[:, :64]
        w1 = w[:, 64:128]
        w2 = w[:, 128:160]
        w3 = w[:, 160:192]
        inv8 = 1.0 / jnp.sqrt(jnp.float32(MUL0))
        inv32 = 1.0 / jnp.sqrt(jnp.float32(MUL1))
        sc = jnp.concatenate([x0 @ Wsc0 * a * inv8, (jnp.einsum('num,uv->nvm', x1, Wsc1) * a[..., None] * inv32).reshape(n, 3 * MUL1)], axis=1)
        f0 = x0 @ Wl1_0 * a * inv8
        f1 = jnp.einsum('num,uv->nvm', x1, Wl1_1) * a[..., None] * inv32
        e0 = f0[edge_src]
        e1 = f1[edge_src]
        sh0 = edge_attr_sh[:, :1]
        sh1 = edge_attr_sh[:, 1:4]
        mid0 = w0 * e0 * sh0
        mid1 = w3 * jnp.einsum('eum,em->eu', e1, sh1) / jnp.sqrt(3.0)
        mid2 = w1[:, :, None] * e0[:, :, None] * sh1[:, None, :]
        mid3 = w2[:, :, None] * e1 * sh0[:, :, None]
        cnt = jnp.clip(jax.ops.segment_sum(jnp.ones(edge_dst.shape, x.dtype), edge_dst, num_segments=n), 1.0)

        def smean(v):
            s = jax.ops.segment_sum(v, edge_dst, num_segments=n)
            return s / cnt.reshape((n,) + (1,) * (v.ndim - 1))
        n0, n1 = (smean(mid0), smean(mid1))
        n2, n3 = (smean(mid2), smean(mid3))
        scal = jnp.concatenate([n0, n1], axis=1)
        vec = jnp.concatenate([n2, n3], axis=1)
        inv96 = 1.0 / jnp.sqrt(jnp.float32(MUL0 + MUL1))
        alpha = scal @ Wa * a * inv96
        out_s = scal @ Wl2_s * a * inv96
        out_v = jnp.einsum('num,uv->nvm', vec, Wl2_v) * a[..., None] * inv96
        conv = jnp.concatenate([out_s, out_v.reshape(n, 3 * MUL1)], axis=1)
        return sc + alpha * conv
    edge_index = jnp.stack([src, dst])
    x = _layernorm(x + _L0_gnn_ref(x, edge_attr_16, edge_attr_4, L0_gnn_gamma_s, L0_gnn_beta_s, L0_gnn_gamma_v, L0_gnn_Ws_src, L0_gnn_Wv_src, L0_gnn_Ws_dst, L0_gnn_Wv_dst, L0_gnn_W_rbf, L0_gnn_W_alpha, L0_gnn_alpha_dot, L0_gnn_Ws_val, L0_gnn_Wv_val, L0_gnn_Wg, L0_gnn_w2_ss, L0_gnn_w2_sv, L0_gnn_w2_vs, L0_gnn_w2_vv0, L0_gnn_w2_vv1, L0_gnn_Ws_vlin, L0_gnn_Wv_vlin, L0_gnn_Wps, L0_gnn_Wpv, edge_index), axis=-1)
    x = _layernorm(x + _L1_gnn_ref(x, node_vec1, edge_attr_16, edge_attr_4, src, dst, L1_gnn_Wfc1, L1_gnn_Wfc2, L1_gnn_Wsc0, L1_gnn_Wsc1, L1_gnn_Wl1_0, L1_gnn_Wl1_1, L1_gnn_Wl2_s, L1_gnn_Wl2_v, L1_gnn_Wa), axis=-1)
    return x

_drawn_inputs = setup_inputs


def setup_inputs(seed=0):
    import zlib

    import numpy as np

    out = dict(_drawn_inputs(seed))
    spreads = {'L0_gnn_gamma_s': (1.0, 0.6), 'L0_gnn_beta_s': (0.0, 0.8), 'L0_gnn_gamma_v': (1.0, 0.6)}
    factors = {'L0_gnn_w2_vv1': 2.671,
     'L1_gnn_Wfc1': 8.0,
     'L1_gnn_Wfc2': 8.0,
     'L1_gnn_Wl1_0': 8.0,
     'L1_gnn_Wl1_1': 8.0,
     'L1_gnn_Wl2_s': 8.0,
     'L1_gnn_Wl2_v': 8.0,
     'L1_gnn_Wa': 8.0,
     'L1_gnn_Wsc0': 5.012,
     'L1_gnn_Wsc1': 4.271}
    for name, (base, spread) in spreads.items():
        noise = np.random.default_rng([zlib.crc32(name.encode()), seed]).standard_normal(out[name].shape)
        drawn = base * np.exp(spread * noise) if base else spread * noise
        out[name] = jnp.asarray(drawn.astype(out[name].dtype))
    for name, factor in factors.items():
        out[name] = (out[name] * factor).astype(out[name].dtype)
    return out
```

```python
import math
from contextlib import ExitStack

import numpy as np

import concourse.bass as bass
from concourse import mybir

P = 128
TILES = 4
GROUP = TILES * P
RING = 4
CS, CV = 64, 32
D = CS + 3 * CV
HEADS, AS, AV = 4, 16, 8
HW = AS + 3 * AV
HROW = HEADS * (HW + 1)
WN = 2 * CS + 3 * CV
WE = 192
UNIT1 = 2
SPARE = 4
SEG_TILES = 16
CHUNK = 7
MID = CS + CV
ACC1 = 4 * MID
EPS = 1e-5
FAR = 1.0e38

F32 = mybir.dt.float32
I32 = mybir.dt.int32
ALU = mybir.AluOpType
ACT = mybir.ActivationFunctionType
AX = mybir.AxisListType.X


def wait(engine, sem, value):
    if not isinstance(value, int) or value > 0:
        engine.wait_ge(sem, value)


class Count:

    def __init__(self, sem, round_, per):
        self.sem, self.base, self.n = sem, round_ * per, 0

    def up(self, instruction):
        instruction.then_inc(self.sem, 1)
        self.n += 1
        return self.base + self.n


def bc(ap, axis, size):
    shape = list(ap.shape)
    shape.insert(axis, size)
    return ap.unsqueeze(axis).broadcast_to(shape)


def row(ap):
    return ap.partition_broadcast(P)


def staircase_steps(units, blocks):
    steps = units + blocks - 1
    return -(-steps // RING) * RING


def constants(nc, ident, iota):
    with ExitStack() as ctx:
        made = ctx.enter_context(nc.semaphore("const_made"))
        iota_i = ctx.enter_context(nc.sbuf_tensor("iota_i", [P, P], I32))
        block = ctx.enter_context(nc.Block())

        @block.gpsimd
        def _(pool):
            nc.gpsimd.memset(ident[:], 0.0).then_inc(made, 1)
            nc.gpsimd.iota(iota_i[:], pattern=[[1, P]], base=0, channel_multiplier=0).then_inc(made, 1)
            pool.wait_ge(made, 2)
            nc.gpsimd.affine_select(out=ident[:], in_=ident[:], compare_op=ALU.not_equal, fill=1.0, base=0,
                                    pattern=[[-1, P]], channel_multiplier=1).then_inc(made, 1)
            nc.gpsimd.tensor_copy(iota[:], iota_i[:]).then_inc(made, 1)


def staircase(nc, name, first_dst, units, blocks, unit_row, slot_row, b128, keep):
    steps = staircase_steps(units, blocks)
    chunks = first_dst.shape[1]
    halves = [(c, min(steps, c + 512)) for c in range(0, steps, 512)]
    with ExitStack() as ctx:
        def sb(n, shape, dt=F32):
            return ctx.enter_context(nc.sbuf_tensor(f"{name}_{n}", shape, dt))

        first = sb("first", [P, chunks], I32)
        fb_i = sb("fb_i", [P, chunks], I32)
        fb = sb("fb", [P, chunks])
        idx_i = sb("idx_i", [P, chunks], I32)
        idx = sb("idx", [P, chunks])
        corner = sb("corner", [P, chunks])
        s_i = sb("s_i", [P, steps], I32)
        spare_i = sb("spare_i", [1, steps], I32)
        s_f = sb("s_f", [P, steps])
        spare = sb("spare", [1, steps])
        ones = sb("ones", [P, P])
        passed = sb("passed", [P, chunks, steps])
        u = sb("u", [P, steps])
        b = sb("b", [P, steps])
        slot = sb("slot", [1, steps])
        psum = [ctx.enter_context(nc.psum_tensor(f"{name}_ps{h}", [P, 512], F32)) for h in range(len(halves))]
        loaded = ctx.enter_context(nc.semaphore(f"{name}_loaded"))
        patterns = ctx.enter_context(nc.semaphore(f"{name}_patterns"))
        done = ctx.enter_context(nc.semaphore(f"{name}_dve"))
        summed = ctx.enter_context(nc.semaphore(f"{name}_summed"))
        block = ctx.enter_context(nc.Block())

        @block.sync
        def _(sp):
            sp.dma_start(first[:], first_dst).then_inc(loaded, 16)

        @block.gpsimd
        def _(pool):
            nc.gpsimd.iota(idx_i[:], pattern=[[P, chunks]], base=1, channel_multiplier=1).then_inc(patterns, 1)
            nc.gpsimd.iota(s_i[:], pattern=[[1, steps]], base=0, channel_multiplier=0).then_inc(patterns, 1)
            nc.gpsimd.iota(spare_i[:], pattern=[[0, steps // 2], [1, 2]], base=blocks,
                           channel_multiplier=0).then_inc(patterns, 1)
            nc.gpsimd.memset(ones[:], 1.0).then_inc(patterns, 1)

        @block.tensor
        def _(pe):
            pe.wait_ge(patterns, 4)
            pe.wait_ge(done, 6 + chunks)
            for h, (lo, hi) in enumerate(halves):
                for c in range(chunks):
                    last = nc.tensor.matmul(psum[h][:, 0:hi - lo], ones[:], passed[:, c, lo:hi],
                                            start=c == 0, stop=c == chunks - 1)
            last.then_inc(summed, 1)

        @block.vector
        def _(dve):
            d = Count(done, 0, 0)
            dve.wait_ge(loaded, 16)
            dve.wait_ge(patterns, 4)
            d.up(nc.vector.tensor_scalar(fb_i[:], first[:], 7, None, ALU.arith_shift_right))
            d.up(nc.vector.tensor_copy(idx[:], idx_i[:]))
            d.up(nc.vector.tensor_copy(s_f[:], s_i[:]))
            d.up(nc.vector.tensor_copy(spare[:], spare_i[:]))
            dve.wait_ge(done, 1)
            d.up(nc.vector.tensor_copy(fb[:], fb_i[:]))
            dve.wait_ge(done, 5)
            dve.wait_ge(done, d.up(nc.vector.tensor_tensor(corner[:], fb[:], idx[:], ALU.add)))
            for c in range(chunks):
                d.up(nc.vector.tensor_scalar(passed[:, c, :], s_f[:], corner[:, c:c + 1], None, ALU.is_ge))
            dve.wait_ge(summed, 1)
            for h, (lo, hi) in enumerate(halves):
                d.up(nc.vector.tensor_copy(u[:, lo:hi], psum[h][:, 0:hi - lo]))
            dve.wait_ge(done, d.base + d.n)
            d.up(nc.vector.tensor_tensor(b[:], s_f[:], u[:], ALU.subtract))
            d.up(nc.vector.memset(keep[:, 0:1], 0.0))
            d.up(nc.vector.tensor_copy(unit_row[:], u[0:1, :]))
            k = d.up(nc.vector.tensor_tensor(keep[:, 1:steps], u[:, 1:steps], u[:, 0:steps - 1], ALU.subtract))
            dve.wait_ge(done, k)
            d.up(nc.vector.tensor_scalar(b128[:], b[:], float(P), None, ALU.mult))
            k = d.up(nc.vector.tensor_tensor(slot[:], spare[:], b[0:1, :], ALU.subtract))
            dve.wait_ge(done, k)
            k = d.up(nc.vector.tensor_tensor(slot[:, 0:steps - 1], slot[:, 0:steps - 1], keep[0:1, 1:steps],
                                             ALU.mult))
            k = d.up(nc.vector.memset(slot[:, steps - 1:steps], 0.0))
            dve.wait_ge(done, k)
            k = d.up(nc.vector.tensor_tensor(slot[:], slot[:], b[0:1, :], ALU.add))
            dve.wait_ge(done, k)
            k = d.up(nc.vector.tensor_copy(slot_row[:], slot[:]))
            dve.wait_ge(done, k)


def tables(nc, xn, table_src, table_dst, w, ident):
    blocks = xn.shape[0] // P
    chunks = blocks // CHUNK
    with ExitStack() as ctx:
        def sb(n, shape, dt=F32):
            return ctx.enter_context(nc.sbuf_tensor(f"t_{n}", shape, dt))

        def sem(n):
            return ctx.enter_context(nc.semaphore(f"t_{n}"))

        x = sb("x", [P, CHUNK, D])
        xc = sb("xc", [P, CHUNK, CS])
        sq = sb("sq", [P, CHUNK, D])
        xnorm = sb("xnorm", [P, CHUNK, D])
        stat = sb("stat", [P, 2 * CHUNK])
        mean = sb("mean", [P, CHUNK])
        root = sb("root", [P, 2 * CHUNK])
        rinv = sb("rinv", [P, 2 * CHUNK])
        gamma_s, beta_s, gamma_v = sb("gs", [P, CS]), sb("bs", [P, CS]), sb("gv", [P, CV])
        wa, wb = sb("wa", [P, 2 * D]), sb("wb", [CV, 2 * D])
        xt_a, xt_b = sb("xt_a", [P, 2, P]), sb("xt_b", [CV, 2, P])
        o = sb("o", [P, CHUNK, 2 * D])
        pt = [ctx.enter_context(nc.psum_tensor(f"t_pt{i}", [P, 512], F32)) for i in range(2)]
        po = [ctx.enter_context(nc.psum_tensor(f"t_po{i}", [P, 512], F32)) for i in range(2)]
        zeroed, weights, loaded, own, rooted = sem("zeroed"), sem("weights"), sem("loaded"), sem("dve"), sem("rooted")
        turned, copied, multiplied, stored = sem("turned"), sem("copied"), sem("multiplied"), sem("stored")
        rested = sem("rested")
        n_weights = 3 + 2 * 4
        NORMED, PER = 17, 17 + CHUNK
        SPREADS = 9
        xv = xn.rearrange("(c b p) f -> c p b f", b=CHUNK, p=P)
        sv = table_src.rearrange("(c b p) f -> c p b f", b=CHUNK, p=P)
        dv = table_dst.rearrange("(c b p) f -> c p b f", b=CHUNK, p=P)
        block = ctx.enter_context(nc.Block())

        @block.sync
        def _(sp):
            sp.dma_start(gamma_s[:], row(w["gamma_s"])).then_inc(weights, 16)
            sp.dma_start(beta_s[:], row(w["beta_s"])).then_inc(weights, 16)
            sp.dma_start(gamma_v[:], row(w["gamma_v"])).then_inc(weights, 16)
            sp.wait_ge(zeroed, 2)
            for side, (ws, wv) in enumerate((("Ws_src", "Wv_src"), ("Ws_dst", "Wv_dst"))):
                at = side * D
                sp.dma_start(wa[0:CS, at:at + CS], w[ws]).then_inc(weights, 16)
                for comp in range(3):
                    to = at + CS + comp * CV
                    into = wa[CS + comp * CV:CS + (comp + 1) * CV, to:to + CV] if comp < 2 else wb[:, to:to + CV]
                    sp.dma_start(into, w[wv]).then_inc(weights, 16)
            with sp.Fori(0, chunks) as c:
                sp.dma_start(x[:], xv[c]).then_inc(loaded, 16)
                sp.wait_ge(own, (c + 1) * PER)
                sp.dma_start(sv[c], o[:, :, 0:D]).then_inc(stored, 16)
                sp.dma_start(dv[c], o[:, :, D:2 * D]).then_inc(stored, 16)
                sp.wait_ge(stored, (c + 1) * 32)
                sp.sem_inc(rested, 1)

        @block.gpsimd
        def _(pool):
            nc.gpsimd.memset(wa[:], 0.0).then_inc(zeroed, 1)
            nc.gpsimd.memset(wb[:], 0.0).then_inc(zeroed, 1)

        @block.scalar
        def _(act):
            with act.Fori(0, chunks) as c:
                act.wait_ge(own, c * PER + SPREADS)
                nc.scalar.activation(root[:], stat[:], ACT.Sqrt).then_inc(rooted, 1)
                for b in range(CHUNK):
                    act.wait_ge(turned, c * CHUNK + (b + 1))
                    act.wait_ge(multiplied, c * CHUNK + (b + 1))
                    nc.scalar.activation(xt_a[:, b % 2, :], pt[b % 2][:, 0:P], ACT.Copy)
                    nc.scalar.activation(xt_b[:, b % 2, :], pt[b % 2][0:CV, P:2 * P], ACT.Copy).then_inc(copied, 1)

        @block.tensor
        def _(pe):
            pe.sem_inc(multiplied, 1)
            pe.wait_ge(weights, 16 * n_weights)
            with pe.Fori(0, chunks) as c:
                pe.wait_ge(own, c * PER + NORMED)
                for b in range(CHUNK + 1):
                    if b < CHUNK:
                        nc.tensor.transpose(pt[b % 2][:, 0:P], xnorm[:, b, 0:P], ident[:])
                        nc.tensor.transpose(pt[b % 2][0:CV, P:2 * P], xnorm[:, b, P:D], ident[:]).then_inc(turned, 1)
                    if b >= 1:
                        pe.wait_ge(copied, c * CHUNK + b)
                        if b >= 3:
                            pe.wait_ge(own, c * PER + NORMED + b - 2)
                        nc.tensor.matmul(po[(b - 1) % 2][:, 0:2 * D], xt_a[:, (b - 1) % 2, :], wa[:],
                                         start=True, stop=False)
                        nc.tensor.matmul(po[(b - 1) % 2][:, 0:2 * D], xt_b[:, (b - 1) % 2, :], wb[:],
                                         start=False, stop=True).then_inc(multiplied, 1)

        @block.vector
        def _(dve):
            dve.wait_ge(weights, 16 * n_weights)
            s, v = x[:, :, 0:CS], x[:, :, CS:D]
            with dve.Fori(0, chunks) as c:
                d = Count(own, c, PER)
                dve.wait_ge(loaded, (c + 1) * 16)
                k = d.up(nc.vector.tensor_reduce(mean[:], s, AX, ALU.add))
                d.up(nc.vector.tensor_tensor(sq[:, :, CS:D], v, v, ALU.mult))
                dve.wait_ge(own, k)
                k = d.up(nc.vector.tensor_scalar(mean[:], mean[:], 1.0 / CS, None, ALU.mult))
                dve.wait_ge(own, k)
                k = d.up(nc.vector.tensor_tensor(xc[:], s, bc(mean[:], 2, CS), ALU.subtract))
                dve.wait_ge(own, k)
                k = d.up(nc.vector.tensor_tensor(sq[:, :, 0:CS], xc[:], xc[:], ALU.mult))
                dve.wait_ge(own, k)
                k = d.up(nc.vector.tensor_reduce(stat[:, 0:CHUNK], sq[:, :, 0:CS], AX, ALU.add))
                dve.wait_ge(own, k)
                d.up(nc.vector.tensor_scalar(stat[:, 0:CHUNK], stat[:, 0:CHUNK], 1.0 / CS, EPS, ALU.mult, ALU.add))
                k = d.up(nc.vector.tensor_reduce(stat[:, CHUNK:], sq[:, :, CS:D], AX, ALU.add))
                dve.wait_ge(own, k)
                k = d.up(nc.vector.tensor_scalar(stat[:, CHUNK:], stat[:, CHUNK:], 1.0 / CV, EPS, ALU.mult, ALU.add))
                assert d.n == SPREADS
                dve.wait_ge(rooted, c + 1)
                k = d.up(nc.vector.reciprocal(rinv[:], root[:]))
                dve.wait_ge(own, k)
                d.up(nc.vector.tensor_tensor(xc[:], xc[:], bc(rinv[:, 0:CHUNK], 2, CS), ALU.mult))
                k = d.up(nc.vector.tensor_tensor(xnorm[:, :, CS:D], v, bc(rinv[:, CHUNK:], 2, 3 * CV), ALU.mult))
                dve.wait_ge(own, k)
                k = d.up(nc.vector.tensor_tensor(xc[:], xc[:], bc(gamma_s[:], 1, CHUNK), ALU.mult))
                for comp in range(3):
                    part = xnorm[:, :, CS + comp * CV:CS + (comp + 1) * CV]
                    d.up(nc.vector.tensor_tensor(part, part, bc(gamma_v[:], 1, CHUNK), ALU.mult))
                dve.wait_ge(own, k)
                d.up(nc.vector.tensor_tensor(xnorm[:, :, 0:CS], xc[:], bc(beta_s[:], 1, CHUNK), ALU.add))
                assert d.n == NORMED
                for b in range(CHUNK):
                    dve.wait_ge(multiplied, c * CHUNK + (b + 2))
                    d.up(nc.vector.tensor_copy(o[:, b, :], po[b % 2][:, 0:2 * D]))
                assert d.n == PER


def edges(nc, idx_d, y_d, rbf_d, table_src, table_dst, h_d, w, ident, logits):
    groups = idx_d.shape[0]
    T = TILES
    with ExitStack() as ctx:
        def sb(n, shape, dt=F32):
            return ctx.enter_context(nc.sbuf_tensor(f"e_{n}", shape, dt))

        def psum(n, size=512):
            return ctx.enter_context(nc.psum_tensor(f"e_{n}", [P, size], F32))

        def sem(n):
            return ctx.enter_context(nc.semaphore(f"e_{n}"))

        w_rbf = sb("w_rbf", [16, WN])
        w_first = sb("w_first", [CS + CV, 2 * CS])
        w_gate = sb("w_gate", [CS + CV, CV])
        w_vec = sb("w_vec", [P, CV])
        w_s2 = sb("w_s2", [CS + CV, HEADS * AS])
        w_v2 = sb("w_v2", [P, HEADS * AV])
        w_valT, w_g = sb("w_valT", [CS, CS + CV]), sb("w_g", [CS, CV])
        scale_s, scale_v = sb("scale_s", [CS + CV, 1]), sb("scale_v", [P, 1])
        dot = sb("dot", [P, HEADS * AS])
        idx = sb("idx", [P, RING, 2 * T], I32)
        y = sb("y", [P, RING, T, 6])
        rbf = sb("rbf", [16, RING, GROUP])
        g_src = sb("g_src", [P, RING, T, D])
        g_dst = sb("g_dst", [P, RING, T, D])
        msg = sb("msg", [P, 2, T, D])
        sy = sb("sy", [P, T, CS])
        vy = sb("vy", [P, T, 3, CV])
        dsum = sb("dsum", [P, T, CV])
        sw = sb("sw", [P, T, CS])
        wy = sb("wy", [P, T, CV])
        c1 = sb("c1", [P, T, 3, CV])
        c2 = sb("c2", [P, T, 3, CV])
        cross = sb("cross", [P, T, 3, CV])
        m1s = sb("m1s", [P, T, CS + CV])
        m1v = sb("m1v", [P, T, 3, P])
        m1t = sb("m1t", [P, 4, GROUP])
        lin = sb("lin", [P, T, CS])
        act8 = sb("act8", [P, T, CS])
        weighed = sb("weighed", [P, T, CS])
        sig = sb("sig", [P, 2, T, CS])
        gate = sb("gate", [P, 2, T, CV])
        gv = sb("gv", [P, T, 3, CV])
        vy2 = sb("vy2", [P, T, 3, CV])
        dsum2 = sb("dsum2", [P, T, CV])
        d1 = sb("d1", [P, T, 3, CV])
        d2 = sb("d2", [P, T, 3, CV])
        m2s = sb("m2s", [P, T, CS + CV])
        m2v = sb("m2v", [P, T, 3, P])
        m2t = sb("m2t", [P, 4, GROUP])
        h = sb("h", [P, 2, T, HEADS, HW + 1])

        ps_w = psum("ps_w", 1024)
        radial_w = ps_w[:].rearrange("p (t k) -> p t k", k=256)
        ps_t = [psum(f"ps_t{i}") for i in range(2)]
        ps_z = psum("ps_z")
        ps_g = psum("ps_g")
        ps_h = psum("ps_h", 1024)
        heads = ps_h[:].rearrange("p (t k) -> p t k", k=256)[:, :, 0:D].rearrange("p t (h k) -> p t h k", k=HW)

        weights, scaled, setup, ones_set = sem("weights"), sem("scaled"), sem("setup"), sem("ones_set")
        idx_in = [sem(f"idx_in{r}") for r in range(RING)]
        y_in = [sem(f"y_in{r}") for r in range(RING)]
        rbf_in = [sem(f"rbf_in{r}") for r in range(RING)]
        gathered = [sem(f"gathered{r}") for r in range(RING)]
        stored = [sem(f"stored{r}") for r in range(2)]
        summed = sem("summed")
        radial = sem("radial")
        first = sem("first")
        second = sem("second")
        turned = sem("turned")
        taken = sem("taken")
        mixed = sem("mixed")
        acted = sem("acted")
        valued = sem("valued")
        kept = sem("kept")
        weighted = sem("weighted")
        issued = sem("issued")
        FIRST, SECOND, ACTED = 16, 13, 4
        DONE_S, DONE_V = 8, 16
        DONE2_S, DONE2_V = 8, 12

        def turn(u, second_tp, k):
            if second_tp:
                return u * 8 + ((4 if isinstance(u, int) and u == groups - 1 else 8) + k + 1)
            return k + 1 if isinstance(u, int) and u == 0 else u * 8 + (k - 3)

        def rounds(engine, body):
            for r in range(RING):
                body(r, r, 0)
            last = groups // RING - 1
            if last > 1:
                with engine.Fori(1, last) as i:
                    for r in range(RING):
                        body(i * RING + r, r, i)
            for r in range(RING):
                body(last * RING + r, r, last)

        def present(u):
            return not isinstance(u, int) or 0 <= u < groups

        block = ctx.enter_context(nc.Block())

        @block.sync
        def _(sp):
            column = lambda v: v.rearrange("(p a) -> p a", a=1)
            for to, source in ((w_rbf[:], w["W_rbf"]), (w_first[:, 0:CS], w["W_alpha"]),
                               (w_first[:, CS:2 * CS], w["Ws_val"]), (w_vec[:], w["Wv_val"]),
                               (w_s2[:], w["Ws_vlin"]), (w_v2[:], w["Wv_vlin"]), (w_g[:], w["Wg"]),
                               (scale_s[0:CS], column(w["w2_ss"])), (scale_s[CS:CS + CV], column(w["w2_vv0"])),
                               (scale_v[0:CS], column(w["w2_sv"])), (scale_v[CS:CS + CV], column(w["w2_vs"])),
                               (scale_v[CS + CV:P], column(w["w2_vv1"])),
                               (dot[:], w["alpha_dot"].rearrange("a h k -> (a h k)").partition_broadcast(P))):
                sp.dma_start(to, source).then_inc(weights, 16)

            def load(u, r, i):
                at = u * GROUP if isinstance(u, int) else sp.snap(u * GROUP)
                wait(sp, gathered[r], i * 32 * T)
                sp.dma_start(idx[:, r, :], idx_d[u]).then_inc(idx_in[r], 16)
                wait(sp, radial, u - (RING - 1))
                sp.dma_start(rbf[:, r, :], rbf_d[:, bass.ds(at, GROUP)]).then_inc(rbf_in[r], 16)
                wait(sp, second, (u - (RING - 1)) * SECOND)
                sp.dma_start(y[:, r], y_d[u]).then_inc(y_in[r], 16)

            rounds(sp, load)

        @block.gpsimd
        def _(pool):
            nc.gpsimd.memset(h[:], 1.0).then_inc(ones_set, 1)

            def gather(u, r, i):
                pool.wait_ge(idx_in[r], (i + 1) * 16)
                wait(pool, summed, u - (RING - 1))
                pool.sem_inc(issued, 1)
                for side, (table, into) in enumerate(((table_src, g_src), (table_dst, g_dst))):
                    for t in range(T):
                        c = side * T + t
                        pool.indirect_dma_start(
                            out=into[:, r, t, :], out_offset=None, in_=table,
                            in_offset=bass.IndirectOffsetOnAxis(ap=idx[:, r, c:c + 1], axis=0),
                        ).then_inc(gathered[r], 16)

            def body(u, r, i):
                ahead = u + 2
                if present(ahead):
                    gather(ahead, (r + 2) % RING, i + (r + 2) // RING)
                pool.wait_ge(gathered[r], (i + 1) * 32 * T)
                wait(pool, first, (u - 1) * FIRST)
                nc.gpsimd.tensor_tensor(msg[:, r % 2], g_src[:, r], g_dst[:, r], ALU.add).then_inc(summed, 1)
                terms(u - 1)

            def terms(v):
                if not present(v):
                    return
                pool.wait_ge(acted, (v + 1) * ACTED)
                wait(pool, second, v * SECOND)
                nc.gpsimd.tensor_tensor(weighed[:], act8[:], lin[:], ALU.add).then_inc(weighted, 1)
                pool.wait_ge(weighted, v * 2 + 1)
                nc.gpsimd.tensor_tensor(weighed[:], weighed[:], bc(dot[:], 1, T), ALU.mult).then_inc(weighted, 1)

            gather(0, 0, 0)
            gather(1, 1, 0)
            rounds(pool, body)
            terms(groups - 1)

        @block.tensor
        def _(pe):
            pe.wait_ge(scaled, 1)
            nc.tensor.transpose(ps_t[0][0:CS, 0:CS + CV], w_first[:, CS:2 * CS],
                                ident[0:CS + CV, 0:CS + CV]).then_inc(setup, 1)
            pe.wait_ge(scaled, 2)
            nc.tensor.matmul(ps_t[1][0:CS + CV, 0:CV], w_valT[:], w_g[:], start=True, stop=True).then_inc(setup, 1)
            pe.wait_ge(scaled, 3)

            def radial_weights(u, r, i):
                pe.wait_ge(rbf_in[r], (i + 1) * 16)
                wait(pe, first, u * FIRST)
                for t in range(T):
                    last = nc.tensor.matmul(radial_w[:, t, 0:WN],
                                            rbf[:, r, t * P:(t + 1) * P], w_rbf[:], start=True, stop=True)
                last.then_inc(radial, 1)

            def transposes(u, second_tp, ready, scalars_at, vectors_at, rows_s, rows_v):
                for k in range(4):
                    pe.wait_ge(ready, scalars_at if k == 0 else vectors_at)
                    wait(pe, taken, turn(u, second_tp, k) - 2)
                    for t in range(T):
                        if k == 0:
                            last = nc.tensor.transpose(ps_t[k % 2][0:CS + CV, t * P:(t + 1) * P],
                                                       rows_s[:, t, :], ident[:])
                        else:
                            last = nc.tensor.transpose(ps_t[k % 2][:, t * P:(t + 1) * P],
                                                       rows_v[:, t, k - 1, :], ident[:])
                    last.then_inc(turned, 1)

            def mix(u):
                pe.wait_ge(taken, turn(u, False, 3))
                if present(u - 1):
                    pe.wait_ge(acted, u * ACTED)
                    pe.wait_ge(second, (u - 1) * SECOND + 1)
                for t in range(T):
                    tile = slice(t * P, (t + 1) * P)
                    nc.tensor.matmul(ps_z[:, tile], m1t[0:CS + CV, 0, tile], w_first[:], start=True, stop=True)
                    nc.tensor.matmul(ps_g[:, t * P:t * P + CV], m1t[0:CS + CV, 0, tile], w_gate[:],
                                     start=True, stop=True)
                    for x in range(3):
                        last = nc.tensor.matmul(ps_g[:, t * P + (1 + x) * CV:t * P + (2 + x) * CV],
                                                m1t[:, 1 + x, tile], w_vec[:], start=True, stop=True)
                last.then_inc(mixed, 1)

            def values(v):
                if not present(v):
                    return
                transposes(v, True, second, v * SECOND + DONE2_S, v * SECOND + DONE2_V, m2s, m2v)
                pe.wait_ge(taken, turn(v, True, 3))
                wait(pe, kept, v * 2)
                for t in range(T):
                    tile = slice(t * P, (t + 1) * P)
                    nc.tensor.matmul(heads[:, t, :, 0:AS], m2t[0:CS + CV, 0, tile], w_s2[:], start=True, stop=True)
                    for x in range(3):
                        last = nc.tensor.matmul(heads[:, t, :, AS + x * AV:AS + (x + 1) * AV],
                                                m2t[:, 1 + x, tile], w_v2[:], start=True, stop=True)
                    if t % 2:
                        last.then_inc(valued, 1)

            def body(u, r, i):
                transposes(u, False, first, u * FIRST + DONE_S, u * FIRST + DONE_V, m1s, m1v)
                mix(u)
                if present(u + 1):
                    radial_weights(u + 1, (r + 1) % RING, i + (r + 1) // RING)
                values(u - 1)

            radial_weights(0, 0, 0)
            rounds(pe, body)
            values(groups - 1)

        @block.scalar
        def _(act):
            act.wait_ge(ones_set, 1)

            def take(u, second_tp, into):
                for k in range(4):
                    act.wait_ge(turned, turn(u, second_tp, k))
                    rows = CS + CV if k == 0 else P
                    nc.scalar.activation(into[0:rows, k, :], ps_t[k % 2][0:rows, :], ACT.Copy).then_inc(taken, 1)

            def body(u, r, i):
                wait(act, mixed, u)
                take(u, False, m1t)
                act.wait_ge(mixed, u + 1)
                if present(u - 2):
                    act.wait_ge(second, (u - 1) * SECOND)
                if present(u - 1):
                    act.wait_ge(weighted, u * 2)
                per_tile = lambda bank, a, b: bank[:].rearrange("p (t k) -> p t k", k=P)[:, :, a:b]
                nc.scalar.activation(gate[:, r % 2], per_tile(ps_g, 0, CV), ACT.Sigmoid).then_inc(acted, 1)
                nc.scalar.activation(sig[:, r % 2], per_tile(ps_z, CS, 2 * CS), ACT.Sigmoid).then_inc(acted, 1)
                nc.scalar.activation(act8[:], per_tile(ps_z, 0, CS), ACT.Relu, scale=0.8).then_inc(acted, 1)
                nc.scalar.activation(lin[:], per_tile(ps_z, 0, CS), ACT.Copy, scale=0.2).then_inc(acted, 1)
                keep(u - 1, (r - 1) % 2, i * 2 + (r - 1) // 2)

            def keep(v, slot, n):
                if not present(v):
                    return
                wait(act, valued, v * 2)
                take(v, True, m2t)
                wait(act, stored[slot], n * 16)
                for half in range(2):
                    act.wait_ge(valued, v * 2 + (half + 1))
                    tiles = slice(2 * half, 2 * half + 2)
                    nc.scalar.activation(h[:, slot, tiles, :, 0:HW], heads[:, tiles], ACT.Copy).then_inc(kept, 1)
                act.wait_ge(kept, v * 2 + 2)
                act.dma_start(h_d[v], h[:, slot].rearrange("p t h k -> p (t h k)")).then_inc(stored[slot], 16)

            rounds(act, body)
            keep(groups - 1, (groups - 1) % 2, (groups - 1) // 2)
            for slot in range(2):
                act.wait_ge(stored[slot], 16 * (groups // 2))

        @block.vector
        def _(dve):
            dve.wait_ge(weights, 16 * 13)
            nc.vector.tensor_scalar(w_rbf[:, 2 * CS + CV:2 * CS + 2 * CV], w_rbf[:, 2 * CS + CV:2 * CS + 2 * CV],
                                    1.0 / math.sqrt(3.0), None, ALU.mult)
            nc.vector.tensor_scalar(w_rbf[:, 2 * CS + 2 * CV:WN], w_rbf[:, 2 * CS + 2 * CV:WN],
                                    1.0 / math.sqrt(2.0), None, ALU.mult)
            nc.vector.tensor_scalar(w_s2[:], w_s2[:], scale_s[:, 0:1], None, ALU.mult)
            nc.vector.tensor_scalar(w_v2[:], w_v2[:], scale_v[:, 0:1], None, ALU.mult).then_inc(scaled, 1)
            dve.wait_ge(setup, 1)
            nc.vector.tensor_copy(w_valT[:], ps_t[0][0:CS, 0:CS + CV]).then_inc(scaled, 1)
            dve.wait_ge(setup, 2)
            nc.vector.tensor_copy(w_gate[:], ps_t[1][0:CS + CV, 0:CV])
            nc.vector.tensor_scalar(w_s2[CS:CS + CV, :], w_s2[CS:CS + CV, :], 1.0 / math.sqrt(3.0), None, ALU.mult)
            nc.vector.tensor_scalar(w_v2[CS + CV:P, :], w_v2[CS + CV:P, :], 1.0 / math.sqrt(2.0), None,
                                    ALU.mult).then_inc(scaled, 1)

            mult = lambda out, a, b: nc.vector.tensor_tensor(out, a, b, ALU.mult)
            add = lambda out, a, b: nc.vector.tensor_tensor(out, a, b, ALU.add)
            subtract = lambda out, a, b: nc.vector.tensor_tensor(out, a, b, ALU.subtract)

            def cross_parts(p1, p2, out, d, k):
                dve.wait_ge(d.sem, k)
                for x in range(3):
                    d.up(subtract(out(x), p1[:, :, (x + 1) % 3, :], p2[:, :, (x + 2) % 3, :]))

            def first_product(u, r, i):
                d = Count(first, u, FIRST)
                m = msg[:, r % 2]
                s, v = m[:, :, 0:CS], m[:, :, CS:D].rearrange("p t (x c) -> p t x c", x=3)
                y0, yx = y[:, r, :, 0], y[:, r, :, 1:4]
                w_ss, w_sv = radial_w[:, :, 0:CS], radial_w[:, :, CS:2 * CS]
                w_vs, w_vv0, w_vv1 = (radial_w[:, :, 2 * CS + n * CV:2 * CS + (n + 1) * CV] for n in range(3))
                dve.wait_ge(summed, u + 1)
                dve.wait_ge(y_in[r], (i + 1) * 16)
                k_vy = d.up(mult(vy[:], v, bc(yx, 3, CV)))
                k_sy = d.up(mult(sy[:], s, bc(y0, 2, CS)))
                d.up(mult(c1[:], v, bc(y[:, r, :, 2:5], 3, CV)))
                dve.wait_ge(first, k_vy)
                k_dot = d.up(add(dsum[:], vy[:, :, 0, :], vy[:, :, 1, :]))
                k_c = d.up(mult(c2[:], v, bc(y[:, r, :, 3:6], 3, CV)))
                dve.wait_ge(first, k_dot)
                k_dot = d.up(add(dsum[:], dsum[:], vy[:, :, 2, :]))
                dve.wait_ge(radial, u + 1)
                if present(u - 1):
                    dve.wait_ge(turned, turn(u - 1, False, 3))
                dve.wait_ge(first, k_sy)
                d.up(mult(m1s[:, :, 0:CS], sy[:], w_ss))
                dve.wait_ge(first, k_dot)
                d.up(mult(m1s[:, :, CS:CS + CV], dsum[:], w_vv0))
                assert d.n == DONE_S
                k_sw = d.up(mult(sw[:], s, w_sv))
                k_wy = d.up(mult(wy[:], w_vs, bc(y0, 2, CV)))
                cross_parts(c1, c2, lambda x: cross[:, :, x, :], d, k_c)
                dve.wait_ge(first, k_sw)
                d.up(mult(m1v[:, :, :, 0:CS], bc(sw[:], 2, 3), bc(yx, 3, CS)))
                dve.wait_ge(first, k_wy)
                k = d.up(mult(m1v[:, :, :, CS:CS + CV], v, bc(wy[:], 2, 3)))
                dve.wait_ge(first, k - 2)
                d.up(mult(m1v[:, :, :, CS + CV:P], cross[:], bc(w_vv1, 2, 3)))
                assert d.n == FIRST == DONE_V

            def second_product(v, r, i):
                if not present(v):
                    return
                d = Count(second, v, SECOND)
                y0, yx = y[:, r, :, 0], y[:, r, :, 1:4]
                sg, gt = sig[:, r % 2], gate[:, r % 2]
                dve.wait_ge(acted, v * ACTED + 2)
                vectors = ps_g[:].rearrange("p (t x c) -> p t x c", x=4, c=CV)[:, :, 1:4, :]
                if present(v - 1):
                    dve.wait_ge(turned, turn(v - 1, True, 3))
                k_gv = d.up(mult(gv[:], vectors, bc(gt, 2, 3)))
                d.up(mult(m2s[:, :, 0:CS], sg, bc(y0, 2, CS)))
                d.up(mult(m2v[:, :, :, 0:CS], bc(sg, 2, 3), bc(yx, 3, CS)))
                dve.wait_ge(second, k_gv)
                k_vy = d.up(mult(vy2[:], gv[:], bc(yx, 3, CV)))
                d.up(mult(d1[:], gv[:], bc(y[:, r, :, 2:5], 3, CV)))
                dve.wait_ge(second, k_vy)
                k_dot = d.up(add(dsum2[:], vy2[:, :, 0, :], vy2[:, :, 1, :]))
                k_c = d.up(mult(d2[:], gv[:], bc(y[:, r, :, 3:6], 3, CV)))
                dve.wait_ge(second, k_dot)
                d.up(add(m2s[:, :, CS:CS + CV], dsum2[:], vy2[:, :, 2, :]))
                assert d.n == DONE2_S
                d.up(mult(m2v[:, :, :, CS:CS + CV], gv[:], bc(bc(y0, 2, 3), 3, CV)))
                cross_parts(d1, d2, lambda x: m2v[:, :, x, CS + CV:P], d, k_c)
                assert d.n == DONE2_V
                dve.wait_ge(weighted, v * 2 + 2)
                d.up(nc.vector.tensor_reduce(logits[:, bass.ds(v * T, T), :],
                                             weighed[:].rearrange("p t (h k) -> p t h k", k=AS), AX, ALU.add))
                assert d.n == SECOND

            def body(u, r, i):
                first_product(u, r, i)
                second_product(u - 1, (r - 1) % RING, None)

            rounds(dve, body)
            second_product(groups - 1, RING - 1, None)
            dve.wait_ge(second, groups * SECOND)


def softmax(nc, dst_windows, logits, ident):
    tiles = logits.shape[1]
    parts = tiles // SEG_TILES
    edges_on = SEG_TILES * P
    with ExitStack() as ctx:
        def sb(n, shape, dt=F32):
            return ctx.enter_context(nc.sbuf_tensor(f"s_{n}", shape, dt))

        def sem(n):
            return ctx.enter_context(nc.semaphore(f"s_{n}"))

        dst_i = sb("dst_i", [parts, edges_on + 2], I32)
        dst = sb("dst", [parts, edges_on + 2])
        breaks = [sb(f"breaks{i}", [parts, edges_on]) for i in range(2)]
        broken = sb("broken", [parts, 2])
        rows = sb("rows", [parts, HEADS, edges_on])
        best = sb("best", [parts, HEADS, edges_on])
        ends = sb("ends", [parts, 2, HEADS])
        breaks4 = sb("breaks4", [parts, 2, HEADS])
        turned_ends = sb("turned_ends", [HEADS, 2, 2 * P])
        carried = sb("carried", [HEADS, 2, parts + 1])
        start = sb("start", [parts, 2, HEADS])
        ps_in = [ctx.enter_context(nc.psum_tensor(f"s_in{i}", [P, 512], F32)) for i in range(2)]
        ps_out = [ctx.enter_context(nc.psum_tensor(f"s_out{i}", [P, 512], F32)) for i in range(2)]
        ps_c = ctx.enter_context(nc.psum_tensor("s_c", [P, 512], F32))
        loaded, own, turned, taken, back, ended, expd = (sem("loaded"), sem("dve"), sem("turned"), sem("taken"),
                                                        sem("back"), sem("ended"), sem("exp"))
        by_tile = logits[:].rearrange("p (q c) h -> p c q h", c=SEG_TILES)
        block = ctx.enter_context(nc.Block())
        C4 = SEG_TILES // 4
        SETUP = 7
        PASS = 2 * HEADS + 6

        @block.sync
        def _(sp):
            sp.dma_start(dst_i[:], dst_windows).then_inc(loaded, 16)

        @block.tensor
        def _(pe):
            for n in range(HEADS * C4):
                hd, c4 = n // C4, n % C4
                if n >= 2:
                    pe.wait_ge(taken, n - 1)
                for j in range(4):
                    last = nc.tensor.transpose(ps_in[n % 2][0:parts, j * P:(j + 1) * P],
                                               by_tile[:, c4 * 4 + j, :, hd], ident[:])
                last.then_inc(turned, 1)
            for side in range(2):
                pe.wait_ge(own, SETUP + side * PASS + HEADS + 2)
                nc.tensor.transpose(ps_c[0:HEADS, 0:parts], ends[:, side, :], ident[0:parts, 0:parts])
                nc.tensor.transpose(ps_c[0:HEADS, P:P + parts], breaks4[:, side, :],
                                    ident[0:parts, 0:parts]).then_inc(ended, 1)
                pe.wait_ge(own, SETUP + side * PASS + HEADS + 5)
                before = carried[:, side, 0:parts] if side == 0 else carried[:, side, 1:parts + 1]
                nc.tensor.transpose(ps_c[0:parts, 256:256 + HEADS], before,
                                    ident[0:HEADS, 0:HEADS]).then_inc(ended, 1)
            pe.wait_ge(own, SETUP + 2 * PASS)
            for n in range(HEADS * C4):
                hd, c4 = n // C4, n % C4
                if n >= 2:
                    pe.wait_ge(own, SETUP + 2 * PASS + n - 1)
                for j in range(4):
                    at = (c4 * 4 + j) * P
                    last = nc.tensor.transpose(ps_out[n % 2][:, j * P:j * P + parts],
                                               rows[:, hd, at:at + P], ident[0:parts, 0:parts])
                last.then_inc(back, 1)

        @block.scalar
        def _(act):
            for n in range(HEADS * C4):
                hd, c4 = n // C4, n % C4
                act.wait_ge(turned, n + 1)
                nc.scalar.activation(rows[:, hd, c4 * 512:(c4 + 1) * 512], ps_in[n % 2][0:parts, :],
                                     ACT.Copy).then_inc(taken, 1)
            act.wait_ge(own, SETUP + 2 * PASS + HEADS * C4)
            nc.scalar.activation(logits[:], logits[:], ACT.Exp).then_inc(expd, 1)
            act.wait_ge(expd, 1)

        @block.vector
        def _(dve):
            d = Count(own, 0, 0)
            dve.wait_ge(loaded, 16)
            dve.wait_ge(own, d.up(nc.vector.tensor_copy(dst[:], dst_i[:])))
            for side in range(2):
                k = d.up(nc.vector.tensor_tensor(breaks[side][:], dst[:, 1:edges_on + 1],
                                                 dst[:, 2 * side:2 * side + edges_on], ALU.not_equal))
                dve.wait_ge(own, k)
                k = d.up(nc.vector.tensor_scalar(breaks[side][:], breaks[side][:], -FAR, None, ALU.mult))
                dve.wait_ge(own, k)
                d.up(nc.vector.tensor_reduce(broken[:, side:side + 1], breaks[side][:], AX, ALU.min))
            assert d.n == SETUP
            dve.wait_ge(taken, HEADS * C4)
            for side in range(2):
                def scans(initial):
                    for hd in range(HEADS):
                        first = -FAR if initial is None else initial[:, hd:hd + 1]
                        if side == 0:
                            out, step, fed = best[:, hd, :], breaks[0][:], rows[:, hd, :]
                        else:
                            out, step, fed = rows[:, hd, ::-1], breaks[1][:, ::-1], best[:, hd, ::-1]
                        d.up(nc.vector.tensor_tensor_scan(out=out, data0=step, data1=fed, initial=first,
                                                          op0=ALU.add, op1=ALU.max))
                    dve.wait_ge(own, d.n)

                scans(None)
                d.up(nc.vector.tensor_copy(ends[:, side, :],
                                           best[:, :, edges_on - 1] if side == 0 else rows[:, :, 0]))
                d.up(nc.vector.tensor_copy(breaks4[:, side, :],
                                           broken[:, side:side + 1].broadcast_to([parts, HEADS])))
                dve.wait_ge(ended, 2 * side + 1)
                d.up(nc.vector.tensor_copy(turned_ends[:, side, :].rearrange("h (k q) -> h k q", k=2)[:, :, 0:parts],
                                           ps_c[0:HEADS, 0:2 * P].rearrange("h (k q) -> h k q", k=2)[:, :, 0:parts]))
                outside = 0 if side == 0 else parts
                d.up(nc.vector.memset(carried[:, side, outside:outside + 1], -FAR))
                dve.wait_ge(own, d.n)
                last, broke = turned_ends[:, side, 0:parts], turned_ends[:, side, P:P + parts]
                if side == 0:
                    out = carried[:, side, 1:parts + 1]
                else:
                    out, last, broke = (a[:, ::-1] for a in (carried[:, side, 0:parts], last, broke))
                d.up(nc.vector.tensor_tensor_scan(out=out, data0=broke, data1=last, initial=-FAR,
                                                  op0=ALU.add, op1=ALU.max))
                dve.wait_ge(ended, 2 * side + 2)
                d.up(nc.vector.tensor_copy(start[:, side, :], ps_c[0:parts, 2 * P:2 * P + HEADS]))
                dve.wait_ge(own, d.n)
                scans(start[:, side, :])
            assert d.n == SETUP + 2 * PASS
            for n in range(HEADS * C4):
                hd, c4 = n // C4, n % C4
                dve.wait_ge(back, n + 1)
                part = by_tile[:, c4 * 4:c4 * 4 + 4, :, hd]
                d.up(nc.vector.tensor_tensor(
                    part, part, ps_out[n % 2][:].rearrange("p (c q) -> p c q", c=4)[:, :, 0:parts], ALU.subtract))


def reduce_values(nc, h_d, unit_row, slot_row, b128, keep, dst_tiles, weights_of_edges, sums_d, iota):
    steps = b128.shape[1]
    groups = h_d.shape[0]
    T = TILES
    with ExitStack() as ctx:
        def sb(n, shape, dt=F32):
            return ctx.enter_context(nc.sbuf_tensor(f"r_{n}", shape, dt))

        def sem(n):
            return ctx.enter_context(nc.semaphore(f"r_{n}"))

        h = sb("h", [P, 2, T, HROW + 1])
        headed = [h[:, r, :, 0:HROW].rearrange("p t (h k) -> p t h k", h=HEADS) for r in range(2)]
        rel = sb("rel", [P, 2, T])
        dst_i = sb("dst_i", list(dst_tiles.shape), I32)
        dst = sb("dst", list(dst_tiles.shape))
        onehot = sb("onehot", [P, 2, T, P])
        acc = sb("acc", [P, 2, HROW + 1])
        ps = [ctx.enter_context(nc.psum_tensor(f"r_ps{i}", [P, 512], F32)) for i in range(2)]
        loaded, stored = [sem(f"loaded{i}") for i in range(2)], [sem(f"stored{i}") for i in range(2)]
        dst_in, dst_f, weighed, hot, added, multiplied = (sem("dst_in"), sem("dst_f"), sem("weighed"), sem("hot"),
                                                          sem("added"), sem("multiplied"))
        block = ctx.enter_context(nc.Block())

        @block.sync
        def _(sp):
            sp.dma_start(dst_i[:], dst_tiles).then_inc(dst_in, 16)

            def load(s, r, i):
                unit = sp.value_load(unit_row[0:1, bass.ds(s, 1)], min_val=0, max_val=groups - 1)
                wait(sp, multiplied, s - 1)
                sp.dma_start(h[:, r, :, 0:HROW], h_d[unit].rearrange("p (t k) -> p t k", t=T)).then_inc(loaded[r], 16)

            def store(s, r, i):
                slot = sp.value_load(slot_row[0:1, bass.ds(s, 1)], min_val=0, max_val=sums_d.shape[0] - 1)
                sp.wait_ge(added, s + 1)
                sp.dma_start(sums_d[slot], acc[:, r, :]).then_inc(stored[r], 16)

            load(0, 0, 0)
            load(1, 1, 0)
            with sp.Fori(0, steps // 2 - 1) as i:
                for r in range(2):
                    store(i * 2 + r, r, i)
                    load(i * 2 + (r + 2), r, i + 1)
            for r in range(2):
                store(steps - 2 + r, r, steps // 2 - 1)
            for r in range(2):
                sp.wait_ge(stored[r], 16 * (steps // 2))

        def steps_of(engine, body):
            for r in range(2):
                body(r, r, 0)
            with engine.Fori(1, steps // 2) as i:
                for r in range(2):
                    body(i * 2 + r, r, i)

        @block.gpsimd
        def _(pool):
            pool.wait_ge(dst_in, 16)
            nc.gpsimd.tensor_copy(dst[:], dst_i[:]).then_inc(dst_f, 1)
            nc.gpsimd.memset(h[:, :, :, HROW:HROW + 1], 1.0).then_inc(dst_f, 1)
            pool.wait_ge(dst_f, 2)

            def body(s, r, i):
                unit = pool.value_load(unit_row[0:1, bass.ds(s, 1)], min_val=0, max_val=groups - 1)
                wait(pool, hot, s - 1)
                nc.gpsimd.tensor_tensor(rel[:, r, :], dst[:, bass.ds(unit * T, T)],
                                        b128[:, bass.ds(s, 1)].broadcast_to([P, T]), ALU.subtract).then_inc(weighed, 1)
                pool.wait_ge(loaded[r], (i + 1) * 16)
                nc.gpsimd.tensor_tensor(
                    headed[r], headed[r], bc(weights_of_edges[:, bass.ds(unit * T, T), :], 3, HW + 1),
                    ALU.mult).then_inc(weighed, 1)

            steps_of(pool, body)

        @block.vector
        def _(dve):
            def hots(s, r, i):
                dve.wait_ge(weighed, s * 2 + 1)
                wait(dve, multiplied, s - 1)
                nc.vector.tensor_tensor(onehot[:, r], bc(iota[:], 1, T), bc(rel[:, r, :], 2, P),
                                        ALU.is_equal).then_inc(hot, 1)

            def add(s, r, i):
                dve.wait_ge(multiplied, s + 1)
                wait(dve, stored[r], i * 16)
                wait(dve, added, s)
                if isinstance(s, int) and s == 0:
                    nc.vector.tensor_copy(acc[:, 0, :], ps[0][:, 0:HROW + 1]).then_inc(added, 1)
                else:
                    nc.vector.scalar_tensor_tensor(acc[:, r, :], acc[:, 1 - r, :], keep[:, bass.ds(s, 1)],
                                                   ps[r][:, 0:HROW + 1], ALU.mult, ALU.add).then_inc(added, 1)

            hots(0, 0, 0)
            hots(1, 1, 0)
            add(0, 0, 0)
            with dve.Fori(0, steps // 2 - 1) as i:
                hots(i * 2 + 2, 0, i + 1)
                add(i * 2 + 1, 1, i)
                hots(i * 2 + 3, 1, i + 1)
                add(i * 2 + 2, 0, i + 1)
            add(steps - 1, 1, steps // 2 - 1)
            dve.wait_ge(added, steps)

        @block.tensor
        def _(pe):
            def body(s, r, i):
                pe.wait_ge(hot, s + 1)
                pe.wait_ge(weighed, s * 2 + 2)
                wait(pe, added, s - 1)
                for t in range(T):
                    last = nc.tensor.matmul(ps[r][:, 0:HROW + 1], onehot[:, r, t, :],
                                            h[:, r, t, :], start=t == 0, stop=t == T - 1)
                last.then_inc(multiplied, 1)

            steps_of(pe, body)


def norm_steps(nc, dve, d, z, centred, squares, stat, root, rinv, rooted, round_, out):
    mean = stat[:, CHUNK:2 * CHUNK]
    spread = stat[:, 0:CHUNK]

    def then(instruction):
        dve.wait_ge(d.sem, d.up(instruction))

    then(nc.vector.tensor_reduce(mean, z, AX, ALU.add))
    then(nc.vector.tensor_scalar(mean, mean, 1.0 / D, None, ALU.mult))
    then(nc.vector.tensor_tensor(centred, z, bc(mean, 2, D), ALU.subtract))
    then(nc.vector.tensor_tensor(squares, centred, centred, ALU.mult))
    then(nc.vector.tensor_reduce(spread, squares, AX, ALU.add))
    d.up(nc.vector.tensor_scalar(spread, spread, 1.0 / D, EPS, ALU.mult, ALU.add))
    dve.wait_ge(rooted, round_ + 1)
    then(nc.vector.reciprocal(rinv, root))
    then(nc.vector.tensor_tensor(out, centred, bc(rinv, 2, D), ALU.mult))


def middle(nc, xn, sums_d, factor_d, table, resid_d, w, w1, ident):
    chunks = xn.shape[0] // P // CHUNK
    with ExitStack() as ctx:
        def sb(n, shape, dt=F32):
            return ctx.enter_context(nc.sbuf_tensor(f"m_{n}", shape, dt))

        def sem(n):
            return ctx.enter_context(nc.semaphore(f"m_{n}"))

        x, z, zc, zq, x1 = (sb(n, [P, CHUNK, D]) for n in ("x", "z", "zc", "zq", "x1"))
        rest = sb("rest", [P, CHUNK, D + 1])
        sums = sb("sums", [P, CHUNK, HROW + 1])
        by_head = sums[:, :, 0:HROW].rearrange("p b (h k) -> p b h k", h=HEADS)
        factor = sb("factor", [P, CHUNK])
        den = sb("den", [P, CHUNK, HEADS])
        agg = sb("agg", [P, CHUNK, HEADS, HW])
        stat, root, rinv = sb("stat", [P, 2 * CHUNK]), sb("root", [P, CHUNK]), sb("rinv", [P, CHUNK])
        wp_a, wp_b = sb("wp_a", [P, D]), sb("wp_b", [D - P, D])
        wl_a, wl_b = sb("wl_a", [P, 2 * D]), sb("wl_b", [CV, 2 * D])
        t_a, t_b = sb("t_a", [P, 2, P]), sb("t_b", [CV, 2, P])
        o = sb("o", [P, CHUNK, 2 * D])
        pt = [ctx.enter_context(nc.psum_tensor(f"m_pt{i}", [P, 512], F32)) for i in range(2)]
        po = [ctx.enter_context(nc.psum_tensor(f"m_po{i}", [P, 512], F32)) for i in range(2)]
        zeroed, weights, loaded, own, rooted = sem("zeroed"), sem("weights"), sem("loaded"), sem("dve"), sem("rooted")
        turned, copied, multiplied, moved, stored = (sem("turned"), sem("copied"), sem("multiplied"), sem("moved"),
                                                     sem("stored"))
        rested = sem("rested")
        AGG, OUT0 = 4, 4 + CHUNK
        SPREAD, NORMED = OUT0 + 6, OUT0 + 8
        PER = NORMED + 1
        SCALES = 3
        xv = xn.rearrange("(c b p) f -> c p b f", b=CHUNK, p=P)
        tv = table.rearrange("(c b p) f -> c p b f", b=CHUNK, p=P)
        rv = resid_d.rearrange("(c b p) f -> c p b f", b=CHUNK, p=P)
        sums_v = sums_d[0:chunks * CHUNK].rearrange("(c b) p f -> c p b f", b=CHUNK)
        placements = []

        def place(lo, hi, row0, col0, source):
            n, m = source.shape
            cut = max(0, min(n, P - row0))
            if cut:
                placements.append((lo[row0:row0 + cut, col0:col0 + m], source[0:cut, :]))
            if cut < n:
                at = row0 + cut - P
                placements.append((hi[at:at + n - cut, col0:col0 + m], source[cut:n, :]))

        for hd in range(HEADS):
            place(wp_a, wp_b, hd * HW, 0, w["Wps"][hd * AS:(hd + 1) * AS, :])
            for comp in range(3):
                place(wp_a, wp_b, hd * HW + AS + comp * AV, CS + comp * CV, w["Wpv"][hd * AV:(hd + 1) * AV, :])
        for side, (ws, wv) in enumerate((("Wl1_0", "Wl1_1"), ("Wsc0", "Wsc1"))):
            place(wl_a, wl_b, 0, side * D, w1[ws])
            for comp in range(3):
                place(wl_a, wl_b, CS + comp * CV, side * D + CS + comp * CV, w1[wv])
        block = ctx.enter_context(nc.Block())

        @block.sync
        def _(sp):
            sp.wait_ge(zeroed, 4)
            for into, source in placements:
                sp.dma_start(into, source).then_inc(weights, 16)
            with sp.Fori(0, chunks) as c:
                sp.dma_start(x[:], xv[c]).then_inc(loaded, 16)
                sp.dma_start(sums[:], sums_v[c]).then_inc(loaded, 16)
                sp.dma_start(factor[:], factor_d[c]).then_inc(loaded, 16)
                sp.wait_ge(own, (c + 1) * PER + SCALES)
                sp.dma_start(tv[c], o[:, :, 0:D]).then_inc(stored, 16)
                sp.dma_start(rv[c], rest[:]).then_inc(stored, 16)
                sp.wait_ge(stored, (c + 1) * 32)
                sp.sem_inc(rested, 1)

        @block.gpsimd
        def _(pool):
            for tile in (wp_a, wp_b, wl_a, wl_b):
                nc.gpsimd.memset(tile[:], 0.0).then_inc(zeroed, 1)

        def project(act, c, b):
            act.wait_ge(multiplied, c * 2 * CHUNK + (CHUNK + b + 2))
            nc.scalar.activation(o[:, b, :], po[b % 2][:, 0:2 * D], ACT.Copy,
                                 scale=factor[:, b:b + 1]).then_inc(moved, 1)

        @block.scalar
        def _(act):
            act.wait_ge(weights, 16 * len(placements))
            with act.Fori(0, chunks) as c:
                for n in range(2 * CHUNK):
                    b = n % CHUNK
                    if n == CHUNK:
                        act.wait_ge(own, c * PER + (SCALES + SPREAD))
                        nc.scalar.activation(root[:], stat[:, 0:CHUNK], ACT.Sqrt).then_inc(rooted, 1)
                    act.wait_ge(turned, c * 2 * CHUNK + (n + 1))
                    act.wait_ge(multiplied, c * 2 * CHUNK + (n + 1))
                    nc.scalar.activation(t_a[:, b % 2, :], pt[b % 2][:, 0:P], ACT.Copy)
                    nc.scalar.activation(t_b[:, b % 2, :], pt[b % 2][0:CV, P:2 * P], ACT.Copy).then_inc(copied, 1)
                    if n > CHUNK:
                        project(act, c, b - 1)
                project(act, c, CHUNK - 1)

        @block.tensor
        def _(pe):
            pe.sem_inc(multiplied, 1)
            pe.wait_ge(weights, 16 * len(placements))
            pe.wait_ge(own, SCALES)
            with pe.Fori(0, chunks) as c:
                for half in range(2):
                    pe.wait_ge(own, c * PER + (SCALES + (AGG if half == 0 else NORMED)))
                    for b in range(CHUNK + 1):
                        if b < CHUNK:
                            rows = (agg[:, b].rearrange("p h k -> p (h k)") if half == 0 else x1[:, b, :])
                            nc.tensor.transpose(pt[b % 2][:, 0:P], rows[:, 0:P], ident[:])
                            nc.tensor.transpose(pt[b % 2][0:CV, P:2 * P], rows[:, P:D], ident[:]).then_inc(turned, 1)
                        if b >= 1:
                            pe.wait_ge(copied, c * 2 * CHUNK + (half * CHUNK + b))
                            if half == 0:
                                if b >= 3:
                                    pe.wait_ge(own, c * PER + (SCALES + AGG + b - 2))
                                else:
                                    pe.wait_ge(moved, c * CHUNK)
                            elif b >= 3:
                                pe.wait_ge(moved, c * CHUNK + (b - 2))
                            width = D if half == 0 else 2 * D
                            wa, wb = (wp_a, wp_b) if half == 0 else (wl_a, wl_b)
                            nc.tensor.matmul(po[(b - 1) % 2][:, 0:width], t_a[:, (b - 1) % 2, :], wa[:],
                                             start=True, stop=False)
                            nc.tensor.matmul(po[(b - 1) % 2][:, 0:width], t_b[:, (b - 1) % 2, :], wb[:],
                                             start=False, stop=True).then_inc(multiplied, 1)

        @block.vector
        def _(dve):
            dve.wait_ge(weights, 16 * len(placements))
            inv8, inv32 = 1.0 / math.sqrt(CS), 1.0 / math.sqrt(CV)
            for tile, by in ((wl_a[0:CS], inv8), (wl_a[CS:P], inv32), (wl_b[:], inv32)):
                nc.vector.tensor_scalar(tile, tile, by, None, ALU.mult).then_inc(own, 1)
            with dve.Fori(0, chunks) as c:
                d = Count(own, c, PER)
                d.base = d.base + SCALES
                dve.wait_ge(loaded, (c + 1) * 48)
                dve.wait_ge(own, d.up(nc.vector.tensor_scalar(den[:], by_head[:, :, :, HW], 1e-16, None, ALU.add)))
                dve.wait_ge(own, d.up(nc.vector.reciprocal(den[:], den[:])))
                d.up(nc.vector.tensor_scalar(rest[:, :, D], sums[:, :, HROW], 1.0, None, ALU.max))
                d.up(nc.vector.tensor_tensor(agg[:], by_head[:, :, :, 0:HW], bc(den[:], 3, HW), ALU.mult))
                for b in range(CHUNK):
                    dve.wait_ge(multiplied, c * 2 * CHUNK + (b + 2))
                    k = d.up(nc.vector.scalar_tensor_tensor(z[:, b, :], x[:, b, :], 2.0, po[b % 2][:, 0:D],
                                                            ALU.mult, ALU.add))
                dve.wait_ge(own, k)
                norm_steps(nc, dve, d, z[:], zc[:], zq[:], stat, root[:], rinv[:], rooted, c, x1[:])
                assert d.n == NORMED
                dve.wait_ge(moved, (c + 1) * CHUNK)
                d.up(nc.vector.tensor_tensor(rest[:, :, 0:D], x1[:], o[:, :, D:2 * D], ALU.add))
                assert d.n == PER


def edges1(nc, src_d, dst_d, y_d, rbf_d, table, unit_row, slot_row, b128, keep, w1, iota, sums_d):
    steps = b128.shape[1]
    units = src_d.shape[0]
    T = UNIT1
    W = T * P
    with ExitStack() as ctx:
        def sb(n, shape, dt=F32):
            return ctx.enter_context(nc.sbuf_tensor(f"f_{n}", shape, dt))

        def sem(n):
            return ctx.enter_context(nc.semaphore(f"f_{n}"))

        def ring_sem(n, size):
            return [sem(f"{n}{r}") for r in range(size)]

        w_1, w_2 = sb("w_1", [16, CS]), sb("w_2", [CS, WE])
        src, dst = sb("src", [P, RING, T], I32), sb("dst", [P, RING, T], I32)
        y, rbf = sb("y", [P, RING, T, 4]), sb("rbf", [16, RING, W])
        e = sb("e", [P, RING, T, D])
        hidden = sb("hidden", [CS, 2, W])
        q = sb("q", [P, 2, T, 2 * CS + 6 * CV])
        rel = sb("rel", [P, 2, T])
        onehot = sb("onehot", [P, 2, T, P])
        hot = sb("hot", [P, 2, T, 4, P])
        acc = sb("acc", [P, 2, ACC1])
        ps_h = [ctx.enter_context(nc.psum_tensor(f"f_ps_h{i}", [P, 512], F32)) for i in range(2)]
        ps_w = [ctx.enter_context(nc.psum_tensor(f"f_ps_w{i}", [P, 512], F32)) for i in range(2)]
        ps_a = [ctx.enter_context(nc.psum_tensor(f"f_ps_a{i}", [P, 512], F32)) for i in range(2)]
        weights, scaled = sem("weights"), sem("scaled")
        src_in, rest_in, rbf_in, gathered = (ring_sem(n, RING) for n in ("src_in", "rest_in", "rbf_in", "gathered"))
        stored = ring_sem("stored", 2)
        hid, silu, radial, product, hot_d, hot_a, multiplied, added, issued = (
            sem(n) for n in ("hid", "silu", "radial", "product", "hot_d", "hot_a", "multiplied", "added", "issued"))
        HOT, PRODUCT = 3, 3

        def rounds(engine, body):
            for r in range(RING):
                body(r, r, 0)
            last = steps // RING - 1
            with engine.Fori(1, last) as i:
                for r in range(RING):
                    body(i * RING + r, r, i)
            for r in range(RING):
                body(last * RING + r, r, last)

        def present(s):
            return not isinstance(s, int) or 0 <= s < steps

        block = ctx.enter_context(nc.Block())

        @block.sync
        def _(sp):
            sp.dma_start(w_1[:], w1["Wfc1"]).then_inc(weights, 16)
            sp.dma_start(w_2[:], w1["Wfc2"]).then_inc(weights, 16)

            def body(s, r, i):
                unit = sp.value_load(unit_row[0:1, bass.ds(s, 1)], min_val=0, max_val=units - 1)
                at = sp.snap(unit * W)
                wait(sp, gathered[r], i * 16 * T)
                sp.dma_start(src[:, r, :], src_d[unit]).then_inc(src_in[r], 16)
                wait(sp, hid, s - (RING - 1))
                sp.dma_start(rbf[:, r, :], rbf_d[:, bass.ds(at, W)]).then_inc(rbf_in[r], 16)
                wait(sp, hot_d, (s - (RING - 1)) * HOT)
                wait(sp, hot_a, s - (RING - 1))
                sp.dma_start(dst[:, r, :], dst_d[unit]).then_inc(rest_in[r], 16)
                sp.dma_start(y[:, r], y_d[unit]).then_inc(rest_in[r], 16)
                if present(s - 4):
                    store(s - 4, r % 2)

            def store(s, slot2):
                slot = sp.value_load(slot_row[0:1, bass.ds(s, 1)], min_val=0, max_val=sums_d.shape[0] - 1)
                sp.wait_ge(added, s + 1)
                sp.dma_start(sums_d[slot], acc[:, slot2, :]).then_inc(stored[slot2], 16)

            rounds(sp, body)
            for r in range(RING):
                store(steps - RING + r, r % 2)
            for slot2 in range(2):
                sp.wait_ge(stored[slot2], 16 * (steps // 2))

        @block.gpsimd
        def _(pool):
            def gather(s, r, i):
                pool.wait_ge(src_in[r], (i + 1) * 16)
                wait(pool, product, (s - (RING - 1)) * PRODUCT)
                pool.sem_inc(issued, 1)
                for t in range(T):
                    pool.indirect_dma_start(
                        out=e[:, r, t, :], out_offset=None, in_=table,
                        in_offset=bass.IndirectOffsetOnAxis(ap=src[:, r, t:t + 1], axis=0),
                    ).then_inc(gathered[r], 16)

            rounds(pool, gather)

        @block.tensor
        def _(pe):
            pe.wait_ge(scaled, 1)

            def hidden_layer(s, r, i):
                if not present(s):
                    return
                pe.wait_ge(rbf_in[r], (i + 1) * 16)
                wait(pe, silu, s - 1)
                nc.tensor.matmul(ps_h[r % 2][0:CS, 0:W], w_1[:], rbf[:, r, :],
                                 start=True, stop=True).then_inc(hid, 1)

            def radial_weights(s, r, i):
                if not present(s):
                    return
                pe.wait_ge(silu, s + 1)
                wait(pe, product, (s - 1) * PRODUCT)
                for t in range(T):
                    last = nc.tensor.matmul(ps_w[r % 2][:, t * 256:t * 256 + WE], hidden[:, r % 2, t * P:(t + 1) * P],
                                            w_2[:], start=True, stop=True)
                last.then_inc(radial, 1)

            def sums(s, r, i):
                slot = r % 2
                into = ps_a[slot]
                vectors = into[:, MID:ACC1].rearrange("p (x c) -> p x c", x=3)
                pe.wait_ge(hot_d, (s + 1) * HOT)
                pe.wait_ge(hot_a, s + 1)
                pe.wait_ge(product, (s + 1) * PRODUCT)
                wait(pe, added, s - 1)
                for t in range(T):
                    of = lambda a, b: q[:, slot, t, a:b]
                    nc.tensor.matmul(into[:, 0:CS], hot[:, slot, t, 0, :], of(0, CS), start=t == 0, stop=False)
                    nc.tensor.matmul(vectors[:, :, CS:MID], hot[:, slot, t, 0, :], of(2 * CS, 2 * CS + 3 * CV),
                                     start=False, stop=False)
                    for x in range(3):
                        at = 2 * CS + (3 + x) * CV
                        nc.tensor.matmul(vectors[:, x, 0:CS], hot[:, slot, t, 1 + x, :], of(CS, 2 * CS),
                                         start=False, stop=False)
                        last = nc.tensor.matmul(into[:, CS:MID], hot[:, slot, t, 1 + x, :], of(at, at + CV),
                                                start=False, stop=t == T - 1 and x == 2)
                last.then_inc(multiplied, 1)

            def body(s, r, i):
                hidden_layer(s + 2, (r + 2) % RING, i + (r + 2) // RING)
                radial_weights(s + 1, (r + 1) % RING, i + (r + 1) // RING)
                sums(s, r, i)

            hidden_layer(0, 0, 0)
            hidden_layer(1, 1, 0)
            radial_weights(0, 0, 0)
            rounds(pe, body)

        @block.scalar
        def _(act):
            def activate(s, r, i):
                if not present(s):
                    return
                act.wait_ge(hid, s + 1)
                wait(act, radial, s - 1)
                nc.scalar.activation(hidden[:, r % 2, :], ps_h[r % 2][0:CS, 0:W], ACT.Silu,
                                     scale=1.0 / math.sqrt(16.0)).then_inc(silu, 1)

            def hots(s, r, i):
                if not present(s):
                    return
                act.wait_ge(hot_d, s * HOT + 2)
                act.wait_ge(rest_in[r], (i + 1) * 32)
                wait(act, multiplied, s - 1)
                for j in range(4):
                    last = nc.scalar.activation(hot[:, r % 2, 1, j, :], onehot[:, r % 2, 1, :], ACT.Copy,
                                                scale=y[:, r, 1, j:j + 1])
                last.then_inc(hot_a, 1)

            def body(s, r, i):
                activate(s + 2, (r + 2) % RING, i + (r + 2) // RING)
                hots(s + 1, (r + 1) % RING, i + (r + 1) // RING)

            activate(0, 0, 0)
            activate(1, 1, 0)
            hots(0, 0, 0)
            rounds(act, body)

        @block.vector
        def _(dve):
            dve.wait_ge(weights, 32)
            nc.vector.tensor_scalar(w_2[:, 0:2 * CS + CV], w_2[:, 0:2 * CS + CV], 1.0 / math.sqrt(CS), None, ALU.mult)
            nc.vector.tensor_scalar(w_2[:, 2 * CS + CV:WE], w_2[:, 2 * CS + CV:WE], 1.0 / math.sqrt(3.0 * CS), None,
                                    ALU.mult).then_inc(scaled, 1)

            def hots(s, r, i):
                if not present(s):
                    return
                d = Count(hot_d, s, HOT)
                slot = r % 2
                dve.wait_ge(rest_in[r], (i + 1) * 32)
                k = d.up(nc.vector.tensor_tensor(rel[:, slot, :], dst[:, r, :],
                                                 b128[:, bass.ds(s, 1)].broadcast_to([P, T]), ALU.subtract))
                wait(dve, hot_a, s - 1)
                dve.wait_ge(hot_d, k)
                k = d.up(nc.vector.tensor_tensor(onehot[:, slot], bc(iota[:], 1, T), bc(rel[:, slot, :], 2, P),
                                                 ALU.is_equal))
                wait(dve, multiplied, s - 1)
                dve.wait_ge(hot_d, k)
                d.up(nc.vector.tensor_tensor(hot[:, slot, 0], bc(onehot[:, slot, 0, :], 1, 4),
                                             bc(y[:, r, 0, :], 2, P), ALU.mult))
                assert d.n == HOT

            def products(s, r, i):
                d = Count(product, s, PRODUCT)
                slot = r % 2
                w = ps_w[slot][:].rearrange("p (t k) -> p t k", t=T)
                of = lambda a, n: q[:, slot, :, a:a + 3 * CV].rearrange("p t (x c) -> p t x c", x=3)
                e0 = e[:, r, :, 0:CS]
                e1 = e[:, r, :, CS:D].rearrange("p t (x c) -> p t x c", x=3)
                dve.wait_ge(gathered[r], (i + 1) * 16 * T)
                dve.wait_ge(radial, s + 1)
                wait(dve, multiplied, s - 1)
                d.up(nc.vector.tensor_tensor(q[:, slot, :, 0:2 * CS].rearrange("p t (k c) -> p t k c", k=2),
                                             w[:, :, 0:2 * CS].rearrange("p t (k c) -> p t k c", k=2),
                                             bc(e0, 2, 2), ALU.mult))
                for k in range(2):
                    at = 2 * CS + k * 3 * CV
                    d.up(nc.vector.tensor_tensor(
                        q[:, slot, :, at:at + 3 * CV].rearrange("p t (x c) -> p t x c", x=3),
                        bc(w[:, :, 2 * CS + k * CV:2 * CS + (k + 1) * CV], 2, 3), e1, ALU.mult))
                assert d.n == PRODUCT

            def add(s, r, i):
                if not present(s):
                    return
                slot = r % 2
                dve.wait_ge(multiplied, s + 1)
                wait(dve, stored[slot], 16 * (i * 2 + r // 2))
                wait(dve, added, s)
                if isinstance(s, int) and s == 0:
                    nc.vector.tensor_copy(acc[:, 0, :], ps_a[0][:, 0:ACC1]).then_inc(added, 1)
                else:
                    nc.vector.scalar_tensor_tensor(acc[:, slot, :], acc[:, 1 - slot, :], keep[:, bass.ds(s, 1)],
                                                   ps_a[slot][:, 0:ACC1], ALU.mult, ALU.add).then_inc(added, 1)

            def body(s, r, i):
                hots(s + 1, (r + 1) % RING, i + (r + 1) // RING)
                products(s, r, i)
                add(s - 1, (r - 1) % RING, i + (r - 1) // RING)

            hots(0, 0, 0)
            rounds(dve, body)
            add(steps - 1, RING - 1, steps // RING - 1)
            dve.wait_ge(added, steps)


def final(nc, sums_d, factor_d, resid_d, out, w1, ident):
    blocks = resid_d.shape[0] // P
    chunks = blocks // CHUNK
    with ExitStack() as ctx:
        def sb(n, shape, dt=F32):
            return ctx.enter_context(nc.sbuf_tensor(f"l_{n}", shape, dt))

        def sem(n):
            return ctx.enter_context(nc.semaphore(f"l_{n}"))

        sums, means = sb("sums", [P, CHUNK, ACC1]), sb("means", [P, CHUNK, ACC1])
        share, factor = sb("share", [P, CHUNK]), sb("factor", [P, CHUNK])
        square, gain = sb("square", [P, CHUNK]), sb("gain", [P, CHUNK])
        resid = sb("resid", [P, CHUNK, D + 1])
        z, zc, zq, o = (sb(n, [P, CHUNK, D]) for n in ("z", "zc", "zq", "o"))
        stat, root, rinv = sb("stat", [P, 2 * CHUNK]), sb("root", [P, CHUNK]), sb("rinv", [P, CHUNK])
        w_s, w_v = sb("w_s", [MID, 1 + CS]), sb("w_v", [MID, CV])
        turned_rows = sb("turned_rows", [MID, 2, 512])
        pt = [ctx.enter_context(nc.psum_tensor(f"l_pt{i}", [P, 512], F32)) for i in range(2)]
        po = [ctx.enter_context(nc.psum_tensor(f"l_po{i}", [P, 512], F32)) for i in range(2)]
        weights, loaded, own, rooted, turned, copied, multiplied, stored, rested = (
            sem(n) for n in ("weights", "loaded", "dve", "rooted", "turned", "copied", "multiplied", "stored",
                             "rested"))
        MEANS, PER_BLOCK = 4, 2
        SPREAD = MEANS + PER_BLOCK * CHUNK + 6
        PER = SPREAD + 2
        block = ctx.enter_context(nc.Block())
        rv = resid_d.rearrange("(c b p) f -> c p b f", b=CHUNK, p=P)
        ov = out.rearrange("(c b p) f -> c p b f", b=CHUNK, p=P)
        sv = sums_d[0:blocks].rearrange("(c b) p f -> c p b f", b=CHUNK)

        @block.sync
        def _(sp):
            sp.dma_start(w_s[:, 0:1], w1["Wa"]).then_inc(weights, 16)
            sp.dma_start(w_s[:, 1:1 + CS], w1["Wl2_s"]).then_inc(weights, 16)
            sp.dma_start(w_v[:], w1["Wl2_v"]).then_inc(weights, 16)
            with sp.Fori(0, chunks) as c:
                sp.dma_start(sums[:], sv[c]).then_inc(loaded, 16)
                sp.dma_start(factor[:], factor_d[c]).then_inc(loaded, 16)
                sp.dma_start(resid[:], rv[c]).then_inc(loaded, 16)
                sp.wait_ge(own, (c + 1) * PER)
                sp.dma_start(ov[c], o[:]).then_inc(stored, 16)
                sp.wait_ge(stored, (c + 1) * 16)
                sp.sem_inc(rested, 1)

        @block.tensor
        def _(pe):
            pe.sem_inc(multiplied, 1)
            pe.wait_ge(weights, 48)
            with pe.Fori(0, chunks) as c:
                pe.wait_ge(own, c * PER + MEANS)
                for b in range(CHUNK + 1):
                    if b < CHUNK:
                        for k in range(4):
                            last = nc.tensor.transpose(pt[b % 2][0:MID, k * P:(k + 1) * P],
                                                       means[:, b, k * MID:(k + 1) * MID], ident[:])
                        last.then_inc(turned, 1)
                    if b >= 1:
                        pe.wait_ge(copied, c * CHUNK + b)
                        if b >= 3:
                            pe.wait_ge(own, c * PER + (MEANS + PER_BLOCK * (b - 2)))
                        rows, into = turned_rows[:, (b - 1) % 2, :], po[(b - 1) % 2]
                        nc.tensor.matmul(into[:, 0:1 + CS], rows[:, 0:P], w_s[:], start=True, stop=True)
                        for x in range(3):
                            at = 1 + CS + x * CV
                            last = nc.tensor.matmul(into[:, at:at + CV], rows[:, (1 + x) * P:(2 + x) * P], w_v[:],
                                                    start=True, stop=True)
                        last.then_inc(multiplied, 1)

        @block.scalar
        def _(act):
            with act.Fori(0, chunks) as c:
                for b in range(CHUNK):
                    act.wait_ge(turned, c * CHUNK + (b + 1))
                    act.wait_ge(multiplied, c * CHUNK + (b + 1))
                    nc.scalar.activation(turned_rows[:, b % 2, :], pt[b % 2][0:MID, :], ACT.Copy).then_inc(copied, 1)
                act.wait_ge(own, c * PER + SPREAD)
                nc.scalar.activation(root[:], stat[:, 0:CHUNK], ACT.Sqrt).then_inc(rooted, 1)

        @block.vector
        def _(dve):
            with dve.Fori(0, chunks) as c:
                d = Count(own, c, PER)
                dve.wait_ge(loaded, (c + 1) * 48)
                k2 = d.up(nc.vector.tensor_tensor(square[:], factor[:], factor[:], ALU.mult))
                k = d.up(nc.vector.reciprocal(share[:], resid[:, :, D]))
                dve.wait_ge(own, k2)
                d.up(nc.vector.tensor_scalar(square[:], square[:], 1.0 / MID, None, ALU.mult))
                dve.wait_ge(own, k)
                d.up(nc.vector.tensor_tensor(means[:], sums[:], bc(share[:], 2, ACC1), ALU.mult))
                assert d.n == MEANS
                for b in range(CHUNK):
                    dve.wait_ge(multiplied, c * CHUNK + (b + 2))
                    k = d.up(nc.vector.tensor_tensor(gain[:, b:b + 1], po[b % 2][:, 0:1], square[:, b:b + 1],
                                                     ALU.mult))
                    dve.wait_ge(own, k)
                    k = d.up(nc.vector.scalar_tensor_tensor(z[:, b, :], po[b % 2][:, 1:1 + D], gain[:, b:b + 1],
                                                            resid[:, b, 0:D], ALU.mult, ALU.add))
                dve.wait_ge(own, k)
                norm_steps(nc, dve, d, z[:], zc[:], zq[:], stat, root[:], rinv[:], rooted, c, o[:])
                assert d.n == PER


def message_passing(nc, xn, idx, harmonics, rbf, dst_windows, dst_tiles, first512, first256, src2, dst2,
                    harmonics2, factor, w, w1, out):
    padded, groups = xn.shape[0], idx.shape[0]
    blocks, units = padded // P, src2.shape[0]
    tiles = groups * TILES

    def dram(name, shape):
        return nc.dram_tensor(name, shape, F32, kind="Internal").ap()

    table_src, table_dst = dram("table_src", [padded, D]), dram("table_dst", [padded, D])
    h = dram("edge_values", [groups, P, TILES * HROW])
    sums0, sums1 = dram("sums0", [blocks + SPARE, P, HROW + 1]), dram("sums1", [blocks + SPARE, P, ACC1])
    table1, resid = dram("table1", [padded, D]), dram("resid", [padded, D + 1])

    with ExitStack() as ctx:
        ident = ctx.enter_context(nc.sbuf_tensor("ident", [P, P], F32))
        iota = ctx.enter_context(nc.sbuf_tensor("iota", [P, P], F32))
        constants(nc, ident, iota)

        def walk(inner, name, steps):
            return (inner.enter_context(nc.sbuf_tensor(f"{name}_unit", [1, steps], I32)),
                    inner.enter_context(nc.sbuf_tensor(f"{name}_slot", [1, steps], I32)),
                    inner.enter_context(nc.sbuf_tensor(f"{name}_b128", [P, steps], F32)),
                    inner.enter_context(nc.sbuf_tensor(f"{name}_keep", [P, steps], F32)))

        tables(nc, xn, table_src, table_dst, w, ident)
        with ExitStack() as inner:
            logits = inner.enter_context(nc.sbuf_tensor("logits", [P, tiles, HEADS], F32))
            edges(nc, idx, harmonics, rbf, table_src, table_dst, h, w, ident, logits)
            softmax(nc, dst_windows, logits, ident)
            rows = walk(inner, "walk0", staircase_steps(groups, blocks))
            staircase(nc, "st0", first512, groups, blocks, *rows)
            reduce_values(nc, h, *rows, dst_tiles, logits, sums0, iota)
        middle(nc, xn, sums0, factor, table1, resid, w, w1, ident)
        with ExitStack() as inner:
            rows = walk(inner, "walk1", staircase_steps(units, blocks))
            staircase(nc, "st1", first256, units, blocks, *rows)
            edges1(nc, src2, dst2, harmonics2, rbf, table1, *rows, w1, iota, sums1)
        final(nc, sums1, factor, resid, out, w1, ident)


_W0 = ["gamma_s", "beta_s", "gamma_v", "Ws_src", "Wv_src", "Ws_dst", "Wv_dst", "W_rbf", "W_alpha", "alpha_dot",
       "Ws_val", "Wv_val", "Wg", "w2_ss", "w2_sv", "w2_vs", "w2_vv0", "w2_vv1", "Ws_vlin", "Wv_vlin", "Wps", "Wpv"]
_W1 = ["Wfc1", "Wfc2", "Wsc0", "Wsc1", "Wl1_0", "Wl1_1", "Wl2_s", "Wl2_v", "Wa"]


def _layout(x, src, dst, edge_attr_16, edge_attr_4, node_vec1):
    n, n_edges = x.shape[0], src.shape[0]
    blocks = -(-n // (P * CHUNK)) * CHUNK
    padded = blocks * P
    edges_p = -(-n_edges // (SEG_TILES * P)) * SEG_TILES * P

    def pad(a, size, fill=0):
        out = np.full((size,) + a.shape[1:], fill, a.dtype)
        out[:a.shape[0]] = a
        return out

    def tiled(a, tiles):
        return a.reshape((-1, tiles, P) + a.shape[1:]).swapaxes(1, 2)

    xp = pad(x, padded)
    by_component = xp[:, CS:].reshape(padded, CV, 3).transpose(0, 2, 1).reshape(padded, 3 * CV)
    s, d = pad(src, edges_p), pad(dst, edges_p, padded - 1)
    y = pad(edge_attr_4, edges_p)
    none = np.full(1, -1, d.dtype)
    window = np.concatenate([none, d, none])
    span = SEG_TILES * P

    def firsts(size):
        got = d[::size][1:]
        got = pad(got, -(-got.shape[0] // P) * P, 1 << 20)
        return got.reshape(-1, P).T

    return {
        "xn": np.concatenate([xp[:, :CS], by_component], 1),
        "idx": np.concatenate([tiled(s, TILES), tiled(d, TILES)], 2),
        "harmonics": tiled(y[:, [0, 1, 2, 3, 1, 2]], TILES),
        "rbf": pad(edge_attr_16, edges_p).T,
        "dst_windows": np.stack([window[q * span:q * span + span + 2] for q in range(edges_p // span)]),
        "dst_tiles": d.reshape(-1, P).T,
        "first512": firsts(GROUP),
        "first256": firsts(UNIT1 * P),
        "src2": tiled(s, UNIT1),
        "dst2": tiled(d, UNIT1),
        "harmonics2": tiled(y, UNIT1),
        "factor": pad(node_vec1, padded).reshape(-1, CHUNK, P).swapaxes(1, 2),
    }


def kernel(**inputs):
    import concourse.bacc as _bacc
    from concourse import mybir as _mybir
    from concourse.bass_utils import run_bass_kernel_spmd as _run

    nc = _bacc.Bacc("TRN2", target_bir_lowering=False, num_devices=1)
    graph = [np.asarray(inputs[n]) for n in ("x", "src", "dst", "edge_attr_16", "edge_attr_4", "node_vec1")]
    n = graph[0].shape[0]
    arrays = {}

    def given(name, a):
        a = np.ascontiguousarray(a)
        arrays[name] = a
        return nc.dram_tensor(name, a.shape, _mybir.dt.from_np(a.dtype), kind="ExternalInput").ap()

    laid = [given(name, a) for name, a in _layout(*graph).items()]
    w = {k: given("w0_" + k, inputs["L0_gnn_" + k]) for k in _W0}
    w1 = {k: given("w1_" + k, inputs["L1_gnn_" + k]) for k in _W1}
    out = nc.dram_tensor("out", laid[0].shape, _mybir.dt.from_np(np.dtype("float32")), kind="ExternalOutput").ap()
    message_passing(nc, *laid, w, w1, out)
    got = _run(nc, [arrays], core_ids=[0]).results[0]["out"][:n]
    vectors = got[:, CS:].reshape(n, 3, CV).transpose(0, 2, 1).reshape(n, 3 * CV)
    return np.concatenate([got[:, :CS], vectors], 1)
```

```python
import math
from contextlib import ExitStack

import numpy as np

import concourse.bass as bass
from concourse import mybir

P = 128
TILES = 4
GROUP = TILES * P
RING = 4
CS, CV = 64, 32
D = CS + 3 * CV
HEADS, AS, AV = 4, 16, 8
HW = AS + 3 * AV
HROW = HEADS * (HW + 1)
WN = 2 * CS + 3 * CV
WE = 192
SPARE = 2 * RING
SEG_TILES = 16
CHUNK = 7
PAIRS = ((0, 0), (0, 1), (0, 2), (1, 0), (1, 1), (2, 0))
BASIS = 16 * len(PAIRS)
MID = CS + CV
ACC1 = 4 * MID
EPS = 1e-5
FAR = 1.0e38

F32 = mybir.dt.float32
I32 = mybir.dt.int32
BF16 = mybir.dt.bfloat16
ALU = mybir.AluOpType
ACT = mybir.ActivationFunctionType
AX = mybir.AxisListType.X


def wait(engine, sem, value):
    if not isinstance(value, int) or value > 0:
        engine.wait_ge(sem, value)


class Count:

    def __init__(self, sem, round_, per):
        self.sem, self.base, self.n = sem, round_ * per, 0

    def up(self, instruction):
        instruction.then_inc(self.sem, 1)
        self.n += 1
        return self.base + self.n


def bc(ap, axis, size):
    shape = list(ap.shape)
    shape.insert(axis, size)
    return ap.unsqueeze(axis).broadcast_to(shape)


def row(ap):
    return ap.partition_broadcast(P)


def staircase_steps(units, blocks):
    steps = units + blocks - 1
    return -(-steps // RING) * RING


def constants(nc, ident, iota):
    with ExitStack() as ctx:
        made = ctx.enter_context(nc.semaphore("const_made"))
        iota_i = ctx.enter_context(nc.sbuf_tensor("iota_i", [P, P], I32))
        block = ctx.enter_context(nc.Block())

        @block.gpsimd
        def _(pool):
            nc.gpsimd.memset(ident[:], 0.0).then_inc(made, 1)
            nc.gpsimd.iota(iota_i[:], pattern=[[1, P]], base=0, channel_multiplier=0).then_inc(made, 1)
            pool.wait_ge(made, 2)
            nc.gpsimd.affine_select(out=ident[:], in_=ident[:], compare_op=ALU.not_equal, fill=1.0, base=0,
                                    pattern=[[-1, P]], channel_multiplier=1).then_inc(made, 1)
            nc.gpsimd.tensor_copy(iota[:], iota_i[:]).then_inc(made, 1)


def staircase(nc, name, first_dst, units, blocks, unit_row, slot_row, b128, keep):
    steps = staircase_steps(units, blocks)
    chunks = first_dst.shape[1]
    halves = [(c, min(steps, c + 512)) for c in range(0, steps, 512)]
    with ExitStack() as ctx:
        def sb(n, shape, dt=F32):
            return ctx.enter_context(nc.sbuf_tensor(f"{name}_{n}", shape, dt))

        first = sb("first", [P, chunks], I32)
        fb_i = sb("fb_i", [P, chunks], I32)
        fb = sb("fb", [P, chunks])
        idx_i = sb("idx_i", [P, chunks], I32)
        idx = sb("idx", [P, chunks])
        corner = sb("corner", [P, chunks])
        s_i = sb("s_i", [P, steps], I32)
        spare_i = sb("spare_i", [1, steps], I32)
        s_f = sb("s_f", [P, steps])
        spare = sb("spare", [1, steps])
        ones = sb("ones", [P, P])
        passed = sb("passed", [P, chunks, steps])
        u = sb("u", [P, steps])
        b = sb("b", [P, steps])
        slot = sb("slot", [1, steps])
        psum = [ctx.enter_context(nc.psum_tensor(f"{name}_ps{h}", [P, 512], F32)) for h in range(len(halves))]
        loaded = ctx.enter_context(nc.semaphore(f"{name}_loaded"))
        patterns = ctx.enter_context(nc.semaphore(f"{name}_patterns"))
        done = ctx.enter_context(nc.semaphore(f"{name}_dve"))
        summed = ctx.enter_context(nc.semaphore(f"{name}_summed"))
        block = ctx.enter_context(nc.Block())

        @block.sync
        def _(sp):
            sp.dma_start(first[:], first_dst).then_inc(loaded, 16)

        @block.gpsimd
        def _(pool):
            nc.gpsimd.iota(idx_i[:], pattern=[[P, chunks]], base=1, channel_multiplier=1).then_inc(patterns, 1)
            nc.gpsimd.iota(s_i[:], pattern=[[1, steps]], base=0, channel_multiplier=0).then_inc(patterns, 1)
            nc.gpsimd.iota(spare_i[:], pattern=[[0, steps // RING], [1, RING]], base=blocks + RING,
                           channel_multiplier=0).then_inc(patterns, 1)
            nc.gpsimd.memset(ones[:], 1.0).then_inc(patterns, 1)

        @block.tensor
        def _(pe):
            pe.wait_ge(patterns, 4)
            pe.wait_ge(done, 6 + chunks)
            for h, (lo, hi) in enumerate(halves):
                for c in range(chunks):
                    last = nc.tensor.matmul(psum[h][:, 0:hi - lo], ones[:], passed[:, c, lo:hi],
                                            start=c == 0, stop=c == chunks - 1)
            last.then_inc(summed, 1)

        @block.vector
        def _(dve):
            d = Count(done, 0, 0)
            dve.wait_ge(loaded, 16)
            dve.wait_ge(patterns, 4)
            d.up(nc.vector.tensor_scalar(fb_i[:], first[:], 7, None, ALU.arith_shift_right))
            d.up(nc.vector.tensor_copy(idx[:], idx_i[:]))
            d.up(nc.vector.tensor_copy(s_f[:], s_i[:]))
            d.up(nc.vector.tensor_copy(spare[:], spare_i[:]))
            dve.wait_ge(done, 1)
            d.up(nc.vector.tensor_copy(fb[:], fb_i[:]))
            dve.wait_ge(done, 5)
            dve.wait_ge(done, d.up(nc.vector.tensor_tensor(corner[:], fb[:], idx[:], ALU.add)))
            for c in range(chunks):
                d.up(nc.vector.tensor_scalar(passed[:, c, :], s_f[:], corner[:, c:c + 1], None, ALU.is_ge))
            dve.wait_ge(summed, 1)
            for h, (lo, hi) in enumerate(halves):
                d.up(nc.vector.tensor_copy(u[:, lo:hi], psum[h][:, 0:hi - lo]))
            dve.wait_ge(done, d.base + d.n)
            d.up(nc.vector.tensor_tensor(b[:], s_f[:], u[:], ALU.subtract))
            d.up(nc.vector.memset(keep[:, 0:1], 0.0))
            d.up(nc.vector.tensor_copy(unit_row[:], u[0:1, :]))
            k = d.up(nc.vector.tensor_tensor(keep[:, 1:steps], u[:, 1:steps], u[:, 0:steps - 1], ALU.subtract))
            dve.wait_ge(done, k)
            d.up(nc.vector.tensor_scalar(b128[:], b[:], float(P), None, ALU.mult))
            k = d.up(nc.vector.tensor_tensor(slot[:], spare[:], b[0:1, :], ALU.subtract))
            dve.wait_ge(done, k)
            k = d.up(nc.vector.tensor_tensor(slot[:, 0:steps - 1], slot[:, 0:steps - 1], keep[0:1, 1:steps],
                                             ALU.mult))
            k = d.up(nc.vector.memset(slot[:, steps - 1:steps], 0.0))
            dve.wait_ge(done, k)
            k = d.up(nc.vector.tensor_tensor(slot[:], slot[:], b[0:1, :], ALU.add))
            dve.wait_ge(done, k)
            k = d.up(nc.vector.tensor_copy(slot_row[:], slot[:]))
            dve.wait_ge(done, k)


def splits(nc, rbf_d, basis_d):
    bases = rbf_d.shape[0]
    lines = P // bases
    whole = rbf_d.rearrange("k (a n) -> (k a) n", a=lines)
    length = whole.shape[1]
    pieces = next(n for n in range(8, 65) if length % n == 0)
    size = length // pieces
    with ExitStack() as ctx:
        x, rest = (ctx.enter_context(nc.sbuf_tensor(f"b_{n}", [P, 2, size], F32)) for n in ("x", "rest"))
        part = ctx.enter_context(nc.sbuf_tensor("b_part", [P, 2, 3, size], BF16))
        loaded, stored = ([ctx.enter_context(nc.semaphore(f"b_{n}{i}")) for i in range(2)]
                          for n in ("loaded", "stored"))
        rounded = ctx.enter_context(nc.semaphore("b_rounded"))
        left = ctx.enter_context(nc.semaphore("b_left"))
        block = ctx.enter_context(nc.Block())
        columns = lambda ap, n: ap[:, n * size:(n + 1) * size]

        def store(sp, n):
            sp.wait_ge(rounded, 3 * (n + 1))
            for g, (k, _) in enumerate(PAIRS):
                rows = basis_d[g * bases:(g + 1) * bases, :].rearrange("k (a n) -> (k a) n", a=lines)
                sp.dma_start(columns(rows, n), part[:, n % 2, k, :]).then_inc(stored[n % 2], 16)

        @block.sync
        def _(sp):
            for n in range(pieces):
                if n >= 2:
                    sp.wait_ge(left, 2 * (n - 2) + 1)
                sp.dma_start(x[:, n % 2, :], columns(whole, n)).then_inc(loaded[n % 2], 16)
                if n >= 1:
                    store(sp, n - 1)
            store(sp, pieces - 1)
            for i in range(2):
                sp.wait_ge(stored[i], 16 * len(PAIRS) * ((pieces + 1 - i) // 2))

        @block.scalar
        def _(act):
            for n in range(pieces + 1):
                if n < pieces:
                    act.wait_ge(loaded[n % 2], 16 * (n // 2 + 1))
                    if n >= 2:
                        act.wait_ge(stored[n % 2], 16 * len(PAIRS) * (n // 2))
                if n >= 1:
                    for k in (1, 2):
                        act.wait_ge(left, 2 * (n - 1) + k)
                        nc.scalar.activation(part[:, (n - 1) % 2, k, :], rest[:, (n - 1) % 2, :],
                                             ACT.Copy).then_inc(rounded, 1)
                if n < pieces:
                    nc.scalar.activation(part[:, n % 2, 0, :], x[:, n % 2, :], ACT.Copy).then_inc(rounded, 1)

        @block.vector
        def _(dve):
            for n in range(pieces):
                at = n % 2
                for k in range(2):
                    dve.wait_ge(rounded, 3 * n + k + 1)
                    whole_part = x[:, at, :] if k == 0 else rest[:, at, :]
                    nc.vector.tensor_tensor(rest[:, at, :], whole_part, part[:, at, k, :],
                                            ALU.subtract).then_inc(left, 1)


def split_weight(nc, dve, whole, rest, parts, parted):
    take = lambda k, source: nc.vector.tensor_copy(parts[:, k, :], source).then_inc(parted, 1)
    leave = lambda k, source: nc.vector.tensor_tensor(rest, source, parts[:, k, :], ALU.subtract).then_inc(parted, 1)
    take(0, whole)
    dve.wait_ge(parted, 1)
    leave(0, whole)
    dve.wait_ge(parted, 2)
    take(1, rest)
    dve.wait_ge(parted, 3)
    leave(1, rest)
    dve.wait_ge(parted, 4)
    take(2, rest)


def stack_weight(engine, parts, stacked, sem):
    n = parts.shape[0]
    for g, (_, part) in enumerate(PAIRS):
        engine.dma_start(stacked[g * n:(g + 1) * n, :], parts[:, part, :]).then_inc(sem, 16)


def tables(nc, xn, table_src, table_dst, w, ident):
    blocks = xn.shape[0] // P
    chunks = blocks // CHUNK
    with ExitStack() as ctx:
        def sb(n, shape, dt=F32):
            return ctx.enter_context(nc.sbuf_tensor(f"t_{n}", shape, dt))

        def sem(n):
            return ctx.enter_context(nc.semaphore(f"t_{n}"))

        x = sb("x", [P, CHUNK, D])
        xc = sb("xc", [P, CHUNK, CS])
        sq = sb("sq", [P, CHUNK, D])
        xnorm = sb("xnorm", [P, CHUNK, D])
        stat = sb("stat", [P, 2 * CHUNK])
        mean = sb("mean", [P, CHUNK])
        root = sb("root", [P, 2 * CHUNK])
        rinv = sb("rinv", [P, 2 * CHUNK])
        gamma_s, beta_s, gamma_v = sb("gs", [P, CS]), sb("bs", [P, CS]), sb("gv", [P, CV])
        wa, wb = sb("wa", [P, 2 * D]), sb("wb", [CV, 2 * D])
        xt_a, xt_b = sb("xt_a", [P, 2, P]), sb("xt_b", [CV, 2, P])
        o = sb("o", [P, CHUNK, 2 * D])
        pt = [ctx.enter_context(nc.psum_tensor(f"t_pt{i}", [P, 512], F32)) for i in range(2)]
        po = [ctx.enter_context(nc.psum_tensor(f"t_po{i}", [P, 512], F32)) for i in range(2)]
        zeroed, weights, loaded, own, rooted = sem("zeroed"), sem("weights"), sem("loaded"), sem("dve"), sem("rooted")
        turned, copied, multiplied, stored = sem("turned"), sem("copied"), sem("multiplied"), sem("stored")
        rested = sem("rested")
        n_weights = 3 + 2 * 4
        NORMED, PER = 17, 17 + CHUNK
        SPREADS = 9
        xv = xn.rearrange("(c b p) f -> c p b f", b=CHUNK, p=P)
        sv = table_src.rearrange("(c b p) f -> c p b f", b=CHUNK, p=P)
        dv = table_dst.rearrange("(c b p) f -> c p b f", b=CHUNK, p=P)
        block = ctx.enter_context(nc.Block())

        @block.sync
        def _(sp):
            sp.dma_start(gamma_s[:], row(w["gamma_s"])).then_inc(weights, 16)
            sp.dma_start(beta_s[:], row(w["beta_s"])).then_inc(weights, 16)
            sp.dma_start(gamma_v[:], row(w["gamma_v"])).then_inc(weights, 16)
            sp.wait_ge(zeroed, 2)
            for side, (ws, wv) in enumerate((("Ws_src", "Wv_src"), ("Ws_dst", "Wv_dst"))):
                at = side * D
                sp.dma_start(wa[0:CS, at:at + CS], w[ws]).then_inc(weights, 16)
                for comp in range(3):
                    to = at + CS + comp * CV
                    into = wa[CS + comp * CV:CS + (comp + 1) * CV, to:to + CV] if comp < 2 else wb[:, to:to + CV]
                    sp.dma_start(into, w[wv]).then_inc(weights, 16)
            with sp.Fori(0, chunks) as c:
                sp.dma_start(x[:], xv[c]).then_inc(loaded, 16)
                sp.wait_ge(own, (c + 1) * PER)
                sp.dma_start(sv[c], o[:, :, 0:D]).then_inc(stored, 16)
                sp.dma_start(dv[c], o[:, :, D:2 * D]).then_inc(stored, 16)
                sp.wait_ge(stored, (c + 1) * 32)
                sp.sem_inc(rested, 1)

        @block.gpsimd
        def _(pool):
            nc.gpsimd.memset(wa[:], 0.0).then_inc(zeroed, 1)
            nc.gpsimd.memset(wb[:], 0.0).then_inc(zeroed, 1)

        @block.scalar
        def _(act):
            with act.Fori(0, chunks) as c:
                act.wait_ge(own, c * PER + SPREADS)
                nc.scalar.activation(root[:], stat[:], ACT.Sqrt).then_inc(rooted, 1)
                for b in range(CHUNK):
                    act.wait_ge(turned, c * CHUNK + (b + 1))
                    act.wait_ge(multiplied, c * CHUNK + (b + 1))
                    nc.scalar.activation(xt_a[:, b % 2, :], pt[b % 2][:, 0:P], ACT.Copy)
                    nc.scalar.activation(xt_b[:, b % 2, :], pt[b % 2][0:CV, P:2 * P], ACT.Copy).then_inc(copied, 1)

        @block.tensor
        def _(pe):
            pe.sem_inc(multiplied, 1)
            pe.wait_ge(weights, 16 * n_weights)
            with pe.Fori(0, chunks) as c:
                pe.wait_ge(own, c * PER + NORMED)
                for b in range(CHUNK + 1):
                    if b < CHUNK:
                        nc.tensor.transpose(pt[b % 2][:, 0:P], xnorm[:, b, 0:P], ident[:])
                        nc.tensor.transpose(pt[b % 2][0:CV, P:2 * P], xnorm[:, b, P:D], ident[:]).then_inc(turned, 1)
                    if b >= 1:
                        pe.wait_ge(copied, c * CHUNK + b)
                        if b >= 3:
                            pe.wait_ge(own, c * PER + NORMED + b - 2)
                        nc.tensor.matmul(po[(b - 1) % 2][:, 0:2 * D], xt_a[:, (b - 1) % 2, :], wa[:],
                                         start=True, stop=False)
                        nc.tensor.matmul(po[(b - 1) % 2][:, 0:2 * D], xt_b[:, (b - 1) % 2, :], wb[:],
                                         start=False, stop=True).then_inc(multiplied, 1)

        @block.vector
        def _(dve):
            dve.wait_ge(weights, 16 * n_weights)
            s, v = x[:, :, 0:CS], x[:, :, CS:D]
            with dve.Fori(0, chunks) as c:
                d = Count(own, c, PER)
                dve.wait_ge(loaded, (c + 1) * 16)
                k = d.up(nc.vector.tensor_reduce(mean[:], s, AX, ALU.add))
                d.up(nc.vector.tensor_tensor(sq[:, :, CS:D], v, v, ALU.mult))
                dve.wait_ge(own, k)
                k = d.up(nc.vector.tensor_scalar(mean[:], mean[:], 1.0 / CS, None, ALU.mult))
                dve.wait_ge(own, k)
                k = d.up(nc.vector.tensor_tensor(xc[:], s, bc(mean[:], 2, CS), ALU.subtract))
                dve.wait_ge(own, k)
                k = d.up(nc.vector.tensor_tensor(sq[:, :, 0:CS], xc[:], xc[:], ALU.mult))
                dve.wait_ge(own, k)
                k = d.up(nc.vector.tensor_reduce(stat[:, 0:CHUNK], sq[:, :, 0:CS], AX, ALU.add))
                dve.wait_ge(own, k)
                d.up(nc.vector.tensor_scalar(stat[:, 0:CHUNK], stat[:, 0:CHUNK], 1.0 / CS, EPS, ALU.mult, ALU.add))
                k = d.up(nc.vector.tensor_reduce(stat[:, CHUNK:], sq[:, :, CS:D], AX, ALU.add))
                dve.wait_ge(own, k)
                k = d.up(nc.vector.tensor_scalar(stat[:, CHUNK:], stat[:, CHUNK:], 1.0 / CV, EPS, ALU.mult, ALU.add))
                assert d.n == SPREADS
                dve.wait_ge(rooted, c + 1)
                k = d.up(nc.vector.reciprocal(rinv[:], root[:]))
                dve.wait_ge(own, k)
                d.up(nc.vector.tensor_tensor(xc[:], xc[:], bc(rinv[:, 0:CHUNK], 2, CS), ALU.mult))
                k = d.up(nc.vector.tensor_tensor(xnorm[:, :, CS:D], v, bc(rinv[:, CHUNK:], 2, 3 * CV), ALU.mult))
                dve.wait_ge(own, k)
                k = d.up(nc.vector.tensor_tensor(xc[:], xc[:], bc(gamma_s[:], 1, CHUNK), ALU.mult))
                for comp in range(3):
                    part = xnorm[:, :, CS + comp * CV:CS + (comp + 1) * CV]
                    d.up(nc.vector.tensor_tensor(part, part, bc(gamma_v[:], 1, CHUNK), ALU.mult))
                dve.wait_ge(own, k)
                d.up(nc.vector.tensor_tensor(xnorm[:, :, 0:CS], xc[:], bc(beta_s[:], 1, CHUNK), ALU.add))
                assert d.n == NORMED
                for b in range(CHUNK):
                    dve.wait_ge(multiplied, c * CHUNK + (b + 2))
                    d.up(nc.vector.tensor_copy(o[:, b, :], po[b % 2][:, 0:2 * D]))
                assert d.n == PER


def edges(nc, idx_d, y_d, rbf_d, table_src, table_dst, h_d, w, ident, logits):
    groups = idx_d.shape[0]
    T = TILES
    HD = HEADS * AS
    with ExitStack() as ctx:
        def sb(n, shape, dt=F32):
            return ctx.enter_context(nc.sbuf_tensor(f"e_{n}", shape, dt))

        def psum(n, size=512):
            return ctx.enter_context(nc.psum_tensor(f"e_{n}", [P, size], F32))

        def sem(n):
            return ctx.enter_context(nc.semaphore(f"e_{n}"))

        w_rbf, rest_rbf = sb("w_rbf", [16, WN]), sb("rest_rbf", [16, WN])
        parts_rbf, stack_rbf = sb("parts_rbf", [16, 3, WN], BF16), sb("stack_rbf", [BASIS, WN], BF16)
        w_first = sb("w_first", [MID, 2 * CS])
        w_val, w_hid = sb("w_val", [CS, MID]), sb("w_hid", [CS, MID])
        w_g = sb("w_g", [CS, CV])
        dot = sb("dot", [CS, HEADS])
        w_gate = sb("w_gate", [MID, CV + HEADS])
        w_v1 = sb("w_v1", [P, 2 * CV])
        w_v2 = sb("w_v2", [P, 2 * CV])
        w_h1 = sb("w_h1", [P, 2 * CV])
        w_h2 = sb("w_h2", [MID, CV + HD])
        w_hs = sb("w_hs", [P, HD + CV + HEADS])
        scale_1, scale_2 = sb("scale_1", [P, 1]), sb("scale_2", [MID, 1])
        scale_ss, scale_sv = sb("scale_ss", [P, 1]), sb("scale_sv", [P, 1])
        idx = sb("idx", [P, RING, 2 * T], I32)
        y = sb("y", [P, RING, T, 6])
        rbf = sb("rbf", [BASIS, RING, GROUP], BF16)
        g_src = sb("g_src", [P, RING, T, D])
        g_dst = sb("g_dst", [P, RING, T, D])
        msg = sb("msg", [P, 2, T, D])
        sy = sb("sy", [P, T, CS])
        vy = sb("vy", [P, T, 3, CV])
        dsum = sb("dsum", [P, T, CV])
        wy = sb("wy", [P, T, CV])
        c1 = sb("c1", [P, T, 3, CV])
        c2 = sb("c2", [P, T, 3, CV])
        cross = sb("cross", [P, T, 3, CV])
        m1s = sb("m1s", [P, T, MID])
        m1v = sb("m1v", [P, T, 2 * P])
        m1t = sb("m1t", [P, 3, GROUP])
        hidden = sb("hidden", [P, 2, GROUP])
        gate = sb("gate", [P, 2, T, CV])
        mixed_v = sb("mixed_v", [P, T, 3, CV])
        gv = sb("gv", [P, T, 3, CV])
        vy2 = sb("vy2", [P, T, 3, CV])
        dsum2 = sb("dsum2", [P, T, CV])
        d1 = sb("d1", [P, T, 3, CV])
        d2 = sb("d2", [P, T, 3, CV])
        m2 = sb("m2", [P, T, 6 * CV + CV])
        m2t = sb("m2t", [P, 2, GROUP])
        hy = sb("hy", [P, T, 3, CV])
        h = sb("h", [P, 2, T, HEADS, HW + 1])

        ps_w = psum("ps_w", 1024)
        radial_w = ps_w[:].rearrange("p (t k) -> p t k", k=256)
        ps_t = [psum(f"ps_t{i}") for i in range(2)]
        ps_v = psum("ps_v", 1024)
        mix_v = ps_v[:].rearrange("p (t k) -> p t k", k=256)
        LIN, VX = CV, CV + HEADS
        VS = VX + 3 * CV
        ps_h = psum("ps_h", 1024)
        mix_h = ps_h[:].rearrange("p (t k) -> p t k", k=256)
        HS = 3 * CV
        HA, HL = HS + HD, HS + HD + CV

        weights, zeroed, scaled, setup, ones_set = (sem("weights"), sem("zeroed"), sem("scaled"), sem("setup"),
                                                    sem("ones_set"))
        idx_in, y_in, rbf_in, gathered = ([sem(f"{n}{r}") for r in range(RING)]
                                          for n in ("idx_in", "y_in", "rbf_in", "gathered"))
        stored = [sem(f"stored{r}") for r in range(2)]
        parted, stacked = sem("parted"), sem("stacked")
        factored = sem("factored")
        issued = sem("issued")
        summed = sem("summed")
        radial = sem("radial")
        first = sem("first")
        second = sem("second")
        third = sem("third")
        turned = sem("turned")
        taken = sem("taken")
        mixed = sem("mixed")
        gated = sem("gated")
        valued = sem("valued")
        headed = sem("headed")
        kept = sem("kept")
        FIRST, SECOND, THIRD = 15, 13, 6
        DONE_S, VREAD = 8, 3

        def turn(u, second_tp, k):
            if second_tp:
                return u * 6 + ((5 if isinstance(u, int) and u == groups - 1 else 9) + k)
            return k + 1 if isinstance(u, int) and u == 0 else u * 6 + (k - 1)

        def rounds(engine, body):
            for r in range(RING):
                body(r, r, 0)
            last = groups // RING - 1
            if last > 1:
                with engine.Fori(1, last) as i:
                    for r in range(RING):
                        body(i * RING + r, r, i)
            for r in range(RING):
                body(last * RING + r, r, last)

        def present(u):
            return not isinstance(u, int) or 0 <= u < groups

        block_wise = (w_v1, w_v2, w_h1, w_h2, w_hs, dot)
        column = lambda v: v.rearrange("(p a) -> p a", a=1)
        alpha_dot = w["alpha_dot"].rearrange("a h k -> h k a")
        val, vlin = w["Wv_val"], w["Wv_vlin"]
        placements = [
            (w_rbf[:], w["W_rbf"]), (w_first[:, 0:CS], w["W_alpha"]), (w_first[:, CS:2 * CS], w["Ws_val"]),
            (w_g[:], w["Wg"]),
            (w_v1[0:CS, 0:CV], val[CS:P]), (w_v1[CS:P, CV:2 * CV], val[CS:P]),
            (w_v2[0:CS, 0:CV], val[CS:P]), (w_v2[CS:P, CV:2 * CV], val[0:CS]),
            (w_h1[0:CS, 0:CV], vlin[CS:P]), (w_h1[CS:P, CV:2 * CV], vlin[CS:P]),
            (w_h2[0:CS, 0:CV], vlin[CS:P]), (w_h2[CS:MID, CV:CV + HD], w["Ws_vlin"][CS:MID]),
            (w_hs[CS:P, 0:HD], w["Ws_vlin"][0:CS]), (w_hs[CS:P, HD:HD + CV], vlin[0:CS]),
            (scale_ss[CS:P], column(w["w2_ss"])), (scale_sv[CS:P], column(w["w2_sv"])),
            (scale_2[CS:MID], column(w["w2_vv0"])),
        ]
        for tile, at in ((scale_1, 0), (scale_1, CS), (scale_2, 0)):
            placements += [(tile[at:at + CV], column(w["w2_vs"])), (tile[at + CV:at + CS], column(w["w2_vv1"]))]
        for hd in range(HEADS):
            rows = slice(hd * AS, (hd + 1) * AS)
            placements += [(dot[rows, hd:hd + 1], alpha_dot[hd]),
                           (w_hs[rows, HD + CV + hd:HD + CV + hd + 1], alpha_dot[hd])]
        block = ctx.enter_context(nc.Block())

        @block.sync
        def _(sp):
            sp.wait_ge(zeroed, len(block_wise))
            for to, source in placements:
                sp.dma_start(to, source).then_inc(weights, 16)
            sp.wait_ge(parted, 5)
            stack_weight(sp, parts_rbf, stack_rbf, stacked)

            def load(u, r, i):
                at = u * GROUP if isinstance(u, int) else sp.snap(u * GROUP)
                wait(sp, gathered[r], i * 32 * T)
                sp.dma_start(idx[:, r, :], idx_d[u]).then_inc(idx_in[r], 16)
                wait(sp, radial, u - (RING - 1))
                sp.dma_start(rbf[:, r, :], rbf_d[:, bass.ds(at, GROUP)]).then_inc(rbf_in[r], 16)

            rounds(sp, load)

        @block.gpsimd
        def _(pool):
            for tile in block_wise:
                nc.gpsimd.memset(tile[:], 0.0).then_inc(zeroed, 1)
            nc.gpsimd.memset(h[:], 1.0).then_inc(ones_set, 1)

            def gather(u, r, i):
                pool.wait_ge(idx_in[r], (i + 1) * 16)
                wait(pool, summed, u - (RING - 1))
                pool.sem_inc(issued, 1)
                for side, (table, into) in enumerate(((table_src, g_src), (table_dst, g_dst))):
                    for t in range(T):
                        c = side * T + t
                        pool.indirect_dma_start(
                            out=into[:, r, t, :], out_offset=None, in_=table,
                            in_offset=bass.IndirectOffsetOnAxis(ap=idx[:, r, c:c + 1], axis=0),
                        ).then_inc(gathered[r], 16)

            def body(u, r, i):
                if present(u + 2):
                    gather(u + 2, (r + 2) % RING, i + (r + 2) // RING)
                pool.wait_ge(gathered[r], (i + 1) * 32 * T)
                wait(pool, first, (u - 1) * FIRST)
                nc.gpsimd.tensor_tensor(msg[:, r % 2], g_src[:, r], g_dst[:, r], ALU.add).then_inc(summed, 1)

            gather(0, 0, 0)
            gather(1, 1, 0)
            rounds(pool, body)

        @block.tensor
        def _(pe):
            pe.wait_ge(scaled, 1)
            nc.tensor.transpose(ps_t[0][0:CS, 0:MID], w_first[:, CS:2 * CS], ident[0:MID, 0:MID])
            nc.tensor.transpose(ps_t[0][0:CS, P:P + MID], w_first[:, 0:CS], ident[0:MID, 0:MID]).then_inc(setup, 1)
            pe.wait_ge(scaled, 2)
            nc.tensor.matmul(ps_t[1][0:MID, 0:CV], w_val[:], w_g[:], start=True, stop=True)
            nc.tensor.matmul(ps_t[1][0:MID, CV:CV + HEADS], w_hid[:], dot[:], start=True, stop=True).then_inc(setup, 1)
            pe.wait_ge(scaled, 3)
            pe.wait_ge(stacked, 16 * len(PAIRS))

            def radial_weights(u, r, i):
                pe.wait_ge(rbf_in[r], (i + 1) * 16)
                wait(pe, first, u * FIRST)
                for t in range(T):
                    last = nc.tensor.matmul(radial_w[:, t, 0:WN],
                                            rbf[:, r, t * P:(t + 1) * P], stack_rbf[:], start=True, stop=True)
                last.then_inc(radial, 1)

            def turn_block(place, bank, rows):
                wait(pe, taken, place - 2)
                for t in range(T):
                    channels = rows(t).shape[1]
                    last = nc.tensor.transpose(ps_t[bank][0:channels, t * P:(t + 1) * P], rows(t), ident[:])
                last.then_inc(turned, 1)

            def first_blocks(u):
                pe.wait_ge(first, u * FIRST + DONE_S)
                turn_block(turn(u, False, 0), 0, lambda t: m1s[:, t, :])
                pe.wait_ge(first, (u + 1) * FIRST)
                turn_block(turn(u, False, 1), 1, lambda t: m1v[:, t, 0:P])
                pe.wait_ge(taken, turn(u, False, 0))
                nc.tensor.matmul(ps_t[0][:], w_first[:], m1t[0:MID, 0, :], start=True, stop=True).then_inc(turned, 1)
                turn_block(turn(u, False, 3), 1, lambda t: m1v[:, t, P:2 * P])

            def mix(u):
                pe.wait_ge(taken, turn(u, False, 3))
                wait(pe, gated, u)
                if present(u - 1):
                    pe.wait_ge(second, (u - 1) * SECOND + VREAD)
                for t in range(T):
                    tile = slice(t * P, (t + 1) * P)
                    nc.tensor.matmul(mix_v[:, t, 0:VX], m1t[0:MID, 0, tile], w_gate[:], start=True, stop=True)
                    nc.tensor.matmul(mix_v[:, t, VX:VX + 2 * CV], m1t[:, 1, tile], w_v1[:], start=True, stop=True)
                    last = nc.tensor.matmul(mix_v[:, t, VX + 2 * CV:VX + 4 * CV], m1t[:, 2, tile], w_v2[:],
                                            start=True, stop=True)
                last.then_inc(mixed, 1)

            def second_blocks(v, slot):
                if not present(v):
                    return
                wait(pe, third, v * THIRD)
                for t in range(T):
                    last = nc.tensor.matmul(mix_h[:, t, HS:HL + HEADS], hidden[:, slot, t * P:(t + 1) * P], w_hs[:],
                                            start=True, stop=True)
                last.then_inc(headed, 1)
                pe.wait_ge(second, (v + 1) * SECOND)
                turn_block(turn(v, True, 0), 0, lambda t: m2[:, t, 0:P])
                turn_block(turn(v, True, 1), 1, lambda t: m2[:, t, P:P + MID])

            def values(v):
                if not present(v):
                    return
                pe.wait_ge(taken, turn(v, True, 1))
                pe.wait_ge(kept, v + 1)
                for t in range(T):
                    tile = slice(t * P, (t + 1) * P)
                    nc.tensor.matmul(mix_h[:, t, 0:2 * CV], m2t[:, 0, tile], w_h1[:], start=True, stop=True)
                    last = nc.tensor.matmul(mix_h[:, t, 2 * CV:HA], m2t[0:MID, 1, tile], w_h2[:],
                                            start=True, stop=True)
                last.then_inc(valued, 1)

            def body(u, r, i):
                first_blocks(u)
                if present(u + 1):
                    radial_weights(u + 1, (r + 1) % RING, i + (r + 1) // RING)
                second_blocks(u - 1, (r - 1) % 2)
                mix(u)
                values(u - 1)

            radial_weights(0, 0, 0)
            rounds(pe, body)
            second_blocks(groups - 1, (groups - 1) % 2)
            values(groups - 1)

        @block.scalar
        def _(act):
            act.wait_ge(ones_set, 1)

            def take(place, bank, into):
                act.wait_ge(turned, place)
                rows = into.shape[0]
                nc.scalar.activation(into, ps_t[bank][0:rows, :], ACT.Copy).then_inc(taken, 1)

            def body(u, r, i):
                slot = r % 2
                wait(act, mixed, u)
                take(turn(u, False, 0), 0, m1t[0:MID, 0, :])
                take(turn(u, False, 1), 1, m1t[:, 1, :])
                act.wait_ge(turned, turn(u, False, 2))
                wait(act, valued, u - 1)
                nc.scalar.activation(hidden[0:CS, slot, :], ps_t[0][0:CS, :], ACT.Relu, scale=0.8)
                nc.scalar.activation(hidden[CS:P, slot, :], ps_t[0][CS:P, :], ACT.Sigmoid).then_inc(taken, 1)
                take(turn(u, False, 3), 1, m1t[:, 2, :])
                store(u - 2, slot)
                if present(u + 2):
                    harmonics(u + 2, (r + 2) % RING)
                keep(u - 1, (r - 1) % RING, 1 - slot, i * 2 + (r - 1) // 2)
                act.wait_ge(mixed, u + 1)
                if present(u - 2):
                    act.wait_ge(second, (u - 1) * SECOND)
                nc.scalar.activation(gate[:, slot], mix_v[:, :, 0:CV], ACT.Sigmoid).then_inc(gated, 1)

            def harmonics(u, r):
                act.dma_start(y[:, r], y_d[u]).then_inc(y_in[r], 16)

            def keep(v, r, slot, n):
                if not present(v):
                    return
                act.wait_ge(headed, v + 1)
                wait(act, stored[slot], n * 16)
                for t in range(T):
                    last = nc.scalar.activation(h[:, slot, t, :, 0:AS],
                                                mix_h[:, t, HS:HA].rearrange("p (h k) -> p h k", k=AS),
                                                ACT.Copy, scale=y[:, r, t, 0:1])
                last.then_inc(kept, 1)
                take(turn(v, True, 0), 0, m2t[:, 0, :])
                take(turn(v, True, 1), 1, m2t[0:MID, 1, :])

            def store(v, slot):
                if not present(v):
                    return
                act.wait_ge(third, (v + 1) * THIRD)
                act.dma_start(h_d[v], h[:, slot].rearrange("p t h k -> p (t h k)")).then_inc(stored[slot], 16)

            harmonics(0, 0)
            harmonics(1, 1)
            rounds(act, body)
            store(groups - 2, groups % 2)
            keep(groups - 1, RING - 1, (groups - 1) % 2, (groups - 1) // 2)
            store(groups - 1, (groups - 1) % 2)
            for slot in range(2):
                act.wait_ge(stored[slot], 16 * (groups // 2))

        @block.vector
        def _(dve):
            dve.wait_ge(weights, 16 * len(placements))
            by = lambda tile, factor: nc.vector.tensor_scalar(tile, tile, factor, None, ALU.mult)
            r2, r3 = 1.0 / math.sqrt(2.0), 1.0 / math.sqrt(3.0)
            for tile, factor in (
                    (w_rbf[:, 2 * CS + CV:2 * CS + 2 * CV], r3), (w_rbf[:, 2 * CS + 2 * CV:WN], r2),
                    (scale_1[CV:CS], r2), (scale_1[MID:P], r2), (scale_2[CV:CS], r2), (scale_2[CS:MID], r3),
                    (w_hs[CS:P, 0:HD], scale_ss[CS:P, 0:1]), (w_hs[CS:P, HD:HD + CV], scale_sv[CS:P, 0:1])):
                by(tile, factor).then_inc(factored, 1)
            dve.wait_ge(factored, 8)
            split_weight(nc, dve, w_rbf[:], rest_rbf[:], parts_rbf, parted)
            by(w_h1[:], scale_1[:, 0:1])
            by(w_h2[:], scale_2[:, 0:1]).then_inc(scaled, 1)
            dve.wait_ge(setup, 1)
            nc.vector.tensor_copy(w_val[:], ps_t[0][0:CS, 0:MID])
            nc.vector.tensor_copy(w_hid[:], ps_t[0][0:CS, P:P + MID]).then_inc(scaled, 1)
            dve.wait_ge(setup, 2)
            nc.vector.tensor_copy(w_gate[:, 0:CV], ps_t[1][0:MID, 0:CV])
            nc.vector.tensor_scalar(w_gate[:, CV:CV + HEADS], ps_t[1][0:MID, CV:CV + HEADS], 0.2, None,
                                    ALU.mult).then_inc(scaled, 1)

            mult = lambda out, a, b: nc.vector.tensor_tensor(out, a, b, ALU.mult)
            add = lambda out, a, b: nc.vector.tensor_tensor(out, a, b, ALU.add)
            subtract = lambda out, a, b: nc.vector.tensor_tensor(out, a, b, ALU.subtract)

            def cross_parts(p1, p2, out, d, k):
                dve.wait_ge(d.sem, k)
                for x in range(3):
                    k = d.up(subtract(out(x), p1[:, :, (x + 1) % 3, :], p2[:, :, (x + 2) % 3, :]))
                return k

            def first_product(u, r, i):
                d = Count(first, u, FIRST)
                m = msg[:, r % 2]
                s, v = m[:, :, 0:CS], m[:, :, CS:D].rearrange("p t (x c) -> p t x c", x=3)
                y0, yx = y[:, r, :, 0], y[:, r, :, 1:4]
                w_ss, w_sv = radial_w[:, :, 0:CS], radial_w[:, :, CS:2 * CS]
                w_vs, w_vv0, w_vv1 = (radial_w[:, :, 2 * CS + n * CV:2 * CS + (n + 1) * CV] for n in range(3))
                pairs = m1v[:, :, 0:6 * CV].rearrange("p t (x k c) -> p t x k c", x=3, k=2)
                dve.wait_ge(summed, u + 1)
                dve.wait_ge(y_in[r], (i + 1) * 16)
                k_vy = d.up(mult(vy[:], v, bc(yx, 3, CV)))
                k_sy = d.up(mult(sy[:], s, bc(y0, 2, CS)))
                d.up(mult(c1[:], v, bc(y[:, r, :, 2:5], 3, CV)))
                dve.wait_ge(first, k_vy)
                k_dot = d.up(add(dsum[:], vy[:, :, 0, :], vy[:, :, 1, :]))
                k_c = d.up(mult(c2[:], v, bc(y[:, r, :, 3:6], 3, CV)))
                dve.wait_ge(first, k_dot)
                k_dot = d.up(add(dsum[:], dsum[:], vy[:, :, 2, :]))
                dve.wait_ge(radial, u + 1)
                if present(u - 1):
                    dve.wait_ge(turned, turn(u - 1, False, 3))
                dve.wait_ge(first, k_sy)
                d.up(mult(m1s[:, :, 0:CS], sy[:], w_ss))
                dve.wait_ge(first, k_dot)
                d.up(mult(m1s[:, :, CS:MID], dsum[:], w_vv0))
                assert d.n == DONE_S
                d.up(mult(m1v[:, :, 6 * CV:2 * P], s, w_sv))
                k_wy = d.up(mult(wy[:], w_vs, bc(y0, 2, CV)))
                k_cross = cross_parts(c1, c2, lambda x: cross[:, :, x, :], d, k_c)
                dve.wait_ge(first, k_wy)
                d.up(mult(pairs[:, :, :, 0, :], v, bc(wy[:], 2, 3)))
                dve.wait_ge(first, k_cross)
                d.up(mult(pairs[:, :, :, 1, :], cross[:], bc(w_vv1, 2, 3)))
                assert d.n == FIRST

            def second_product(v, r):
                if not present(v):
                    return
                d = Count(second, v, SECOND)
                y0, yx = y[:, r, :, 0], y[:, r, :, 1:4]
                vectors = mix_v[:, :, VX:VS].rearrange("p t (x c) -> p t x c", x=3)
                pairs = m2[:, :, 0:6 * CV].rearrange("p t (x k c) -> p t x k c", x=3, k=2)
                dve.wait_ge(gated, v + 1)
                if present(v - 1):
                    dve.wait_ge(turned, turn(v - 1, True, 1))
                k = d.up(mult(mixed_v[:], bc(mix_v[:, :, VS:VS + CV], 2, 3), bc(yx, 3, CV)))
                d.up(nc.vector.tensor_copy(logits[:, bass.ds(v * T, T), :], mix_v[:, :, LIN:LIN + HEADS]))
                dve.wait_ge(second, k)
                k = d.up(add(mixed_v[:], mixed_v[:], vectors))
                assert d.n == VREAD
                dve.wait_ge(second, k)
                k_gv = d.up(mult(gv[:], mixed_v[:], bc(gate[:, r % 2], 2, 3)))
                dve.wait_ge(second, k_gv)
                k_vy = d.up(mult(vy2[:], gv[:], bc(yx, 3, CV)))
                d.up(mult(d1[:], gv[:], bc(y[:, r, :, 2:5], 3, CV)))
                dve.wait_ge(second, k_vy)
                k_dot = d.up(add(dsum2[:], vy2[:, :, 0, :], vy2[:, :, 1, :]))
                k_c = d.up(mult(d2[:], gv[:], bc(y[:, r, :, 3:6], 3, CV)))
                dve.wait_ge(second, k_dot)
                d.up(add(m2[:, :, 6 * CV:7 * CV], dsum2[:], vy2[:, :, 2, :]))
                d.up(mult(pairs[:, :, :, 0, :], gv[:], bc(bc(y0, 2, 3), 3, CV)))
                cross_parts(d1, d2, lambda x: pairs[:, :, x, 1, :], d, k_c)
                assert d.n == SECOND

            def last_step(v, r):
                if not present(v):
                    return
                d = Count(third, v, THIRD)
                yx = y[:, r, :, 1:4]
                dve.wait_ge(valued, v + 1)
                k = d.up(mult(hy[:], bc(mix_h[:, :, HA:HL], 2, 3), bc(yx, 3, CV)))
                d.up(add(logits[:, bass.ds(v * T, T), :], logits[:, bass.ds(v * T, T), :],
                         mix_h[:, :, HL:HL + HEADS]))
                dve.wait_ge(third, k)
                for x in range(3):
                    by_head = h[:, r % 2, :, :, AS + x * AV:AS + (x + 1) * AV]
                    d.up(add(by_head, hy[:, :, x, :].rearrange("p t (h k) -> p t h k", k=AV),
                             mix_h[:, :, x * CV:(x + 1) * CV].rearrange("p t (h k) -> p t h k", k=AV)))
                scalars = h[:, r % 2, :, :, 0:AS]
                d.up(add(scalars, scalars, mix_h[:, :, HS:HA].rearrange("p t (h k) -> p t h k", k=AS)))
                assert d.n == THIRD

            def body(u, r, i):
                first_product(u, r, i)
                second_product(u - 1, (r - 1) % RING)
                last_step(u - 2, (r - 2) % RING)

            rounds(dve, body)
            second_product(groups - 1, RING - 1)
            last_step(groups - 2, RING - 2)
            last_step(groups - 1, RING - 1)
            dve.wait_ge(third, groups * THIRD)


def softmax(nc, dst_windows, logits, ident):
    tiles = logits.shape[1]
    parts = tiles // SEG_TILES
    edges_on = SEG_TILES * P
    with ExitStack() as ctx:
        def sb(n, shape, dt=F32):
            return ctx.enter_context(nc.sbuf_tensor(f"s_{n}", shape, dt))

        def sem(n):
            return ctx.enter_context(nc.semaphore(f"s_{n}"))

        dst_i = sb("dst_i", [parts, edges_on + 2], I32)
        dst = sb("dst", [parts, edges_on + 2])
        breaks = [sb(f"breaks{i}", [parts, edges_on]) for i in range(2)]
        broken = sb("broken", [parts, 2])
        rows = sb("rows", [parts, HEADS, edges_on])
        best = sb("best", [parts, HEADS, edges_on])
        ends = sb("ends", [parts, 2, HEADS])
        breaks4 = sb("breaks4", [parts, 2, HEADS])
        turned_ends = sb("turned_ends", [HEADS, 2, 2 * P])
        carried = sb("carried", [HEADS, 2, parts + 1])
        start = sb("start", [parts, 2, HEADS])
        ps_in = [ctx.enter_context(nc.psum_tensor(f"s_in{i}", [P, 512], F32)) for i in range(2)]
        ps_out = [ctx.enter_context(nc.psum_tensor(f"s_out{i}", [P, 512], F32)) for i in range(2)]
        ps_c = ctx.enter_context(nc.psum_tensor("s_c", [P, 512], F32))
        loaded, own, turned, taken, back, ended, expd = (sem("loaded"), sem("dve"), sem("turned"), sem("taken"),
                                                        sem("back"), sem("ended"), sem("exp"))
        by_tile = logits[:].rearrange("p (q c) h -> p c q h", c=SEG_TILES)
        block = ctx.enter_context(nc.Block())
        C4 = SEG_TILES // 4
        SETUP = 7
        PASS = 2 * HEADS + 6

        @block.sync
        def _(sp):
            sp.dma_start(dst_i[:], dst_windows).then_inc(loaded, 16)

        @block.tensor
        def _(pe):
            for n in range(HEADS * C4):
                hd, c4 = n // C4, n % C4
                if n >= 2:
                    pe.wait_ge(taken, n - 1)
                for j in range(4):
                    last = nc.tensor.transpose(ps_in[n % 2][0:parts, j * P:(j + 1) * P],
                                               by_tile[:, c4 * 4 + j, :, hd], ident[:])
                last.then_inc(turned, 1)
            for side in range(2):
                pe.wait_ge(own, SETUP + side * PASS + HEADS + 2)
                nc.tensor.transpose(ps_c[0:HEADS, 0:parts], ends[:, side, :], ident[0:parts, 0:parts])
                nc.tensor.transpose(ps_c[0:HEADS, P:P + parts], breaks4[:, side, :],
                                    ident[0:parts, 0:parts]).then_inc(ended, 1)
                pe.wait_ge(own, SETUP + side * PASS + HEADS + 5)
                before = carried[:, side, 0:parts] if side == 0 else carried[:, side, 1:parts + 1]
                nc.tensor.transpose(ps_c[0:parts, 256:256 + HEADS], before,
                                    ident[0:HEADS, 0:HEADS]).then_inc(ended, 1)
            pe.wait_ge(own, SETUP + 2 * PASS)
            for n in range(HEADS * C4):
                hd, c4 = n // C4, n % C4
                if n >= 2:
                    pe.wait_ge(own, SETUP + 2 * PASS + n - 1)
                for j in range(4):
                    at = (c4 * 4 + j) * P
                    last = nc.tensor.transpose(ps_out[n % 2][:, j * P:j * P + parts],
                                               rows[:, hd, at:at + P], ident[0:parts, 0:parts])
                last.then_inc(back, 1)

        @block.scalar
        def _(act):
            for n in range(HEADS * C4):
                hd, c4 = n // C4, n % C4
                act.wait_ge(turned, n + 1)
                nc.scalar.activation(rows[:, hd, c4 * 512:(c4 + 1) * 512], ps_in[n % 2][0:parts, :],
                                     ACT.Copy).then_inc(taken, 1)
            act.wait_ge(own, SETUP + 2 * PASS + HEADS * C4)
            nc.scalar.activation(logits[:], logits[:], ACT.Exp).then_inc(expd, 1)
            act.wait_ge(expd, 1)

        @block.vector
        def _(dve):
            d = Count(own, 0, 0)
            dve.wait_ge(loaded, 16)
            dve.wait_ge(own, d.up(nc.vector.tensor_copy(dst[:], dst_i[:])))
            for side in range(2):
                k = d.up(nc.vector.tensor_tensor(breaks[side][:], dst[:, 1:edges_on + 1],
                                                 dst[:, 2 * side:2 * side + edges_on], ALU.not_equal))
                dve.wait_ge(own, k)
                k = d.up(nc.vector.tensor_scalar(breaks[side][:], breaks[side][:], -FAR, None, ALU.mult))
                dve.wait_ge(own, k)
                d.up(nc.vector.tensor_reduce(broken[:, side:side + 1], breaks[side][:], AX, ALU.min))
            assert d.n == SETUP
            dve.wait_ge(taken, HEADS * C4)
            for side in range(2):
                def scans(initial):
                    for hd in range(HEADS):
                        first = -FAR if initial is None else initial[:, hd:hd + 1]
                        if side == 0:
                            out, step, fed = best[:, hd, :], breaks[0][:], rows[:, hd, :]
                        else:
                            out, step, fed = rows[:, hd, ::-1], breaks[1][:, ::-1], best[:, hd, ::-1]
                        d.up(nc.vector.tensor_tensor_scan(out=out, data0=step, data1=fed, initial=first,
                                                          op0=ALU.add, op1=ALU.max))
                    dve.wait_ge(own, d.n)

                scans(None)
                d.up(nc.vector.tensor_copy(ends[:, side, :],
                                           best[:, :, edges_on - 1] if side == 0 else rows[:, :, 0]))
                d.up(nc.vector.tensor_copy(breaks4[:, side, :],
                                           broken[:, side:side + 1].broadcast_to([parts, HEADS])))
                dve.wait_ge(ended, 2 * side + 1)
                d.up(nc.vector.tensor_copy(turned_ends[:, side, :].rearrange("h (k q) -> h k q", k=2)[:, :, 0:parts],
                                           ps_c[0:HEADS, 0:2 * P].rearrange("h (k q) -> h k q", k=2)[:, :, 0:parts]))
                outside = 0 if side == 0 else parts
                d.up(nc.vector.memset(carried[:, side, outside:outside + 1], -FAR))
                dve.wait_ge(own, d.n)
                last, broke = turned_ends[:, side, 0:parts], turned_ends[:, side, P:P + parts]
                if side == 0:
                    out = carried[:, side, 1:parts + 1]
                else:
                    out, last, broke = (a[:, ::-1] for a in (carried[:, side, 0:parts], last, broke))
                d.up(nc.vector.tensor_tensor_scan(out=out, data0=broke, data1=last, initial=-FAR,
                                                  op0=ALU.add, op1=ALU.max))
                dve.wait_ge(ended, 2 * side + 2)
                d.up(nc.vector.tensor_copy(start[:, side, :], ps_c[0:parts, 2 * P:2 * P + HEADS]))
                dve.wait_ge(own, d.n)
                scans(start[:, side, :])
            assert d.n == SETUP + 2 * PASS
            for n in range(HEADS * C4):
                hd, c4 = n // C4, n % C4
                dve.wait_ge(back, n + 1)
                part = by_tile[:, c4 * 4:c4 * 4 + 4, :, hd]
                d.up(nc.vector.tensor_tensor(
                    part, part, ps_out[n % 2][:].rearrange("p (c q) -> p c q", c=4)[:, :, 0:parts], ALU.subtract))


def reduce_values(nc, h_d, unit_row, slot_row, b128, keep, dst_tiles, weights_of_edges, sums_d, iota):
    steps = b128.shape[1]
    groups = h_d.shape[0]
    T = TILES
    with ExitStack() as ctx:
        def sb(n, shape, dt=F32):
            return ctx.enter_context(nc.sbuf_tensor(f"r_{n}", shape, dt))

        def sem(n):
            return ctx.enter_context(nc.semaphore(f"r_{n}"))

        h = sb("h", [P, RING, T, HROW + 1])
        headed = [h[:, r, :, 0:HROW].rearrange("p t (h k) -> p t h k", h=HEADS) for r in range(RING)]
        rel = sb("rel", [P, 2, T])
        dst_i = sb("dst_i", list(dst_tiles.shape), I32)
        dst = sb("dst", list(dst_tiles.shape))
        onehot = sb("onehot", [P, 2, T, P])
        acc = sb("acc", [P, RING, HROW + 1])
        ps = [ctx.enter_context(nc.psum_tensor(f"r_ps{i}", [P, 512], F32)) for i in range(2)]
        loaded, stored = ([sem(f"{n}{i}") for i in range(RING)] for n in ("loaded", "stored"))
        dst_in, dst_f, weighed, hot, added, multiplied = (sem("dst_in"), sem("dst_f"), sem("weighed"), sem("hot"),
                                                          sem("added"), sem("multiplied"))

        def rounds(engine, body):
            for r in range(RING):
                body(r, r, 0)
            last = steps // RING - 1
            with engine.Fori(1, last) as i:
                for r in range(RING):
                    body(i * RING + r, r, i)
            for r in range(RING):
                body(last * RING + r, r, last)

        def present(s):
            return not isinstance(s, int) or 0 <= s < steps

        block = ctx.enter_context(nc.Block())

        @block.sync
        def _(sp):
            sp.dma_start(dst_i[:], dst_tiles).then_inc(dst_in, 16)

            def load(s, r, i):
                if not present(s):
                    return
                unit = sp.value_load(unit_row[0:1, bass.ds(s, 1)], min_val=0, max_val=groups - 1)
                wait(sp, multiplied, s - (RING - 1))
                sp.dma_start(h[:, r, :, 0:HROW], h_d[unit].rearrange("p (t k) -> p t k", t=T)).then_inc(loaded[r], 16)

            rounds(sp, load)

        @block.scalar
        def _(act):
            def store(s, r, i):
                slot = act.value_load(slot_row[0:1, bass.ds(s, 1)], min_val=0, max_val=sums_d.shape[0] - 1)
                act.wait_ge(added, s + 1)
                act.dma_start(sums_d[slot], acc[:, r, :]).then_inc(stored[r], 16)

            rounds(act, store)
            for r in range(RING):
                act.wait_ge(stored[r], 16 * (steps // RING))

        @block.gpsimd
        def _(pool):
            pool.wait_ge(dst_in, 16)
            nc.gpsimd.tensor_copy(dst[:], dst_i[:]).then_inc(dst_f, 1)
            nc.gpsimd.memset(h[:, :, :, HROW:HROW + 1], 1.0).then_inc(dst_f, 1)
            pool.wait_ge(dst_f, 2)

            def body(s, r, i):
                unit = pool.value_load(unit_row[0:1, bass.ds(s, 1)], min_val=0, max_val=groups - 1)
                wait(pool, hot, s - 1)
                nc.gpsimd.tensor_tensor(rel[:, r % 2, :], dst[:, bass.ds(unit * T, T)],
                                        b128[:, bass.ds(s, 1)].broadcast_to([P, T]), ALU.subtract).then_inc(weighed, 1)
                pool.wait_ge(loaded[r], (i + 1) * 16)
                nc.gpsimd.tensor_tensor(
                    headed[r], headed[r], bc(weights_of_edges[:, bass.ds(unit * T, T), :], 3, HW + 1),
                    ALU.mult).then_inc(weighed, 1)

            rounds(pool, body)

        @block.vector
        def _(dve):
            def hots(s, r, i):
                if not present(s):
                    return
                dve.wait_ge(weighed, s * 2 + 1)
                wait(dve, multiplied, s - 1)
                nc.vector.tensor_tensor(onehot[:, r % 2], bc(iota[:], 1, T), bc(rel[:, r % 2, :], 2, P),
                                        ALU.is_equal).then_inc(hot, 1)

            def add(s, r, i):
                dve.wait_ge(multiplied, s + 1)
                wait(dve, stored[r], i * 16)
                wait(dve, added, s)
                if isinstance(s, int) and s == 0:
                    nc.vector.tensor_copy(acc[:, 0, :], ps[0][:, 0:HROW + 1]).then_inc(added, 1)
                else:
                    nc.vector.scalar_tensor_tensor(acc[:, r, :], acc[:, (r - 1) % RING, :], keep[:, bass.ds(s, 1)],
                                                   ps[r % 2][:, 0:HROW + 1], ALU.mult, ALU.add).then_inc(added, 1)

            def body(s, r, i):
                hots(s + 1, (r + 1) % RING, i + (r + 1) // RING)
                add(s, r, i)

            hots(0, 0, 0)
            rounds(dve, body)
            dve.wait_ge(added, steps)

        @block.tensor
        def _(pe):
            def body(s, r, i):
                pe.wait_ge(hot, s + 1)
                pe.wait_ge(weighed, s * 2 + 2)
                wait(pe, added, s - 1)
                for t in range(T):
                    last = nc.tensor.matmul(ps[r % 2][:, 0:HROW + 1], onehot[:, r % 2, t, :],
                                            h[:, r, t, :], start=t == 0, stop=t == T - 1)
                last.then_inc(multiplied, 1)

            rounds(pe, body)


def norm_steps(nc, dve, d, z, centred, squares, stat, root, rinv, rooted, round_, out):
    mean = stat[:, CHUNK:2 * CHUNK]
    spread = stat[:, 0:CHUNK]

    def then(instruction):
        dve.wait_ge(d.sem, d.up(instruction))

    then(nc.vector.tensor_reduce(mean, z, AX, ALU.add))
    then(nc.vector.tensor_scalar(mean, mean, 1.0 / D, None, ALU.mult))
    then(nc.vector.tensor_tensor(centred, z, bc(mean, 2, D), ALU.subtract))
    then(nc.vector.tensor_tensor(squares, centred, centred, ALU.mult))
    then(nc.vector.tensor_reduce(spread, squares, AX, ALU.add))
    d.up(nc.vector.tensor_scalar(spread, spread, 1.0 / D, EPS, ALU.mult, ALU.add))
    dve.wait_ge(rooted, round_ + 1)
    then(nc.vector.reciprocal(rinv, root))
    then(nc.vector.tensor_tensor(out, centred, bc(rinv, 2, D), ALU.mult))


def middle(nc, xn, sums_d, factor_d, table, resid_d, w, w1, ident):
    chunks = xn.shape[0] // P // CHUNK
    with ExitStack() as ctx:
        def sb(n, shape, dt=F32):
            return ctx.enter_context(nc.sbuf_tensor(f"m_{n}", shape, dt))

        def sem(n):
            return ctx.enter_context(nc.semaphore(f"m_{n}"))

        x, z, zc, zq, x1 = (sb(n, [P, CHUNK, D]) for n in ("x", "z", "zc", "zq", "x1"))
        rest = sb("rest", [P, CHUNK, D + 1])
        sums = sb("sums", [P, CHUNK, HROW + 1])
        by_head = sums[:, :, 0:HROW].rearrange("p b (h k) -> p b h k", h=HEADS)
        factor = sb("factor", [P, CHUNK])
        den = sb("den", [P, CHUNK, HEADS])
        agg = sb("agg", [P, CHUNK, HEADS, HW])
        stat, root, rinv = sb("stat", [P, 2 * CHUNK]), sb("root", [P, CHUNK]), sb("rinv", [P, CHUNK])
        wp_a, wp_b = sb("wp_a", [P, D]), sb("wp_b", [D - P, D])
        wl_a, wl_b = sb("wl_a", [P, 2 * D]), sb("wl_b", [CV, 2 * D])
        t_a, t_b = sb("t_a", [P, 2, P]), sb("t_b", [CV, 2, P])
        o = sb("o", [P, CHUNK, 2 * D])
        pt = [ctx.enter_context(nc.psum_tensor(f"m_pt{i}", [P, 512], F32)) for i in range(2)]
        po = [ctx.enter_context(nc.psum_tensor(f"m_po{i}", [P, 512], F32)) for i in range(2)]
        zeroed, weights, loaded, own, rooted = sem("zeroed"), sem("weights"), sem("loaded"), sem("dve"), sem("rooted")
        turned, copied, multiplied, moved, stored = (sem("turned"), sem("copied"), sem("multiplied"), sem("moved"),
                                                     sem("stored"))
        rested = sem("rested")
        AGG, OUT0 = 4, 4 + CHUNK
        SPREAD, NORMED = OUT0 + 6, OUT0 + 8
        PER = NORMED + 1
        SCALES = 3
        xv = xn.rearrange("(c b p) f -> c p b f", b=CHUNK, p=P)
        tv = table.rearrange("(c b p) f -> c p b f", b=CHUNK, p=P)
        rv = resid_d.rearrange("(c b p) f -> c p b f", b=CHUNK, p=P)
        sums_v = sums_d[0:chunks * CHUNK].rearrange("(c b) p f -> c p b f", b=CHUNK)
        placements = []

        def place(lo, hi, row0, col0, source):
            n, m = source.shape
            cut = max(0, min(n, P - row0))
            if cut:
                placements.append((lo[row0:row0 + cut, col0:col0 + m], source[0:cut, :]))
            if cut < n:
                at = row0 + cut - P
                placements.append((hi[at:at + n - cut, col0:col0 + m], source[cut:n, :]))

        for hd in range(HEADS):
            place(wp_a, wp_b, hd * HW, 0, w["Wps"][hd * AS:(hd + 1) * AS, :])
            for comp in range(3):
                place(wp_a, wp_b, hd * HW + AS + comp * AV, CS + comp * CV, w["Wpv"][hd * AV:(hd + 1) * AV, :])
        for side, (ws, wv) in enumerate((("Wl1_0", "Wl1_1"), ("Wsc0", "Wsc1"))):
            place(wl_a, wl_b, 0, side * D, w1[ws])
            for comp in range(3):
                place(wl_a, wl_b, CS + comp * CV, side * D + CS + comp * CV, w1[wv])
        block = ctx.enter_context(nc.Block())

        @block.sync
        def _(sp):
            sp.wait_ge(zeroed, 4)
            for into, source in placements:
                sp.dma_start(into, source).then_inc(weights, 16)
            with sp.Fori(0, chunks) as c:
                sp.dma_start(x[:], xv[c]).then_inc(loaded, 16)
                sp.dma_start(sums[:], sums_v[c]).then_inc(loaded, 16)
                sp.dma_start(factor[:], factor_d[c]).then_inc(loaded, 16)
                sp.wait_ge(own, (c + 1) * PER + SCALES)
                sp.dma_start(tv[c], o[:, :, 0:D]).then_inc(stored, 16)
                sp.dma_start(rv[c], rest[:]).then_inc(stored, 16)
                sp.wait_ge(stored, (c + 1) * 32)
                sp.sem_inc(rested, 1)

        @block.gpsimd
        def _(pool):
            for tile in (wp_a, wp_b, wl_a, wl_b):
                nc.gpsimd.memset(tile[:], 0.0).then_inc(zeroed, 1)

        def project(act, c, b):
            act.wait_ge(multiplied, c * 2 * CHUNK + (CHUNK + b + 2))
            nc.scalar.activation(o[:, b, :], po[b % 2][:, 0:2 * D], ACT.Copy,
                                 scale=factor[:, b:b + 1]).then_inc(moved, 1)

        @block.scalar
        def _(act):
            act.wait_ge(weights, 16 * len(placements))
            with act.Fori(0, chunks) as c:
                for n in range(2 * CHUNK):
                    b = n % CHUNK
                    if n == CHUNK:
                        act.wait_ge(own, c * PER + (SCALES + SPREAD))
                        nc.scalar.activation(root[:], stat[:, 0:CHUNK], ACT.Sqrt).then_inc(rooted, 1)
                    act.wait_ge(turned, c * 2 * CHUNK + (n + 1))
                    act.wait_ge(multiplied, c * 2 * CHUNK + (n + 1))
                    nc.scalar.activation(t_a[:, b % 2, :], pt[b % 2][:, 0:P], ACT.Copy)
                    nc.scalar.activation(t_b[:, b % 2, :], pt[b % 2][0:CV, P:2 * P], ACT.Copy).then_inc(copied, 1)
                    if n > CHUNK:
                        project(act, c, b - 1)
                project(act, c, CHUNK - 1)

        @block.tensor
        def _(pe):
            pe.sem_inc(multiplied, 1)
            pe.wait_ge(weights, 16 * len(placements))
            pe.wait_ge(own, SCALES)
            with pe.Fori(0, chunks) as c:
                for half in range(2):
                    pe.wait_ge(own, c * PER + (SCALES + (AGG if half == 0 else NORMED)))
                    for b in range(CHUNK + 1):
                        if b < CHUNK:
                            rows = (agg[:, b].rearrange("p h k -> p (h k)") if half == 0 else x1[:, b, :])
                            nc.tensor.transpose(pt[b % 2][:, 0:P], rows[:, 0:P], ident[:])
                            nc.tensor.transpose(pt[b % 2][0:CV, P:2 * P], rows[:, P:D], ident[:]).then_inc(turned, 1)
                        if b >= 1:
                            pe.wait_ge(copied, c * 2 * CHUNK + (half * CHUNK + b))
                            if half == 0:
                                if b >= 3:
                                    pe.wait_ge(own, c * PER + (SCALES + AGG + b - 2))
                                else:
                                    pe.wait_ge(moved, c * CHUNK)
                            elif b >= 3:
                                pe.wait_ge(moved, c * CHUNK + (b - 2))
                            width = D if half == 0 else 2 * D
                            wa, wb = (wp_a, wp_b) if half == 0 else (wl_a, wl_b)
                            nc.tensor.matmul(po[(b - 1) % 2][:, 0:width], t_a[:, (b - 1) % 2, :], wa[:],
                                             start=True, stop=False)
                            nc.tensor.matmul(po[(b - 1) % 2][:, 0:width], t_b[:, (b - 1) % 2, :], wb[:],
                                             start=False, stop=True).then_inc(multiplied, 1)

        @block.vector
        def _(dve):
            dve.wait_ge(weights, 16 * len(placements))
            inv8, inv32 = 1.0 / math.sqrt(CS), 1.0 / math.sqrt(CV)
            for tile, by in ((wl_a[0:CS], inv8), (wl_a[CS:P], inv32), (wl_b[:], inv32)):
                nc.vector.tensor_scalar(tile, tile, by, None, ALU.mult).then_inc(own, 1)
            with dve.Fori(0, chunks) as c:
                d = Count(own, c, PER)
                d.base = d.base + SCALES
                dve.wait_ge(loaded, (c + 1) * 48)
                dve.wait_ge(own, d.up(nc.vector.tensor_scalar(den[:], by_head[:, :, :, HW], 1e-16, None, ALU.add)))
                dve.wait_ge(own, d.up(nc.vector.reciprocal(den[:], den[:])))
                d.up(nc.vector.tensor_scalar(rest[:, :, D], sums[:, :, HROW], 1.0, None, ALU.max))
                d.up(nc.vector.tensor_tensor(agg[:], by_head[:, :, :, 0:HW], bc(den[:], 3, HW), ALU.mult))
                for b in range(CHUNK):
                    dve.wait_ge(multiplied, c * 2 * CHUNK + (b + 2))
                    k = d.up(nc.vector.scalar_tensor_tensor(z[:, b, :], x[:, b, :], 2.0, po[b % 2][:, 0:D],
                                                            ALU.mult, ALU.add))
                dve.wait_ge(own, k)
                norm_steps(nc, dve, d, z[:], zc[:], zq[:], stat, root[:], rinv[:], rooted, c, x1[:])
                assert d.n == NORMED
                dve.wait_ge(moved, (c + 1) * CHUNK)
                d.up(nc.vector.tensor_tensor(rest[:, :, 0:D], x1[:], o[:, :, D:2 * D], ALU.add))
                assert d.n == PER


def edges1(nc, idx_d, y_d, rbf_d, table, unit_row, slot_row, b128, keep, w1, iota, sums_d):
    steps = b128.shape[1]
    groups = idx_d.shape[0]
    T = TILES
    with ExitStack() as ctx:
        def sb(n, shape, dt=F32):
            return ctx.enter_context(nc.sbuf_tensor(f"f_{n}", shape, dt))

        def sem(n):
            return ctx.enter_context(nc.semaphore(f"f_{n}"))

        def ring_sem(n, size):
            return [sem(f"{n}{r}") for r in range(size)]

        W0, W2, W1, W3 = 0, CS, CS + CV, 2 * CS + CV
        w_1, rest_1, w_2 = sb("w_1", [16, CS]), sb("rest_1", [16, CS]), sb("w_2", [CS, WE])
        parts_1, stack_1 = sb("parts_1", [16, 3, CS], BF16), sb("stack_1", [BASIS, CS], BF16)
        idx = sb("idx", [P, RING, 2 * T], I32)
        y, rbf = sb("y", [P, RING, T, 6]), sb("rbf", [BASIS, RING, GROUP], BF16)
        e = sb("e", [P, RING, T, D])
        hidden = sb("hidden", [CS, 2, GROUP])
        wy = sb("wy", [P, 2, T, MID])
        ey = sb("ey", [P, T, 3, CV])
        dot = sb("dot", [P, T, CV])
        we = sb("we", [P, T, CS])
        q = sb("q", [P, 2, T, ACC1])
        rel = sb("rel", [P, RING, T])
        onehot = sb("onehot", [P, RING, T, P])
        acc = sb("acc", [P, RING, ACC1])
        ps_h = [ctx.enter_context(nc.psum_tensor(f"f_ps_h{i}", [P, 512], F32)) for i in range(2)]
        ps_w = [ctx.enter_context(nc.psum_tensor(f"f_ps_w{i}", [P, 1024], F32)) for i in range(2)]
        ps_a = [ctx.enter_context(nc.psum_tensor(f"f_ps_a{i}", [P, 512], F32)) for i in range(2)]
        weights, scaled, parted, stacked = sem("weights"), sem("scaled"), sem("parted"), sem("stacked")
        idx_in, y_in, rbf_in, gathered, stored = (
            ring_sem(n, RING) for n in ("idx_in", "y_in", "rbf_in", "gathered", "stored"))
        hid, silu, radial, scalar_w, product, hot, multiplied, added, issued = (
            sem(n) for n in ("hid", "silu", "radial", "scalar_w", "product", "hot", "multiplied", "added", "issued"))
        HOT, PRODUCT = 2, 8

        def rounds(engine, body):
            for r in range(RING):
                body(r, r, 0)
            last = steps // RING - 1
            with engine.Fori(1, last) as i:
                for r in range(RING):
                    body(i * RING + r, r, i)
            for r in range(RING):
                body(last * RING + r, r, last)

        def present(s):
            return not isinstance(s, int) or 0 <= s < steps

        block = ctx.enter_context(nc.Block())

        @block.sync
        def _(sp):
            sp.dma_start(w_1[:], w1["Wfc1"]).then_inc(weights, 16)
            for at, source, n in ((W0, 0, CS), (W2, 2 * CS, CV), (W1, CS, CS), (W3, 2 * CS + CV, CV)):
                sp.dma_start(w_2[:, at:at + n], w1["Wfc2"][:, source:source + n]).then_inc(weights, 16)
            sp.wait_ge(parted, 5)
            stack_weight(sp, parts_1, stack_1, stacked)

            def body(s, r, i):
                unit = sp.value_load(unit_row[0:1, bass.ds(s, 1)], min_val=0, max_val=groups - 1)
                at = sp.snap(unit * GROUP)
                wait(sp, product, (s - (RING - 1)) * PRODUCT)
                sp.dma_start(idx[:, r, :], idx_d[unit]).then_inc(idx_in[r], 16)
                sp.dma_start(y[:, r], y_d[unit]).then_inc(y_in[r], 16)
                wait(sp, hid, s - (RING - 1))
                sp.dma_start(rbf[:, r, :], rbf_d[:, bass.ds(at, GROUP)]).then_inc(rbf_in[r], 16)

            rounds(sp, body)

        @block.gpsimd
        def _(pool):
            def gather(s, r, i):
                if not present(s):
                    return
                pool.wait_ge(idx_in[r], (i + 1) * 16)
                wait(pool, product, (s - (RING - 1)) * PRODUCT)
                pool.sem_inc(issued, 1)
                for t in range(T):
                    pool.indirect_dma_start(
                        out=e[:, r, t, :], out_offset=None, in_=table,
                        in_offset=bass.IndirectOffsetOnAxis(ap=idx[:, r, t:t + 1], axis=0),
                    ).then_inc(gathered[r], 16)

            rounds(pool, gather)

        @block.tensor
        def _(pe):
            pe.wait_ge(scaled, 1)
            pe.wait_ge(stacked, 16 * len(PAIRS))

            def hidden_layer(s, r, i):
                if not present(s):
                    return
                pe.wait_ge(rbf_in[r], (i + 1) * 16)
                wait(pe, silu, s - 1)
                nc.tensor.matmul(ps_h[r % 2][0:CS, :], stack_1[:], rbf[:, r, :],
                                 start=True, stop=True).then_inc(hid, 1)

            def radial_weights(s, r, i):
                if not present(s):
                    return
                pe.wait_ge(silu, s + 1)
                wait(pe, product, (s - 1) * PRODUCT)
                for t in range(T):
                    last = nc.tensor.matmul(ps_w[r % 2][:, t * 256:t * 256 + WE], hidden[:, r % 2, t * P:(t + 1) * P],
                                            w_2[:], start=True, stop=True)
                last.then_inc(radial, 1)

            def sums(s, r, i):
                slot = r % 2
                pe.wait_ge(hot, (s + 1) * HOT)
                pe.wait_ge(product, (s + 1) * PRODUCT)
                wait(pe, added, s - 1)
                for t in range(T):
                    last = nc.tensor.matmul(ps_a[slot][:, 0:ACC1], onehot[:, r, t, :], q[:, slot, t, :],
                                            start=t == 0, stop=t == T - 1)
                last.then_inc(multiplied, 1)

            def body(s, r, i):
                hidden_layer(s + 2, (r + 2) % RING, i + (r + 2) // RING)
                radial_weights(s + 1, (r + 1) % RING, i + (r + 1) // RING)
                sums(s, r, i)

            hidden_layer(0, 0, 0)
            hidden_layer(1, 1, 0)
            radial_weights(0, 0, 0)
            rounds(pe, body)

        @block.scalar
        def _(act):
            def activate(s, r, i):
                if not present(s):
                    return
                act.wait_ge(hid, s + 1)
                wait(act, radial, s - 1)
                nc.scalar.activation(hidden[:, r % 2, :], ps_h[r % 2][0:CS, :], ACT.Silu,
                                     scale=1.0 / math.sqrt(16.0)).then_inc(silu, 1)

            def with_scalar(s, r, i):
                if not present(s):
                    return
                act.wait_ge(radial, s + 1)
                act.wait_ge(y_in[r], (i + 1) * 16)
                wait(act, product, (s - 1) * PRODUCT)
                for t in range(T):
                    last = nc.scalar.activation(wy[:, r % 2, t, :], ps_w[r % 2][:, t * 256:t * 256 + MID], ACT.Copy,
                                                scale=y[:, r, t, 0:1])
                last.then_inc(scalar_w, 1)

            def store(s, r, i):
                if not present(s):
                    return
                slot = act.value_load(slot_row[0:1, bass.ds(s, 1)], min_val=0, max_val=sums_d.shape[0] - 1)
                act.wait_ge(added, s + 1)
                act.dma_start(sums_d[slot], acc[:, r, :]).then_inc(stored[r], 16)

            def body(s, r, i):
                activate(s + 2, (r + 2) % RING, i + (r + 2) // RING)
                with_scalar(s + 1, (r + 1) % RING, i + (r + 1) // RING)
                store(s - 2, (r - 2) % RING, None)

            activate(0, 0, 0)
            activate(1, 1, 0)
            with_scalar(0, 0, 0)
            rounds(act, body)
            store(steps - 2, RING - 2, None)
            store(steps - 1, RING - 1, None)
            for r in range(RING):
                act.wait_ge(stored[r], 16 * (steps // RING))

        @block.vector
        def _(dve):
            dve.wait_ge(weights, 16 * 5)
            nc.vector.tensor_scalar(w_2[:, 0:W3], w_2[:, 0:W3], 1.0 / math.sqrt(CS), None, ALU.mult)
            nc.vector.tensor_scalar(w_2[:, W3:WE], w_2[:, W3:WE], 1.0 / math.sqrt(3.0 * CS), None,
                                    ALU.mult).then_inc(scaled, 1)
            split_weight(nc, dve, w_1[:], rest_1[:], parts_1, parted)
            mult = lambda out, a, b: nc.vector.tensor_tensor(out, a, b, ALU.mult)
            plus = lambda out, a, b: nc.vector.tensor_tensor(out, a, b, ALU.add)

            def hots(s, r, i):
                if not present(s):
                    return
                d = Count(hot, s, HOT)
                dve.wait_ge(idx_in[r], (i + 1) * 16)
                k = d.up(nc.vector.tensor_tensor(rel[:, r, :], idx[:, r, T:2 * T],
                                                 b128[:, bass.ds(s, 1)].broadcast_to([P, T]), ALU.subtract))
                wait(dve, multiplied, s - (RING - 1))
                dve.wait_ge(hot, k)
                d.up(nc.vector.tensor_tensor(onehot[:, r], bc(iota[:], 1, T), bc(rel[:, r, :], 2, P),
                                             ALU.is_equal))
                assert d.n == HOT

            def products(s, r, i):
                d = Count(product, s, PRODUCT)
                slot = r % 2
                w = ps_w[slot][:].rearrange("p (t k) -> p t k", t=T)
                e0 = e[:, r, :, 0:CS]
                e1 = e[:, r, :, CS:D].rearrange("p t (x c) -> p t x c", x=3)
                yx = y[:, r, :, 1:4]
                vectors = q[:, slot, :, MID:ACC1].rearrange("p t (x c) -> p t x c", x=3)
                dve.wait_ge(gathered[r], (i + 1) * 16 * T)
                dve.wait_ge(y_in[r], (i + 1) * 16)
                k_ey = d.up(mult(ey[:], e1, bc(yx, 3, CV)))
                dve.wait_ge(scalar_w, s + 1)
                wait(dve, product, s * PRODUCT)
                k_we = d.up(mult(we[:], w[:, :, W1:W1 + CS], e0))
                dve.wait_ge(product, k_ey)
                k_dot = d.up(plus(dot[:], ey[:, :, 0, :], ey[:, :, 1, :]))
                wait(dve, multiplied, s - 1)
                d.up(mult(q[:, slot, :, 0:CS], wy[:, slot, :, 0:CS], e0))
                dve.wait_ge(product, k_dot)
                k_dot = d.up(plus(dot[:], dot[:], ey[:, :, 2, :]))
                d.up(mult(vectors[:, :, :, CS:MID], bc(wy[:, slot, :, CS:MID], 2, 3), e1))
                dve.wait_ge(product, k_dot)
                d.up(mult(q[:, slot, :, CS:MID], w[:, :, W3:W3 + CV], dot[:]))
                dve.wait_ge(product, k_we)
                d.up(mult(vectors[:, :, :, 0:CS], bc(we[:], 2, 3), bc(yx, 3, CS)))
                assert d.n == PRODUCT

            def add(s, r, i):
                if not present(s):
                    return
                slot = r % 2
                dve.wait_ge(multiplied, s + 1)
                wait(dve, stored[r], 16 * i)
                wait(dve, added, s)
                if isinstance(s, int) and s == 0:
                    nc.vector.tensor_copy(acc[:, 0, :], ps_a[0][:, 0:ACC1]).then_inc(added, 1)
                else:
                    nc.vector.scalar_tensor_tensor(acc[:, r, :], acc[:, (r - 1) % RING, :], keep[:, bass.ds(s, 1)],
                                                   ps_a[slot][:, 0:ACC1], ALU.mult, ALU.add).then_inc(added, 1)

            def body(s, r, i):
                hots(s + 1, (r + 1) % RING, i + (r + 1) // RING)
                products(s, r, i)
                add(s - 1, (r - 1) % RING, i + (r - 1) // RING)

            hots(0, 0, 0)
            rounds(dve, body)
            add(steps - 1, RING - 1, steps // RING - 1)
            dve.wait_ge(added, steps)


def final(nc, sums_d, factor_d, resid_d, out, w1, ident):
    blocks = resid_d.shape[0] // P
    chunks = blocks // CHUNK
    with ExitStack() as ctx:
        def sb(n, shape, dt=F32):
            return ctx.enter_context(nc.sbuf_tensor(f"l_{n}", shape, dt))

        def sem(n):
            return ctx.enter_context(nc.semaphore(f"l_{n}"))

        sums, means = sb("sums", [P, CHUNK, ACC1]), sb("means", [P, CHUNK, ACC1])
        share, factor = sb("share", [P, CHUNK]), sb("factor", [P, CHUNK])
        square, gain = sb("square", [P, CHUNK]), sb("gain", [P, CHUNK])
        resid = sb("resid", [P, CHUNK, D + 1])
        z, zc, zq, o = (sb(n, [P, CHUNK, D]) for n in ("z", "zc", "zq", "o"))
        stat, root, rinv = sb("stat", [P, 2 * CHUNK]), sb("root", [P, CHUNK]), sb("rinv", [P, CHUNK])
        w_s, w_v = sb("w_s", [MID, 1 + CS]), sb("w_v", [MID, CV])
        turned_rows = sb("turned_rows", [MID, 2, 512])
        pt = [ctx.enter_context(nc.psum_tensor(f"l_pt{i}", [P, 512], F32)) for i in range(2)]
        po = [ctx.enter_context(nc.psum_tensor(f"l_po{i}", [P, 512], F32)) for i in range(2)]
        weights, loaded, own, rooted, turned, copied, multiplied, stored, rested = (
            sem(n) for n in ("weights", "loaded", "dve", "rooted", "turned", "copied", "multiplied", "stored",
                             "rested"))
        MEANS, PER_BLOCK = 4, 2
        SPREAD = MEANS + PER_BLOCK * CHUNK + 6
        PER = SPREAD + 2
        block = ctx.enter_context(nc.Block())
        rv = resid_d.rearrange("(c b p) f -> c p b f", b=CHUNK, p=P)
        ov = out.rearrange("(c b p) f -> c p b f", b=CHUNK, p=P)
        sv = sums_d[0:blocks].rearrange("(c b) p f -> c p b f", b=CHUNK)

        @block.sync
        def _(sp):
            sp.dma_start(w_s[:, 0:1], w1["Wa"]).then_inc(weights, 16)
            sp.dma_start(w_s[:, 1:1 + CS], w1["Wl2_s"]).then_inc(weights, 16)
            sp.dma_start(w_v[:], w1["Wl2_v"]).then_inc(weights, 16)
            with sp.Fori(0, chunks) as c:
                sp.dma_start(sums[:], sv[c]).then_inc(loaded, 16)
                sp.dma_start(factor[:], factor_d[c]).then_inc(loaded, 16)
                sp.dma_start(resid[:], rv[c]).then_inc(loaded, 16)
                sp.wait_ge(own, (c + 1) * PER)
                sp.dma_start(ov[c], o[:]).then_inc(stored, 16)
                sp.wait_ge(stored, (c + 1) * 16)
                sp.sem_inc(rested, 1)

        @block.tensor
        def _(pe):
            pe.sem_inc(multiplied, 1)
            pe.wait_ge(weights, 48)
            with pe.Fori(0, chunks) as c:
                pe.wait_ge(own, c * PER + MEANS)
                for b in range(CHUNK + 1):
                    if b < CHUNK:
                        for k in range(4):
                            last = nc.tensor.transpose(pt[b % 2][0:MID, k * P:(k + 1) * P],
                                                       means[:, b, k * MID:(k + 1) * MID], ident[:])
                        last.then_inc(turned, 1)
                    if b >= 1:
                        pe.wait_ge(copied, c * CHUNK + b)
                        if b >= 3:
                            pe.wait_ge(own, c * PER + (MEANS + PER_BLOCK * (b - 2)))
                        rows, into = turned_rows[:, (b - 1) % 2, :], po[(b - 1) % 2]
                        nc.tensor.matmul(into[:, 0:1 + CS], rows[:, 0:P], w_s[:], start=True, stop=True)
                        for x in range(3):
                            at = 1 + CS + x * CV
                            last = nc.tensor.matmul(into[:, at:at + CV], rows[:, (1 + x) * P:(2 + x) * P], w_v[:],
                                                    start=True, stop=True)
                        last.then_inc(multiplied, 1)

        @block.scalar
        def _(act):
            with act.Fori(0, chunks) as c:
                for b in range(CHUNK):
                    act.wait_ge(turned, c * CHUNK + (b + 1))
                    act.wait_ge(multiplied, c * CHUNK + (b + 1))
                    nc.scalar.activation(turned_rows[:, b % 2, :], pt[b % 2][0:MID, :], ACT.Copy).then_inc(copied, 1)
                act.wait_ge(own, c * PER + SPREAD)
                nc.scalar.activation(root[:], stat[:, 0:CHUNK], ACT.Sqrt).then_inc(rooted, 1)

        @block.vector
        def _(dve):
            with dve.Fori(0, chunks) as c:
                d = Count(own, c, PER)
                dve.wait_ge(loaded, (c + 1) * 48)
                k2 = d.up(nc.vector.tensor_tensor(square[:], factor[:], factor[:], ALU.mult))
                k = d.up(nc.vector.reciprocal(share[:], resid[:, :, D]))
                dve.wait_ge(own, k2)
                d.up(nc.vector.tensor_scalar(square[:], square[:], 1.0 / MID, None, ALU.mult))
                dve.wait_ge(own, k)
                d.up(nc.vector.tensor_tensor(means[:], sums[:], bc(share[:], 2, ACC1), ALU.mult))
                assert d.n == MEANS
                for b in range(CHUNK):
                    dve.wait_ge(multiplied, c * CHUNK + (b + 2))
                    k = d.up(nc.vector.tensor_tensor(gain[:, b:b + 1], po[b % 2][:, 0:1], square[:, b:b + 1],
                                                     ALU.mult))
                    dve.wait_ge(own, k)
                    k = d.up(nc.vector.scalar_tensor_tensor(z[:, b, :], po[b % 2][:, 1:1 + D], gain[:, b:b + 1],
                                                            resid[:, b, 0:D], ALU.mult, ALU.add))
                dve.wait_ge(own, k)
                norm_steps(nc, dve, d, z[:], zc[:], zq[:], stat, root[:], rinv[:], rooted, c, o[:])
                assert d.n == PER


def message_passing(nc, xn, idx, harmonics, rbf, dst_windows, dst_tiles, first_dst, factor, w, w1, out):
    padded, groups = xn.shape[0], idx.shape[0]
    blocks = padded // P
    tiles = groups * TILES

    def dram(name, shape):
        return nc.dram_tensor(name, shape, F32, kind="Internal").ap()

    table_src, table_dst = dram("table_src", [padded, D]), dram("table_dst", [padded, D])
    h = dram("edge_values", [groups, P, TILES * HROW])
    sums0, sums1 = dram("sums0", [blocks + SPARE, P, HROW + 1]), dram("sums1", [blocks + SPARE, P, ACC1])
    table1, resid = dram("table1", [padded, D]), dram("resid", [padded, D + 1])

    basis = nc.dram_tensor("basis", [BASIS, rbf.shape[1]], BF16, kind="Internal").ap()

    with ExitStack() as ctx:
        ident = ctx.enter_context(nc.sbuf_tensor("ident", [P, P], F32))
        iota = ctx.enter_context(nc.sbuf_tensor("iota", [P, P], F32))
        constants(nc, ident, iota)

        splits(nc, rbf, basis)
        tables(nc, xn, table_src, table_dst, w, ident)
        steps = staircase_steps(groups, blocks)
        rows = (ctx.enter_context(nc.sbuf_tensor("unit_row", [1, steps], I32)),
                ctx.enter_context(nc.sbuf_tensor("slot_row", [1, steps], I32)),
                ctx.enter_context(nc.sbuf_tensor("b128", [P, steps], F32)),
                ctx.enter_context(nc.sbuf_tensor("keep", [P, steps], F32)))
        staircase(nc, "walk", first_dst, groups, blocks, *rows)
        with ExitStack() as inner:
            logits = inner.enter_context(nc.sbuf_tensor("logits", [P, tiles, HEADS], F32))
            edges(nc, idx, harmonics, basis, table_src, table_dst, h, w, ident, logits)
            softmax(nc, dst_windows, logits, ident)
            reduce_values(nc, h, *rows, dst_tiles, logits, sums0, iota)
        middle(nc, xn, sums0, factor, table1, resid, w, w1, ident)
        edges1(nc, idx, harmonics, basis, table1, *rows, w1, iota, sums1)
        final(nc, sums1, factor, resid, out, w1, ident)


_W0 = ["gamma_s", "beta_s", "gamma_v", "Ws_src", "Wv_src", "Ws_dst", "Wv_dst", "W_rbf", "W_alpha", "alpha_dot",
       "Ws_val", "Wv_val", "Wg", "w2_ss", "w2_sv", "w2_vs", "w2_vv0", "w2_vv1", "Ws_vlin", "Wv_vlin", "Wps", "Wpv"]
_W1 = ["Wfc1", "Wfc2", "Wsc0", "Wsc1", "Wl1_0", "Wl1_1", "Wl2_s", "Wl2_v", "Wa"]


def _layout(x, src, dst, edge_attr_16, edge_attr_4, node_vec1):
    n, n_edges = x.shape[0], src.shape[0]
    blocks = -(-n // (P * CHUNK)) * CHUNK
    padded = blocks * P
    edges_p = -(-n_edges // (SEG_TILES * P)) * SEG_TILES * P

    def pad(a, size, fill=0):
        out = np.full((size,) + a.shape[1:], fill, a.dtype)
        out[:a.shape[0]] = a
        return out

    def tiled(a, tiles):
        return a.reshape((-1, tiles, P) + a.shape[1:]).swapaxes(1, 2)

    xp = pad(x, padded)
    by_component = xp[:, CS:].reshape(padded, CV, 3).transpose(0, 2, 1).reshape(padded, 3 * CV)
    s, d = pad(src, edges_p), pad(dst, edges_p, padded - 1)
    y = pad(edge_attr_4, edges_p)
    none = np.full(1, -1, d.dtype)
    window = np.concatenate([none, d, none])
    span = SEG_TILES * P

    def firsts(size):
        got = d[::size][1:]
        got = pad(got, -(-got.shape[0] // P) * P, 1 << 20)
        return got.reshape(-1, P).T

    return {
        "xn": np.concatenate([xp[:, :CS], by_component], 1),
        "idx": np.concatenate([tiled(s, TILES), tiled(d, TILES)], 2),
        "harmonics": tiled(y[:, [0, 1, 2, 3, 1, 2]], TILES),
        "rbf": pad(edge_attr_16, edges_p).T,
        "dst_windows": np.stack([window[q * span:q * span + span + 2] for q in range(edges_p // span)]),
        "dst_tiles": d.reshape(-1, P).T,
        "first_dst": firsts(GROUP),
        "factor": pad(node_vec1, padded).reshape(-1, CHUNK, P).swapaxes(1, 2),
    }


def kernel(**inputs):
    import concourse.bacc as _bacc
    from concourse import mybir as _mybir
    from concourse.bass_utils import run_bass_kernel_spmd as _run

    nc = _bacc.Bacc("TRN2", target_bir_lowering=False, num_devices=1)
    graph = [np.asarray(inputs[n]) for n in ("x", "src", "dst", "edge_attr_16", "edge_attr_4", "node_vec1")]
    n = graph[0].shape[0]
    arrays = {}

    def given(name, a):
        a = np.ascontiguousarray(a)
        arrays[name] = a
        return nc.dram_tensor(name, a.shape, _mybir.dt.from_np(a.dtype), kind="ExternalInput").ap()

    laid = [given(name, a) for name, a in _layout(*graph).items()]
    w = {k: given("w0_" + k, inputs["L0_gnn_" + k]) for k in _W0}
    w1 = {k: given("w1_" + k, inputs["L1_gnn_" + k]) for k in _W1}
    out = nc.dram_tensor("out", laid[0].shape, _mybir.dt.from_np(np.dtype("float32")), kind="ExternalOutput").ap()
    message_passing(nc, *laid, w, w1, out)
    got = _run(nc, [arrays], core_ids=[0]).results[0]["out"][:n]
    vectors = got[:, CS:].reshape(n, 3, CV).transpose(0, 2, 1).reshape(n, 3 * CV)
    return np.concatenate([got[:, :CS], vectors], 1)
```

```python
import math
from contextlib import ExitStack

import numpy as np

import concourse.bass as bass
from concourse import mybir

P = 128
TILES = 4
GROUP = TILES * P
RING = 4
CS, CV = 64, 32
D = CS + 3 * CV
HEADS, AS, AV = 4, 16, 8
HW = AS + 3 * AV
HROW = HEADS * (HW + 1)
WN = 2 * CS + 3 * CV
WE = 192
SPARE = 2 * RING
SEG_TILES = 16
CHUNK = 7
PAIRS = ((0, 0), (0, 1), (0, 2), (1, 0), (1, 1), (2, 0))
BASIS = 16 * len(PAIRS)
MID = CS + CV
ACC1 = 4 * MID
EPS = 1e-5
FAR = 1.0e38

F32 = mybir.dt.float32
I32 = mybir.dt.int32
BF16 = mybir.dt.bfloat16
ALU = mybir.AluOpType
ACT = mybir.ActivationFunctionType
AX = mybir.AxisListType.X


def wait(engine, sem, value):
    if not isinstance(value, int) or value > 0:
        engine.wait_ge(sem, value)


class Count:

    def __init__(self, sem, round_, per):
        self.sem, self.base, self.n = sem, round_ * per, 0

    def up(self, instruction):
        instruction.then_inc(self.sem, 1)
        self.n += 1
        return self.base + self.n


def bc(ap, axis, size):
    shape = list(ap.shape)
    shape.insert(axis, size)
    return ap.unsqueeze(axis).broadcast_to(shape)


def row(ap):
    return ap.partition_broadcast(P)


def staircase_steps(units, blocks):
    steps = units + blocks - 1
    return -(-steps // RING) * RING


def constants(nc, ident, iota):
    with ExitStack() as ctx:
        made = ctx.enter_context(nc.semaphore("const_made"))
        iota_i = ctx.enter_context(nc.sbuf_tensor("iota_i", [P, P], I32))
        block = ctx.enter_context(nc.Block())

        @block.gpsimd
        def _(pool):
            nc.gpsimd.memset(ident[:], 0.0).then_inc(made, 1)
            nc.gpsimd.iota(iota_i[:], pattern=[[1, P]], base=0, channel_multiplier=0).then_inc(made, 1)
            pool.wait_ge(made, 2)
            nc.gpsimd.affine_select(out=ident[:], in_=ident[:], compare_op=ALU.not_equal, fill=1.0, base=0,
                                    pattern=[[-1, P]], channel_multiplier=1).then_inc(made, 1)
            nc.gpsimd.tensor_copy(iota[:], iota_i[:]).then_inc(made, 1)


def staircase(nc, name, first_dst, units, blocks, unit_row, slot_row, b128, keep):
    steps = staircase_steps(units, blocks)
    chunks = first_dst.shape[1]
    halves = [(c, min(steps, c + 512)) for c in range(0, steps, 512)]
    with ExitStack() as ctx:
        def sb(n, shape, dt=F32):
            return ctx.enter_context(nc.sbuf_tensor(f"{name}_{n}", shape, dt))

        first = sb("first", [P, chunks], I32)
        fb_i = sb("fb_i", [P, chunks], I32)
        fb = sb("fb", [P, chunks])
        idx_i = sb("idx_i", [P, chunks], I32)
        idx = sb("idx", [P, chunks])
        corner = sb("corner", [P, chunks])
        s_i = sb("s_i", [P, steps], I32)
        spare_i = sb("spare_i", [1, steps], I32)
        s_f = sb("s_f", [P, steps])
        spare = sb("spare", [1, steps])
        ones = sb("ones", [P, P])
        passed = sb("passed", [P, chunks, steps])
        u = sb("u", [P, steps])
        b = sb("b", [P, steps])
        slot = sb("slot", [1, steps])
        psum = [ctx.enter_context(nc.psum_tensor(f"{name}_ps{h}", [P, 512], F32)) for h in range(len(halves))]
        loaded = ctx.enter_context(nc.semaphore(f"{name}_loaded"))
        patterns = ctx.enter_context(nc.semaphore(f"{name}_patterns"))
        done = ctx.enter_context(nc.semaphore(f"{name}_dve"))
        summed = ctx.enter_context(nc.semaphore(f"{name}_summed"))
        block = ctx.enter_context(nc.Block())

        @block.sync
        def _(sp):
            sp.dma_start(first[:], first_dst).then_inc(loaded, 16)

        @block.gpsimd
        def _(pool):
            nc.gpsimd.iota(idx_i[:], pattern=[[P, chunks]], base=1, channel_multiplier=1).then_inc(patterns, 1)
            nc.gpsimd.iota(s_i[:], pattern=[[1, steps]], base=0, channel_multiplier=0).then_inc(patterns, 1)
            nc.gpsimd.iota(spare_i[:], pattern=[[0, steps // RING], [1, RING]], base=blocks + RING,
                           channel_multiplier=0).then_inc(patterns, 1)
            nc.gpsimd.memset(ones[:], 1.0).then_inc(patterns, 1)

        @block.tensor
        def _(pe):
            pe.wait_ge(patterns, 4)
            pe.wait_ge(done, 6 + chunks)
            for h, (lo, hi) in enumerate(halves):
                for c in range(chunks):
                    last = nc.tensor.matmul(psum[h][:, 0:hi - lo], ones[:], passed[:, c, lo:hi],
                                            start=c == 0, stop=c == chunks - 1)
            last.then_inc(summed, 1)

        @block.vector
        def _(dve):
            d = Count(done, 0, 0)
            dve.wait_ge(loaded, 16)
            dve.wait_ge(patterns, 4)
            d.up(nc.vector.tensor_scalar(fb_i[:], first[:], 7, None, ALU.arith_shift_right))
            d.up(nc.vector.tensor_copy(idx[:], idx_i[:]))
            d.up(nc.vector.tensor_copy(s_f[:], s_i[:]))
            d.up(nc.vector.tensor_copy(spare[:], spare_i[:]))
            dve.wait_ge(done, 1)
            d.up(nc.vector.tensor_copy(fb[:], fb_i[:]))
            dve.wait_ge(done, 5)
            dve.wait_ge(done, d.up(nc.vector.tensor_tensor(corner[:], fb[:], idx[:], ALU.add)))
            for c in range(chunks):
                d.up(nc.vector.tensor_scalar(passed[:, c, :], s_f[:], corner[:, c:c + 1], None, ALU.is_ge))
            dve.wait_ge(summed, 1)
            for h, (lo, hi) in enumerate(halves):
                d.up(nc.vector.tensor_copy(u[:, lo:hi], psum[h][:, 0:hi - lo]))
            dve.wait_ge(done, d.base + d.n)
            d.up(nc.vector.tensor_tensor(b[:], s_f[:], u[:], ALU.subtract))
            d.up(nc.vector.memset(keep[:, 0:1], 0.0))
            d.up(nc.vector.tensor_copy(unit_row[:], u[0:1, :]))
            k = d.up(nc.vector.tensor_tensor(keep[:, 1:steps], u[:, 1:steps], u[:, 0:steps - 1], ALU.subtract))
            dve.wait_ge(done, k)
            d.up(nc.vector.tensor_scalar(b128[:], b[:], float(P), None, ALU.mult))
            k = d.up(nc.vector.tensor_tensor(slot[:], spare[:], b[0:1, :], ALU.subtract))
            dve.wait_ge(done, k)
            k = d.up(nc.vector.tensor_tensor(slot[:, 0:steps - 1], slot[:, 0:steps - 1], keep[0:1, 1:steps],
                                             ALU.mult))
            k = d.up(nc.vector.memset(slot[:, steps - 1:steps], 0.0))
            dve.wait_ge(done, k)
            k = d.up(nc.vector.tensor_tensor(slot[:], slot[:], b[0:1, :], ALU.add))
            dve.wait_ge(done, k)
            k = d.up(nc.vector.tensor_copy(slot_row[:], slot[:]))
            dve.wait_ge(done, k)


def splits(nc, rbf_d, basis_d):
    bases = rbf_d.shape[0]
    lines = P // bases
    whole = rbf_d.rearrange("k (a n) -> (k a) n", a=lines)
    length = whole.shape[1]
    pieces = next(n for n in range(8, 65) if length % n == 0)
    size = length // pieces
    with ExitStack() as ctx:
        x, rest = (ctx.enter_context(nc.sbuf_tensor(f"b_{n}", [P, 2, size], F32)) for n in ("x", "rest"))
        part = ctx.enter_context(nc.sbuf_tensor("b_part", [P, 2, 3, size], BF16))
        loaded, stored = ([ctx.enter_context(nc.semaphore(f"b_{n}{i}")) for i in range(2)]
                          for n in ("loaded", "stored"))
        rounded = ctx.enter_context(nc.semaphore("b_rounded"))
        left = ctx.enter_context(nc.semaphore("b_left"))
        block = ctx.enter_context(nc.Block())
        columns = lambda ap, n: ap[:, n * size:(n + 1) * size]

        def store(sp, n):
            sp.wait_ge(rounded, 3 * (n + 1))
            for g, (k, _) in enumerate(PAIRS):
                rows = basis_d[g * bases:(g + 1) * bases, :].rearrange("k (a n) -> (k a) n", a=lines)
                sp.dma_start(columns(rows, n), part[:, n % 2, k, :]).then_inc(stored[n % 2], 16)

        @block.sync
        def _(sp):
            for n in range(pieces):
                if n >= 2:
                    sp.wait_ge(left, 2 * (n - 2) + 1)
                sp.dma_start(x[:, n % 2, :], columns(whole, n)).then_inc(loaded[n % 2], 16)
                if n >= 1:
                    store(sp, n - 1)
            store(sp, pieces - 1)
            for i in range(2):
                sp.wait_ge(stored[i], 16 * len(PAIRS) * ((pieces + 1 - i) // 2))

        @block.scalar
        def _(act):
            for n in range(pieces + 1):
                if n < pieces:
                    act.wait_ge(loaded[n % 2], 16 * (n // 2 + 1))
                    if n >= 2:
                        act.wait_ge(stored[n % 2], 16 * len(PAIRS) * (n // 2))
                if n >= 1:
                    for k in (1, 2):
                        act.wait_ge(left, 2 * (n - 1) + k)
                        nc.scalar.activation(part[:, (n - 1) % 2, k, :], rest[:, (n - 1) % 2, :],
                                             ACT.Copy).then_inc(rounded, 1)
                if n < pieces:
                    nc.scalar.activation(part[:, n % 2, 0, :], x[:, n % 2, :], ACT.Copy).then_inc(rounded, 1)

        @block.vector
        def _(dve):
            for n in range(pieces):
                at = n % 2
                for k in range(2):
                    dve.wait_ge(rounded, 3 * n + k + 1)
                    whole_part = x[:, at, :] if k == 0 else rest[:, at, :]
                    nc.vector.tensor_tensor(rest[:, at, :], whole_part, part[:, at, k, :],
                                            ALU.subtract).then_inc(left, 1)


def split_weight(nc, dve, whole, rest, parts, parted):
    take = lambda k, source: nc.vector.tensor_copy(parts[:, k, :], source).then_inc(parted, 1)
    leave = lambda k, source: nc.vector.tensor_tensor(rest, source, parts[:, k, :], ALU.subtract).then_inc(parted, 1)
    take(0, whole)
    dve.wait_ge(parted, 1)
    leave(0, whole)
    dve.wait_ge(parted, 2)
    take(1, rest)
    dve.wait_ge(parted, 3)
    leave(1, rest)
    dve.wait_ge(parted, 4)
    take(2, rest)


def stack_weight(engine, parts, stacked, sem):
    n = parts.shape[0]
    for g, (_, part) in enumerate(PAIRS):
        engine.dma_start(stacked[g * n:(g + 1) * n, :], parts[:, part, :]).then_inc(sem, 16)


def in_pairs(engine, chunks, body):
    for r in range(2):
        body(r, r, 0)
    with engine.Fori(1, chunks // 2) as j:
        for r in range(2):
            body(j * 2 + r, r, j)


def tables(nc, xn, table_src, table_dst, w, ident):
    blocks = xn.shape[0] // P
    chunks = blocks // CHUNK
    with ExitStack() as ctx:
        def sb(n, shape, dt=F32):
            return ctx.enter_context(nc.sbuf_tensor(f"t_{n}", shape, dt))

        def sem(n):
            return ctx.enter_context(nc.semaphore(f"t_{n}"))

        x = sb("x", [P, 2, CHUNK, D])
        xc = sb("xc", [P, CHUNK, CS])
        sq = sb("sq", [P, CHUNK, D])
        xnorm = sb("xnorm", [P, 2, CHUNK, D])
        stat = sb("stat", [P, 2 * CHUNK])
        mean = sb("mean", [P, CHUNK])
        root = sb("root", [P, 2 * CHUNK])
        rinv = sb("rinv", [P, 2 * CHUNK])
        gamma_s, beta_s, gamma_v = sb("gs", [P, CS]), sb("bs", [P, CS]), sb("gv", [P, CV])
        wa, wb = sb("wa", [P, 2 * D]), sb("wb", [CV, 2 * D])
        xt_a, xt_b = sb("xt_a", [P, 2, P]), sb("xt_b", [CV, 2, P])
        o = sb("o", [P, 2, CHUNK, 2 * D])
        pt = [ctx.enter_context(nc.psum_tensor(f"t_pt{i}", [P, 512], F32)) for i in range(2)]
        po = [ctx.enter_context(nc.psum_tensor(f"t_po{i}", [P, 512], F32)) for i in range(2)]
        zeroed, weights, own, rooted = sem("zeroed"), sem("weights"), sem("dve"), sem("rooted")
        turned, copied, multiplied, moved = sem("turned"), sem("copied"), sem("multiplied"), sem("moved")
        loaded, stored = ([sem(f"{n}{r}") for r in range(2)] for n in ("loaded", "stored"))
        n_weights = 3 + 2 * 4
        NORMED = 17
        SPREADS = 9
        xv = xn.rearrange("(c b p) f -> c p b f", b=CHUNK, p=P)
        sv = table_src.rearrange("(c b p) f -> c p b f", b=CHUNK, p=P)
        dv = table_dst.rearrange("(c b p) f -> c p b f", b=CHUNK, p=P)
        block = ctx.enter_context(nc.Block())

        @block.sync
        def _(sp):
            sp.dma_start(gamma_s[:], row(w["gamma_s"])).then_inc(weights, 16)
            sp.dma_start(beta_s[:], row(w["beta_s"])).then_inc(weights, 16)
            sp.dma_start(gamma_v[:], row(w["gamma_v"])).then_inc(weights, 16)
            sp.wait_ge(zeroed, 2)
            for side, (ws, wv) in enumerate((("Ws_src", "Wv_src"), ("Ws_dst", "Wv_dst"))):
                at = side * D
                sp.dma_start(wa[0:CS, at:at + CS], w[ws]).then_inc(weights, 16)
                for comp in range(3):
                    to = at + CS + comp * CV
                    into = wa[CS + comp * CV:CS + (comp + 1) * CV, to:to + CV] if comp < 2 else wb[:, to:to + CV]
                    sp.dma_start(into, w[wv]).then_inc(weights, 16)

            def store(c, r):
                if isinstance(c, int) and c < 0:
                    return
                sp.wait_ge(moved, (c + 1) * CHUNK)
                sp.dma_start(sv[c], o[:, r, :, 0:D]).then_inc(stored[r], 16)
                sp.dma_start(dv[c], o[:, r, :, D:2 * D]).then_inc(stored[r], 16)

            def body(c, r, j):
                wait(sp, own, (c - 1) * NORMED)
                sp.dma_start(x[:, r], xv[c]).then_inc(loaded[r], 16)
                store(c - 2, r)

            in_pairs(sp, chunks, body)
            store(chunks - 2, 0)
            store(chunks - 1, 1)
            for r in range(2):
                sp.wait_ge(stored[r], 32 * (chunks // 2))

        @block.gpsimd
        def _(pool):
            nc.gpsimd.memset(wa[:], 0.0).then_inc(zeroed, 1)
            nc.gpsimd.memset(wb[:], 0.0).then_inc(zeroed, 1)

        @block.scalar
        def _(act):
            def body(c, r, j):
                act.wait_ge(own, c * NORMED + SPREADS)
                nc.scalar.activation(root[:], stat[:], ACT.Sqrt).then_inc(rooted, 1)
                blocks(c - 1, 1 - r, j if r else j - 1)

            def blocks(c, r, j):
                if isinstance(c, int) and c < 0:
                    return
                for b in range(CHUNK + 1):
                    n = c * CHUNK + b
                    if b < CHUNK:
                        act.wait_ge(turned, n + 1)
                        wait(act, multiplied, n)
                        nc.scalar.activation(xt_a[:, b % 2, :], pt[b % 2][:, 0:P], ACT.Copy)
                        nc.scalar.activation(xt_b[:, b % 2, :], pt[b % 2][0:CV, P:2 * P],
                                             ACT.Copy).then_inc(copied, 1)
                    if b >= 1:
                        act.wait_ge(multiplied, n)
                        if b == 1:
                            wait(act, stored[r], j * 32)
                        nc.scalar.activation(o[:, r, b - 1, :], po[(b - 1) % 2][:, 0:2 * D],
                                             ACT.Copy).then_inc(moved, 1)

            in_pairs(act, chunks, body)
            blocks(chunks - 1, 1, chunks // 2 - 1)

        @block.tensor
        def _(pe):
            pe.wait_ge(weights, 16 * n_weights)

            def body(c, r, j):
                pe.wait_ge(own, (c + 1) * NORMED)
                for b in range(CHUNK + 1):
                    if b < CHUNK:
                        nc.tensor.transpose(pt[b % 2][:, 0:P], xnorm[:, r, b, 0:P], ident[:])
                        nc.tensor.transpose(pt[b % 2][0:CV, P:2 * P], xnorm[:, r, b, P:D],
                                            ident[:]).then_inc(turned, 1)
                    if b >= 1:
                        n = c * CHUNK + (b - 1)
                        pe.wait_ge(copied, n + 1)
                        wait(pe, moved, n if b == 1 else n - 1)
                        into = po[(b - 1) % 2][:, 0:2 * D]
                        nc.tensor.matmul(into, xt_a[:, (b - 1) % 2, :], wa[:], start=True, stop=False)
                        nc.tensor.matmul(into, xt_b[:, (b - 1) % 2, :], wb[:], start=False,
                                         stop=True).then_inc(multiplied, 1)

            in_pairs(pe, chunks, body)

        @block.vector
        def _(dve):
            dve.wait_ge(weights, 16 * n_weights)

            def body(c, r, j):
                s, v, rows = x[:, r, :, 0:CS], x[:, r, :, CS:D], xnorm[:, r]
                d = Count(own, c, NORMED)
                dve.wait_ge(loaded[r], (j + 1) * 16)
                wait(dve, own, c * NORMED)
                wait(dve, turned, (c - 1) * CHUNK)
                k = d.up(nc.vector.tensor_reduce(mean[:], s, AX, ALU.add))
                d.up(nc.vector.tensor_tensor(sq[:, :, CS:D], v, v, ALU.mult))
                dve.wait_ge(own, k)
                k = d.up(nc.vector.tensor_scalar(mean[:], mean[:], 1.0 / CS, None, ALU.mult))
                dve.wait_ge(own, k)
                k = d.up(nc.vector.tensor_tensor(xc[:], s, bc(mean[:], 2, CS), ALU.subtract))
                dve.wait_ge(own, k)
                k = d.up(nc.vector.tensor_tensor(sq[:, :, 0:CS], xc[:], xc[:], ALU.mult))
                dve.wait_ge(own, k)
                k = d.up(nc.vector.tensor_reduce(stat[:, 0:CHUNK], sq[:, :, 0:CS], AX, ALU.add))
                dve.wait_ge(own, k)
                d.up(nc.vector.tensor_scalar(stat[:, 0:CHUNK], stat[:, 0:CHUNK], 1.0 / CS, EPS, ALU.mult, ALU.add))
                k = d.up(nc.vector.tensor_reduce(stat[:, CHUNK:], sq[:, :, CS:D], AX, ALU.add))
                dve.wait_ge(own, k)
                k = d.up(nc.vector.tensor_scalar(stat[:, CHUNK:], stat[:, CHUNK:], 1.0 / CV, EPS, ALU.mult, ALU.add))
                assert d.n == SPREADS
                dve.wait_ge(rooted, c + 1)
                k = d.up(nc.vector.reciprocal(rinv[:], root[:]))
                dve.wait_ge(own, k)
                d.up(nc.vector.tensor_tensor(xc[:], xc[:], bc(rinv[:, 0:CHUNK], 2, CS), ALU.mult))
                k = d.up(nc.vector.tensor_tensor(rows[:, :, CS:D], v, bc(rinv[:, CHUNK:], 2, 3 * CV), ALU.mult))
                dve.wait_ge(own, k)
                k = d.up(nc.vector.tensor_tensor(xc[:], xc[:], bc(gamma_s[:], 1, CHUNK), ALU.mult))
                for comp in range(3):
                    part = rows[:, :, CS + comp * CV:CS + (comp + 1) * CV]
                    d.up(nc.vector.tensor_tensor(part, part, bc(gamma_v[:], 1, CHUNK), ALU.mult))
                dve.wait_ge(own, k)
                d.up(nc.vector.tensor_tensor(rows[:, :, 0:CS], xc[:], bc(beta_s[:], 1, CHUNK), ALU.add))
                assert d.n == NORMED

            in_pairs(dve, chunks, body)


def edges(nc, idx_d, y_d, rbf_d, table_src, table_dst, h_d, w, ident, logits):
    groups = idx_d.shape[0]
    T = TILES
    HD = HEADS * AS
    with ExitStack() as ctx:
        def sb(n, shape, dt=F32):
            return ctx.enter_context(nc.sbuf_tensor(f"e_{n}", shape, dt))

        def psum(n, size=512):
            return ctx.enter_context(nc.psum_tensor(f"e_{n}", [P, size], F32))

        def sem(n):
            return ctx.enter_context(nc.semaphore(f"e_{n}"))

        w_rbf, rest_rbf = sb("w_rbf", [16, WN]), sb("rest_rbf", [16, WN])
        parts_rbf, stack_rbf = sb("parts_rbf", [16, 3, WN], BF16), sb("stack_rbf", [BASIS, WN], BF16)
        w_first = sb("w_first", [MID, 2 * CS])
        w_val, w_hid = sb("w_val", [CS, MID]), sb("w_hid", [CS, MID])
        w_g = sb("w_g", [CS, CV])
        dot = sb("dot", [CS, HEADS])
        w_gate = sb("w_gate", [MID, CV + HEADS])
        w_v1 = sb("w_v1", [P, 2 * CV])
        w_v2 = sb("w_v2", [P, 2 * CV])
        w_h1 = sb("w_h1", [P, 2 * CV])
        w_h2 = sb("w_h2", [MID, CV + HD])
        w_hs = sb("w_hs", [P, HD + CV + HEADS])
        scale_1, scale_2 = sb("scale_1", [P, 1]), sb("scale_2", [MID, 1])
        scale_ss, scale_sv = sb("scale_ss", [P, 1]), sb("scale_sv", [P, 1])
        idx = sb("idx", [P, RING, 2 * T], I32)
        y = sb("y", [P, RING, T, 6])
        rbf = sb("rbf", [BASIS, RING, GROUP], BF16)
        g_src = sb("g_src", [P, RING, T, D])
        g_dst = sb("g_dst", [P, RING, T, D])
        msg = sb("msg", [P, 2, T, D])
        sy = sb("sy", [P, 2, T, CS])
        vy = sb("vy", [P, T, 3, CV])
        dsum = sb("dsum", [P, T, CV])
        wy = sb("wy", [P, T, CV])
        c1 = sb("c1", [P, T, 3, CV])
        c2 = sb("c2", [P, T, 3, CV])
        cross = sb("cross", [P, T, 3, CV])
        m1s = sb("m1s", [P, T, MID])
        m1v = sb("m1v", [P, T, 2 * P])
        m1t = sb("m1t", [P, 3, GROUP])
        hidden = sb("hidden", [P, 2, GROUP])
        gate = sb("gate", [P, 2, T, CV])
        mixed_v = sb("mixed_v", [P, T, 3, CV])
        gv = sb("gv", [P, T, 3, CV])
        vy2 = sb("vy2", [P, T, 3, CV])
        dsum2 = sb("dsum2", [P, T, CV])
        d1 = sb("d1", [P, T, 3, CV])
        d2 = sb("d2", [P, T, 3, CV])
        m2 = sb("m2", [P, T, 6 * CV + CV])
        m2t = sb("m2t", [P, 2, GROUP])
        hy = sb("hy", [P, T, 3, CV])
        h = sb("h", [P, 2, T, HEADS, HW + 1])

        ps_w = psum("ps_w", 1024)
        radial_w = ps_w[:].rearrange("p (t k) -> p t k", k=256)
        ps_t = [psum(f"ps_t{i}") for i in range(2)]
        ps_v = psum("ps_v", 1024)
        mix_v = ps_v[:].rearrange("p (t k) -> p t k", k=256)
        LIN, VX = CV, CV + HEADS
        VS = VX + 3 * CV
        ps_h = psum("ps_h", 1024)
        mix_h = ps_h[:].rearrange("p (t k) -> p t k", k=256)
        HS = 3 * CV
        HA, HL = HS + HD, HS + HD + CV

        weights, zeroed, scaled, setup, ones_set = (sem("weights"), sem("zeroed"), sem("scaled"), sem("setup"),
                                                    sem("ones_set"))
        idx_in, y_in, rbf_in, gathered = ([sem(f"{n}{r}") for r in range(RING)]
                                          for n in ("idx_in", "y_in", "rbf_in", "gathered"))
        stored = [sem(f"stored{r}") for r in range(2)]
        parted, stacked = sem("parted"), sem("stacked")
        factored = sem("factored")
        issued = sem("issued")
        summed = sem("summed")
        scalars_y = sem("scalars_y")
        radial = sem("radial")
        first = sem("first")
        second = sem("second")
        third = sem("third")
        turned = sem("turned")
        taken = sem("taken")
        mixed = sem("mixed")
        gated = sem("gated")
        valued = sem("valued")
        headed = sem("headed")
        kept = sem("kept")
        FIRST, SECOND, THIRD = 14, 13, 6
        DONE_S, VREAD = 7, 3

        def turn(u, second_tp, k):
            if second_tp:
                return u * 6 + ((5 if isinstance(u, int) and u == groups - 1 else 9) + k)
            return k + 1 if isinstance(u, int) and u == 0 else u * 6 + (k - 1)

        def rounds(engine, body):
            for r in range(RING):
                body(r, r, 0)
            last = groups // RING - 1
            if last > 1:
                with engine.Fori(1, last) as i:
                    for r in range(RING):
                        body(i * RING + r, r, i)
            for r in range(RING):
                body(last * RING + r, r, last)

        def present(u):
            return not isinstance(u, int) or 0 <= u < groups

        block_wise = (w_v1, w_v2, w_h1, w_h2, w_hs, dot)
        column = lambda v: v.rearrange("(p a) -> p a", a=1)
        alpha_dot = w["alpha_dot"].rearrange("a h k -> h k a")
        val, vlin = w["Wv_val"], w["Wv_vlin"]
        placements = [
            (w_rbf[:], w["W_rbf"]), (w_first[:, 0:CS], w["W_alpha"]), (w_first[:, CS:2 * CS], w["Ws_val"]),
            (w_g[:], w["Wg"]),
            (w_v1[0:CS, 0:CV], val[CS:P]), (w_v1[CS:P, CV:2 * CV], val[CS:P]),
            (w_v2[0:CS, 0:CV], val[CS:P]), (w_v2[CS:P, CV:2 * CV], val[0:CS]),
            (w_h1[0:CS, 0:CV], vlin[CS:P]), (w_h1[CS:P, CV:2 * CV], vlin[CS:P]),
            (w_h2[0:CS, 0:CV], vlin[CS:P]), (w_h2[CS:MID, CV:CV + HD], w["Ws_vlin"][CS:MID]),
            (w_hs[CS:P, 0:HD], w["Ws_vlin"][0:CS]), (w_hs[CS:P, HD:HD + CV], vlin[0:CS]),
            (scale_ss[CS:P], column(w["w2_ss"])), (scale_sv[CS:P], column(w["w2_sv"])),
            (scale_2[CS:MID], column(w["w2_vv0"])),
        ]
        for tile, at in ((scale_1, 0), (scale_1, CS), (scale_2, 0)):
            placements += [(tile[at:at + CV], column(w["w2_vs"])), (tile[at + CV:at + CS], column(w["w2_vv1"]))]
        for hd in range(HEADS):
            rows = slice(hd * AS, (hd + 1) * AS)
            placements += [(dot[rows, hd:hd + 1], alpha_dot[hd]),
                           (w_hs[rows, HD + CV + hd:HD + CV + hd + 1], alpha_dot[hd])]
        block = ctx.enter_context(nc.Block())

        @block.sync
        def _(sp):
            sp.wait_ge(zeroed, len(block_wise))
            for to, source in placements:
                sp.dma_start(to, source).then_inc(weights, 16)
            sp.wait_ge(parted, 5)
            stack_weight(sp, parts_rbf, stack_rbf, stacked)

            def load(u, r, i):
                at = u * GROUP if isinstance(u, int) else sp.snap(u * GROUP)
                wait(sp, gathered[r], i * 32 * T)
                sp.dma_start(idx[:, r, :], idx_d[u]).then_inc(idx_in[r], 16)
                wait(sp, radial, u - (RING - 1))
                sp.dma_start(rbf[:, r, :], rbf_d[:, bass.ds(at, GROUP)]).then_inc(rbf_in[r], 16)

            rounds(sp, load)

        @block.gpsimd
        def _(pool):
            for tile in block_wise:
                nc.gpsimd.memset(tile[:], 0.0).then_inc(zeroed, 1)
            nc.gpsimd.memset(h[:], 1.0).then_inc(ones_set, 1)

            def gather(u, r, i):
                pool.wait_ge(idx_in[r], (i + 1) * 16)
                wait(pool, summed, u - (RING - 1))
                pool.sem_inc(issued, 1)
                for side, (table, into) in enumerate(((table_src, g_src), (table_dst, g_dst))):
                    for t in range(T):
                        c = side * T + t
                        pool.indirect_dma_start(
                            out=into[:, r, t, :], out_offset=None, in_=table,
                            in_offset=bass.IndirectOffsetOnAxis(ap=idx[:, r, c:c + 1], axis=0),
                        ).then_inc(gathered[r], 16)

            def body(u, r, i):
                if present(u + 2):
                    gather(u + 2, (r + 2) % RING, i + (r + 2) // RING)
                add_up(u + 1, (r + 1) % RING, i + (r + 1) // RING)

            def add_up(u, r, i):
                if not present(u):
                    return
                pool.wait_ge(gathered[r], (i + 1) * 32 * T)
                wait(pool, first, (u - 1) * FIRST)
                nc.gpsimd.tensor_tensor(msg[:, r % 2], g_src[:, r], g_dst[:, r], ALU.add).then_inc(summed, 1)

            gather(0, 0, 0)
            gather(1, 1, 0)
            add_up(0, 0, 0)
            rounds(pool, body)

        @block.tensor
        def _(pe):
            pe.wait_ge(scaled, 1)
            nc.tensor.transpose(ps_t[0][0:CS, 0:MID], w_first[:, CS:2 * CS], ident[0:MID, 0:MID])
            nc.tensor.transpose(ps_t[0][0:CS, P:P + MID], w_first[:, 0:CS], ident[0:MID, 0:MID]).then_inc(setup, 1)
            pe.wait_ge(scaled, 2)
            nc.tensor.matmul(ps_t[1][0:MID, 0:CV], w_val[:], w_g[:], start=True, stop=True)
            nc.tensor.matmul(ps_t[1][0:MID, CV:CV + HEADS], w_hid[:], dot[:], start=True, stop=True).then_inc(setup, 1)
            pe.wait_ge(scaled, 3)
            pe.wait_ge(stacked, 16 * len(PAIRS))

            def radial_weights(u, r, i):
                pe.wait_ge(rbf_in[r], (i + 1) * 16)
                wait(pe, first, u * FIRST)
                for t in range(T):
                    last = nc.tensor.matmul(radial_w[:, t, 0:WN],
                                            rbf[:, r, t * P:(t + 1) * P], stack_rbf[:], start=True, stop=True)
                last.then_inc(radial, 1)

            def turn_block(place, bank, rows):
                wait(pe, taken, place - 2)
                for t in range(T):
                    channels = rows(t).shape[1]
                    last = nc.tensor.transpose(ps_t[bank][0:channels, t * P:(t + 1) * P], rows(t), ident[:])
                last.then_inc(turned, 1)

            def first_blocks(u):
                pe.wait_ge(first, u * FIRST + DONE_S)
                turn_block(turn(u, False, 0), 0, lambda t: m1s[:, t, :])
                pe.wait_ge(first, (u + 1) * FIRST)
                turn_block(turn(u, False, 1), 1, lambda t: m1v[:, t, 0:P])
                pe.wait_ge(taken, turn(u, False, 0))
                nc.tensor.matmul(ps_t[0][:], w_first[:], m1t[0:MID, 0, :], start=True, stop=True).then_inc(turned, 1)
                turn_block(turn(u, False, 3), 1, lambda t: m1v[:, t, P:2 * P])

            def mix(u):
                pe.wait_ge(taken, turn(u, False, 3))
                wait(pe, gated, u)
                if present(u - 1):
                    pe.wait_ge(second, (u - 1) * SECOND + VREAD)
                for t in range(T):
                    tile = slice(t * P, (t + 1) * P)
                    nc.tensor.matmul(mix_v[:, t, 0:VX], m1t[0:MID, 0, tile], w_gate[:], start=True, stop=True)
                    nc.tensor.matmul(mix_v[:, t, VX:VX + 2 * CV], m1t[:, 1, tile], w_v1[:], start=True, stop=True)
                    last = nc.tensor.matmul(mix_v[:, t, VX + 2 * CV:VX + 4 * CV], m1t[:, 2, tile], w_v2[:],
                                            start=True, stop=True)
                last.then_inc(mixed, 1)

            def second_blocks(v, slot):
                if not present(v):
                    return
                wait(pe, third, v * THIRD)
                for t in range(T):
                    last = nc.tensor.matmul(mix_h[:, t, HS:HL + HEADS], hidden[:, slot, t * P:(t + 1) * P], w_hs[:],
                                            start=True, stop=True)
                last.then_inc(headed, 1)
                pe.wait_ge(second, (v + 1) * SECOND)
                turn_block(turn(v, True, 0), 0, lambda t: m2[:, t, 0:P])
                turn_block(turn(v, True, 1), 1, lambda t: m2[:, t, P:P + MID])

            def values(v):
                if not present(v):
                    return
                pe.wait_ge(taken, turn(v, True, 1))
                pe.wait_ge(kept, v + 1)
                for t in range(T):
                    tile = slice(t * P, (t + 1) * P)
                    nc.tensor.matmul(mix_h[:, t, 0:2 * CV], m2t[:, 0, tile], w_h1[:], start=True, stop=True)
                    last = nc.tensor.matmul(mix_h[:, t, 2 * CV:HA], m2t[0:MID, 1, tile], w_h2[:],
                                            start=True, stop=True)
                last.then_inc(valued, 1)

            def body(u, r, i):
                first_blocks(u)
                if present(u + 1):
                    radial_weights(u + 1, (r + 1) % RING, i + (r + 1) // RING)
                second_blocks(u - 1, (r - 1) % 2)
                mix(u)
                values(u - 1)

            radial_weights(0, 0, 0)
            rounds(pe, body)
            second_blocks(groups - 1, (groups - 1) % 2)
            values(groups - 1)

        @block.scalar
        def _(act):
            act.wait_ge(ones_set, 1)

            def take(place, bank, into):
                act.wait_ge(turned, place)
                rows = into.shape[0]
                nc.scalar.activation(into, ps_t[bank][0:rows, :], ACT.Copy).then_inc(taken, 1)

            def body(u, r, i):
                slot = r % 2
                wait(act, mixed, u)
                take(turn(u, False, 0), 0, m1t[0:MID, 0, :])
                take(turn(u, False, 1), 1, m1t[:, 1, :])
                act.wait_ge(turned, turn(u, False, 2))
                wait(act, valued, u - 1)
                nc.scalar.activation(hidden[0:CS, slot, :], ps_t[0][0:CS, :], ACT.Relu, scale=0.8)
                nc.scalar.activation(hidden[CS:P, slot, :], ps_t[0][CS:P, :], ACT.Sigmoid).then_inc(taken, 1)
                take(turn(u, False, 3), 1, m1t[:, 2, :])
                store(u - 2, slot)
                if present(u + 2):
                    harmonics(u + 2, (r + 2) % RING)
                with_y0(u + 1, (r + 1) % RING, i + (r + 1) // RING)
                keep(u - 1, (r - 1) % RING, 1 - slot, i * 2 + (r - 1) // 2)
                act.wait_ge(mixed, u + 1)
                if present(u - 2):
                    act.wait_ge(second, (u - 1) * SECOND)
                nc.scalar.activation(gate[:, slot], mix_v[:, :, 0:CV], ACT.Sigmoid).then_inc(gated, 1)

            def harmonics(u, r):
                act.dma_start(y[:, r], y_d[u]).then_inc(y_in[r], 16)

            def keep(v, r, slot, n):
                if not present(v):
                    return
                act.wait_ge(headed, v + 1)
                wait(act, stored[slot], n * 16)
                for t in range(T):
                    last = nc.scalar.activation(h[:, slot, t, :, 0:AS],
                                                mix_h[:, t, HS:HA].rearrange("p (h k) -> p h k", k=AS),
                                                ACT.Copy, scale=y[:, r, t, 0:1])
                last.then_inc(kept, 1)
                take(turn(v, True, 0), 0, m2t[:, 0, :])
                take(turn(v, True, 1), 1, m2t[0:MID, 1, :])

            def store(v, slot):
                if not present(v):
                    return
                act.wait_ge(third, (v + 1) * THIRD)
                act.dma_start(h_d[v], h[:, slot].rearrange("p t h k -> p (t h k)")).then_inc(stored[slot], 16)

            def with_y0(u, r, i):
                if not present(u):
                    return
                act.wait_ge(summed, u + 1)
                act.wait_ge(y_in[r], (i + 1) * 16)
                wait(act, first, (u - 1) * FIRST)
                for t in range(T):
                    last = nc.scalar.activation(sy[:, r % 2, t, :], msg[:, r % 2, t, 0:CS], ACT.Copy,
                                                scale=y[:, r, t, 0:1])
                last.then_inc(scalars_y, 1)

            harmonics(0, 0)
            harmonics(1, 1)
            with_y0(0, 0, 0)
            rounds(act, body)
            store(groups - 2, groups % 2)
            keep(groups - 1, RING - 1, (groups - 1) % 2, (groups - 1) // 2)
            store(groups - 1, (groups - 1) % 2)
            for slot in range(2):
                act.wait_ge(stored[slot], 16 * (groups // 2))

        @block.vector
        def _(dve):
            dve.wait_ge(weights, 16 * len(placements))
            by = lambda tile, factor: nc.vector.tensor_scalar(tile, tile, factor, None, ALU.mult)
            r2, r3 = 1.0 / math.sqrt(2.0), 1.0 / math.sqrt(3.0)
            for tile, factor in (
                    (w_rbf[:, 2 * CS + CV:2 * CS + 2 * CV], r3), (w_rbf[:, 2 * CS + 2 * CV:WN], r2),
                    (scale_1[CV:CS], r2), (scale_1[MID:P], r2), (scale_2[CV:CS], r2), (scale_2[CS:MID], r3),
                    (w_hs[CS:P, 0:HD], scale_ss[CS:P, 0:1]), (w_hs[CS:P, HD:HD + CV], scale_sv[CS:P, 0:1])):
                by(tile, factor).then_inc(factored, 1)
            dve.wait_ge(factored, 8)
            split_weight(nc, dve, w_rbf[:], rest_rbf[:], parts_rbf, parted)
            by(w_h1[:], scale_1[:, 0:1])
            by(w_h2[:], scale_2[:, 0:1]).then_inc(scaled, 1)
            dve.wait_ge(setup, 1)
            nc.vector.tensor_copy(w_val[:], ps_t[0][0:CS, 0:MID])
            nc.vector.tensor_copy(w_hid[:], ps_t[0][0:CS, P:P + MID]).then_inc(scaled, 1)
            dve.wait_ge(setup, 2)
            nc.vector.tensor_copy(w_gate[:, 0:CV], ps_t[1][0:MID, 0:CV])
            nc.vector.tensor_scalar(w_gate[:, CV:CV + HEADS], ps_t[1][0:MID, CV:CV + HEADS], 0.2, None,
                                    ALU.mult).then_inc(scaled, 1)

            mult = lambda out, a, b: nc.vector.tensor_tensor(out, a, b, ALU.mult)
            add = lambda out, a, b: nc.vector.tensor_tensor(out, a, b, ALU.add)
            subtract = lambda out, a, b: nc.vector.tensor_tensor(out, a, b, ALU.subtract)

            def cross_parts(p1, p2, out, d, k):
                dve.wait_ge(d.sem, k)
                for x in range(3):
                    k = d.up(subtract(out(x), p1[:, :, (x + 1) % 3, :], p2[:, :, (x + 2) % 3, :]))
                return k

            def first_product(u, r, i):
                d = Count(first, u, FIRST)
                m = msg[:, r % 2]
                s, v = m[:, :, 0:CS], m[:, :, CS:D].rearrange("p t (x c) -> p t x c", x=3)
                y0, yx = y[:, r, :, 0], y[:, r, :, 1:4]
                w_ss, w_sv = radial_w[:, :, 0:CS], radial_w[:, :, CS:2 * CS]
                w_vs, w_vv0, w_vv1 = (radial_w[:, :, 2 * CS + n * CV:2 * CS + (n + 1) * CV] for n in range(3))
                pairs = m1v[:, :, 0:6 * CV].rearrange("p t (x k c) -> p t x k c", x=3, k=2)
                dve.wait_ge(summed, u + 1)
                dve.wait_ge(y_in[r], (i + 1) * 16)
                k_vy = d.up(mult(vy[:], v, bc(yx, 3, CV)))
                d.up(mult(c1[:], v, bc(y[:, r, :, 2:5], 3, CV)))
                dve.wait_ge(first, k_vy)
                k_dot = d.up(add(dsum[:], vy[:, :, 0, :], vy[:, :, 1, :]))
                k_c = d.up(mult(c2[:], v, bc(y[:, r, :, 3:6], 3, CV)))
                dve.wait_ge(first, k_dot)
                k_dot = d.up(add(dsum[:], dsum[:], vy[:, :, 2, :]))
                dve.wait_ge(radial, u + 1)
                if present(u - 1):
                    dve.wait_ge(turned, turn(u - 1, False, 3))
                dve.wait_ge(scalars_y, u + 1)
                d.up(mult(m1s[:, :, 0:CS], sy[:, r % 2], w_ss))
                dve.wait_ge(first, k_dot)
                d.up(mult(m1s[:, :, CS:MID], dsum[:], w_vv0))
                assert d.n == DONE_S
                d.up(mult(m1v[:, :, 6 * CV:2 * P], s, w_sv))
                k_wy = d.up(mult(wy[:], w_vs, bc(y0, 2, CV)))
                k_cross = cross_parts(c1, c2, lambda x: cross[:, :, x, :], d, k_c)
                dve.wait_ge(first, k_wy)
                d.up(mult(pairs[:, :, :, 0, :], v, bc(wy[:], 2, 3)))
                dve.wait_ge(first, k_cross)
                d.up(mult(pairs[:, :, :, 1, :], cross[:], bc(w_vv1, 2, 3)))
                assert d.n == FIRST

            def second_product(v, r, between):
                if not present(v):
                    return
                d = Count(second, v, SECOND)
                y0, yx = y[:, r, :, 0], y[:, r, :, 1:4]
                vectors = mix_v[:, :, VX:VS].rearrange("p t (x c) -> p t x c", x=3)
                pairs = m2[:, :, 0:6 * CV].rearrange("p t (x k c) -> p t x k c", x=3, k=2)
                dve.wait_ge(gated, v + 1)
                if present(v - 1):
                    dve.wait_ge(turned, turn(v - 1, True, 1))
                k = d.up(mult(mixed_v[:], bc(mix_v[:, :, VS:VS + CV], 2, 3), bc(yx, 3, CV)))
                d.up(nc.vector.tensor_copy(logits[:, bass.ds(v * T, T), :], mix_v[:, :, LIN:LIN + HEADS]))
                dve.wait_ge(second, k)
                k = d.up(add(mixed_v[:], mixed_v[:], vectors))
                assert d.n == VREAD
                between()
                dve.wait_ge(second, k)
                k_gv = d.up(mult(gv[:], mixed_v[:], bc(gate[:, r % 2], 2, 3)))
                dve.wait_ge(second, k_gv)
                k_vy = d.up(mult(vy2[:], gv[:], bc(yx, 3, CV)))
                d.up(mult(d1[:], gv[:], bc(y[:, r, :, 2:5], 3, CV)))
                dve.wait_ge(second, k_vy)
                k_dot = d.up(add(dsum2[:], vy2[:, :, 0, :], vy2[:, :, 1, :]))
                k_c = d.up(mult(d2[:], gv[:], bc(y[:, r, :, 3:6], 3, CV)))
                dve.wait_ge(second, k_dot)
                d.up(add(m2[:, :, 6 * CV:7 * CV], dsum2[:], vy2[:, :, 2, :]))
                d.up(mult(pairs[:, :, :, 0, :], gv[:], bc(bc(y0, 2, 3), 3, CV)))
                cross_parts(d1, d2, lambda x: pairs[:, :, x, 1, :], d, k_c)
                assert d.n == SECOND

            def last_step(v, r):
                if not present(v):
                    return
                d = Count(third, v, THIRD)
                yx = y[:, r, :, 1:4]
                dve.wait_ge(valued, v + 1)
                k = d.up(mult(hy[:], bc(mix_h[:, :, HA:HL], 2, 3), bc(yx, 3, CV)))
                d.up(add(logits[:, bass.ds(v * T, T), :], logits[:, bass.ds(v * T, T), :],
                         mix_h[:, :, HL:HL + HEADS]))
                dve.wait_ge(third, k)
                for x in range(3):
                    by_head = h[:, r % 2, :, :, AS + x * AV:AS + (x + 1) * AV]
                    d.up(add(by_head, hy[:, :, x, :].rearrange("p t (h k) -> p t h k", k=AV),
                             mix_h[:, :, x * CV:(x + 1) * CV].rearrange("p t (h k) -> p t h k", k=AV)))
                scalars = h[:, r % 2, :, :, 0:AS]
                d.up(add(scalars, scalars, mix_h[:, :, HS:HA].rearrange("p t (h k) -> p t h k", k=AS)))
                assert d.n == THIRD

            def body(u, r, i):
                first_product(u, r, i)
                second_product(u - 1, (r - 1) % RING, lambda: last_step(u - 2, (r - 2) % RING))

            rounds(dve, body)
            second_product(groups - 1, RING - 1, lambda: last_step(groups - 2, RING - 2))
            last_step(groups - 1, RING - 1)
            dve.wait_ge(third, groups * THIRD)


def softmax(nc, dst_windows, logits, ident):
    tiles = logits.shape[1]
    parts = tiles // SEG_TILES
    edges_on = SEG_TILES * P
    with ExitStack() as ctx:
        def sb(n, shape, dt=F32):
            return ctx.enter_context(nc.sbuf_tensor(f"s_{n}", shape, dt))

        def sem(n):
            return ctx.enter_context(nc.semaphore(f"s_{n}"))

        dst_i = sb("dst_i", [parts, edges_on + 2], I32)
        dst = sb("dst", [parts, edges_on + 2])
        breaks = [sb(f"breaks{i}", [parts, edges_on]) for i in range(2)]
        broken = sb("broken", [parts, 2])
        rows = sb("rows", [parts, HEADS, edges_on])
        best = sb("best", [parts, HEADS, edges_on])
        ends = sb("ends", [parts, 2, HEADS])
        breaks4 = sb("breaks4", [parts, 2, HEADS])
        turned_ends = sb("turned_ends", [HEADS, 2, 2 * P])
        carried = sb("carried", [HEADS, 2, parts + 1])
        start = sb("start", [parts, 2, HEADS])
        ps_in = [ctx.enter_context(nc.psum_tensor(f"s_in{i}", [P, 512], F32)) for i in range(2)]
        ps_out = [ctx.enter_context(nc.psum_tensor(f"s_out{i}", [P, 512], F32)) for i in range(2)]
        ps_c = ctx.enter_context(nc.psum_tensor("s_c", [P, 512], F32))
        loaded, own, turned, taken, back, ended, expd = (sem("loaded"), sem("dve"), sem("turned"), sem("taken"),
                                                        sem("back"), sem("ended"), sem("exp"))
        by_tile = logits[:].rearrange("p (q c) h -> p c q h", c=SEG_TILES)
        block = ctx.enter_context(nc.Block())
        C4 = SEG_TILES // 4
        SETUP = 7
        PASS = 2 * HEADS + 6

        @block.sync
        def _(sp):
            sp.dma_start(dst_i[:], dst_windows).then_inc(loaded, 16)

        @block.tensor
        def _(pe):
            for n in range(HEADS * C4):
                hd, c4 = n // C4, n % C4
                if n >= 2:
                    pe.wait_ge(taken, n - 1)
                for j in range(4):
                    last = nc.tensor.transpose(ps_in[n % 2][0:parts, j * P:(j + 1) * P],
                                               by_tile[:, c4 * 4 + j, :, hd], ident[:])
                last.then_inc(turned, 1)
            for side in range(2):
                pe.wait_ge(own, SETUP + side * PASS + HEADS + 2)
                nc.tensor.transpose(ps_c[0:HEADS, 0:parts], ends[:, side, :], ident[0:parts, 0:parts])
                nc.tensor.transpose(ps_c[0:HEADS, P:P + parts], breaks4[:, side, :],
                                    ident[0:parts, 0:parts]).then_inc(ended, 1)
                pe.wait_ge(own, SETUP + side * PASS + HEADS + 5)
                before = carried[:, side, 0:parts] if side == 0 else carried[:, side, 1:parts + 1]
                nc.tensor.transpose(ps_c[0:parts, 256:256 + HEADS], before,
                                    ident[0:HEADS, 0:HEADS]).then_inc(ended, 1)
            pe.wait_ge(own, SETUP + 2 * PASS)
            for n in range(HEADS * C4):
                hd, c4 = n // C4, n % C4
                if n >= 2:
                    pe.wait_ge(own, SETUP + 2 * PASS + n - 1)
                for j in range(4):
                    at = (c4 * 4 + j) * P
                    last = nc.tensor.transpose(ps_out[n % 2][:, j * P:j * P + parts],
                                               rows[:, hd, at:at + P], ident[0:parts, 0:parts])
                last.then_inc(back, 1)

        @block.scalar
        def _(act):
            for n in range(HEADS * C4):
                hd, c4 = n // C4, n % C4
                act.wait_ge(turned, n + 1)
                nc.scalar.activation(rows[:, hd, c4 * 512:(c4 + 1) * 512], ps_in[n % 2][0:parts, :],
                                     ACT.Copy).then_inc(taken, 1)
            act.wait_ge(own, SETUP + 2 * PASS + HEADS * C4)
            nc.scalar.activation(logits[:], logits[:], ACT.Exp).then_inc(expd, 1)
            act.wait_ge(expd, 1)

        @block.vector
        def _(dve):
            d = Count(own, 0, 0)
            dve.wait_ge(loaded, 16)
            dve.wait_ge(own, d.up(nc.vector.tensor_copy(dst[:], dst_i[:])))
            for side in range(2):
                k = d.up(nc.vector.tensor_tensor(breaks[side][:], dst[:, 1:edges_on + 1],
                                                 dst[:, 2 * side:2 * side + edges_on], ALU.not_equal))
                dve.wait_ge(own, k)
                k = d.up(nc.vector.tensor_scalar(breaks[side][:], breaks[side][:], -FAR, None, ALU.mult))
                dve.wait_ge(own, k)
                d.up(nc.vector.tensor_reduce(broken[:, side:side + 1], breaks[side][:], AX, ALU.min))
            assert d.n == SETUP
            dve.wait_ge(taken, HEADS * C4)
            for side in range(2):
                def scans(initial):
                    for hd in range(HEADS):
                        first = -FAR if initial is None else initial[:, hd:hd + 1]
                        if side == 0:
                            out, step, fed = best[:, hd, :], breaks[0][:], rows[:, hd, :]
                        else:
                            out, step, fed = rows[:, hd, ::-1], breaks[1][:, ::-1], best[:, hd, ::-1]
                        d.up(nc.vector.tensor_tensor_scan(out=out, data0=step, data1=fed, initial=first,
                                                          op0=ALU.add, op1=ALU.max))
                    dve.wait_ge(own, d.n)

                scans(None)
                d.up(nc.vector.tensor_copy(ends[:, side, :],
                                           best[:, :, edges_on - 1] if side == 0 else rows[:, :, 0]))
                d.up(nc.vector.tensor_copy(breaks4[:, side, :],
                                           broken[:, side:side + 1].broadcast_to([parts, HEADS])))
                dve.wait_ge(ended, 2 * side + 1)
                d.up(nc.vector.tensor_copy(turned_ends[:, side, :].rearrange("h (k q) -> h k q", k=2)[:, :, 0:parts],
                                           ps_c[0:HEADS, 0:2 * P].rearrange("h (k q) -> h k q", k=2)[:, :, 0:parts]))
                outside = 0 if side == 0 else parts
                d.up(nc.vector.memset(carried[:, side, outside:outside + 1], -FAR))
                dve.wait_ge(own, d.n)
                last, broke = turned_ends[:, side, 0:parts], turned_ends[:, side, P:P + parts]
                if side == 0:
                    out = carried[:, side, 1:parts + 1]
                else:
                    out, last, broke = (a[:, ::-1] for a in (carried[:, side, 0:parts], last, broke))
                d.up(nc.vector.tensor_tensor_scan(out=out, data0=broke, data1=last, initial=-FAR,
                                                  op0=ALU.add, op1=ALU.max))
                dve.wait_ge(ended, 2 * side + 2)
                d.up(nc.vector.tensor_copy(start[:, side, :], ps_c[0:parts, 2 * P:2 * P + HEADS]))
                dve.wait_ge(own, d.n)
                scans(start[:, side, :])
            assert d.n == SETUP + 2 * PASS
            for n in range(HEADS * C4):
                hd, c4 = n // C4, n % C4
                dve.wait_ge(back, n + 1)
                part = by_tile[:, c4 * 4:c4 * 4 + 4, :, hd]
                d.up(nc.vector.tensor_tensor(
                    part, part, ps_out[n % 2][:].rearrange("p (c q) -> p c q", c=4)[:, :, 0:parts], ALU.subtract))


def reduce_values(nc, h_d, unit_row, slot_row, b128, keep, dst_tiles, weights_of_edges, sums_d, iota):
    steps = b128.shape[1]
    groups = h_d.shape[0]
    T = TILES
    with ExitStack() as ctx:
        def sb(n, shape, dt=F32):
            return ctx.enter_context(nc.sbuf_tensor(f"r_{n}", shape, dt))

        def sem(n):
            return ctx.enter_context(nc.semaphore(f"r_{n}"))

        h = sb("h", [P, RING, T, HROW + 1])
        headed = [h[:, r, :, 0:HROW].rearrange("p t (h k) -> p t h k", h=HEADS) for r in range(RING)]
        rel = sb("rel", [P, 2, T])
        dst_i = sb("dst_i", list(dst_tiles.shape), I32)
        dst = sb("dst", list(dst_tiles.shape))
        onehot = sb("onehot", [P, 2, T, P])
        acc = sb("acc", [P, RING, HROW + 1])
        ps = [ctx.enter_context(nc.psum_tensor(f"r_ps{i}", [P, 512], F32)) for i in range(2)]
        loaded, stored = ([sem(f"{n}{i}") for i in range(RING)] for n in ("loaded", "stored"))
        dst_in, dst_f, weighed, hot, added, multiplied = (sem("dst_in"), sem("dst_f"), sem("weighed"), sem("hot"),
                                                          sem("added"), sem("multiplied"))

        def rounds(engine, body):
            for r in range(RING):
                body(r, r, 0)
            last = steps // RING - 1
            with engine.Fori(1, last) as i:
                for r in range(RING):
                    body(i * RING + r, r, i)
            for r in range(RING):
                body(last * RING + r, r, last)

        def present(s):
            return not isinstance(s, int) or 0 <= s < steps

        block = ctx.enter_context(nc.Block())

        @block.sync
        def _(sp):
            sp.dma_start(dst_i[:], dst_tiles).then_inc(dst_in, 16)

            def load(s, r, i):
                if not present(s):
                    return
                unit = sp.value_load(unit_row[0:1, bass.ds(s, 1)], min_val=0, max_val=groups - 1)
                wait(sp, multiplied, s - (RING - 1))
                sp.dma_start(h[:, r, :, 0:HROW], h_d[unit].rearrange("p (t k) -> p t k", t=T)).then_inc(loaded[r], 16)

            rounds(sp, load)

        @block.scalar
        def _(act):
            def store(s, r, i):
                slot = act.value_load(slot_row[0:1, bass.ds(s, 1)], min_val=0, max_val=sums_d.shape[0] - 1)
                act.wait_ge(added, s + 1)
                act.dma_start(sums_d[slot], acc[:, r, :]).then_inc(stored[r], 16)

            rounds(act, store)
            for r in range(RING):
                act.wait_ge(stored[r], 16 * (steps // RING))

        @block.gpsimd
        def _(pool):
            pool.wait_ge(dst_in, 16)
            nc.gpsimd.tensor_copy(dst[:], dst_i[:]).then_inc(dst_f, 1)
            nc.gpsimd.memset(h[:, :, :, HROW:HROW + 1], 1.0).then_inc(dst_f, 1)
            pool.wait_ge(dst_f, 2)

            def body(s, r, i):
                unit = pool.value_load(unit_row[0:1, bass.ds(s, 1)], min_val=0, max_val=groups - 1)
                wait(pool, hot, s - 1)
                nc.gpsimd.tensor_tensor(rel[:, r % 2, :], dst[:, bass.ds(unit * T, T)],
                                        b128[:, bass.ds(s, 1)].broadcast_to([P, T]), ALU.subtract).then_inc(weighed, 1)
                pool.wait_ge(loaded[r], (i + 1) * 16)
                nc.gpsimd.tensor_tensor(
                    headed[r], headed[r], bc(weights_of_edges[:, bass.ds(unit * T, T), :], 3, HW + 1),
                    ALU.mult).then_inc(weighed, 1)

            rounds(pool, body)

        @block.vector
        def _(dve):
            def hots(s, r, i):
                if not present(s):
                    return
                dve.wait_ge(weighed, s * 2 + 1)
                wait(dve, multiplied, s - 1)
                nc.vector.tensor_tensor(onehot[:, r % 2], bc(iota[:], 1, T), bc(rel[:, r % 2, :], 2, P),
                                        ALU.is_equal).then_inc(hot, 1)

            def add(s, r, i):
                dve.wait_ge(multiplied, s + 1)
                wait(dve, stored[r], i * 16)
                wait(dve, added, s)
                if isinstance(s, int) and s == 0:
                    nc.vector.tensor_copy(acc[:, 0, :], ps[0][:, 0:HROW + 1]).then_inc(added, 1)
                else:
                    nc.vector.scalar_tensor_tensor(acc[:, r, :], acc[:, (r - 1) % RING, :], keep[:, bass.ds(s, 1)],
                                                   ps[r % 2][:, 0:HROW + 1], ALU.mult, ALU.add).then_inc(added, 1)

            def body(s, r, i):
                hots(s + 1, (r + 1) % RING, i + (r + 1) // RING)
                add(s, r, i)

            hots(0, 0, 0)
            rounds(dve, body)
            dve.wait_ge(added, steps)

        @block.tensor
        def _(pe):
            def body(s, r, i):
                pe.wait_ge(hot, s + 1)
                pe.wait_ge(weighed, s * 2 + 2)
                wait(pe, added, s - 1)
                for t in range(T):
                    last = nc.tensor.matmul(ps[r % 2][:, 0:HROW + 1], onehot[:, r % 2, t, :],
                                            h[:, r, t, :], start=t == 0, stop=t == T - 1)
                last.then_inc(multiplied, 1)

            rounds(pe, body)


def norm_steps(nc, dve, d, z, centred, squares, stat, root, rinv, rooted, round_, out):
    mean = stat[:, CHUNK:2 * CHUNK]
    spread = stat[:, 0:CHUNK]

    def then(instruction):
        dve.wait_ge(d.sem, d.up(instruction))

    then(nc.vector.tensor_reduce(mean, z, AX, ALU.add))
    then(nc.vector.tensor_scalar(mean, mean, 1.0 / D, None, ALU.mult))
    then(nc.vector.tensor_tensor(centred, z, bc(mean, 2, D), ALU.subtract))
    then(nc.vector.tensor_tensor(squares, centred, centred, ALU.mult))
    then(nc.vector.tensor_reduce(spread, squares, AX, ALU.add))
    d.up(nc.vector.tensor_scalar(spread, spread, 1.0 / D, EPS, ALU.mult, ALU.add))
    dve.wait_ge(rooted, round_ + 1)
    then(nc.vector.reciprocal(rinv, root))
    then(nc.vector.tensor_tensor(out, centred, bc(rinv, 2, D), ALU.mult))


def middle(nc, xn, sums_d, factor_d, table, resid_d, w, w1, ident):
    chunks = xn.shape[0] // P // CHUNK
    with ExitStack() as ctx:
        def sb(n, shape, dt=F32):
            return ctx.enter_context(nc.sbuf_tensor(f"m_{n}", shape, dt))

        def sem(n):
            return ctx.enter_context(nc.semaphore(f"m_{n}"))

        x, x1, proj = (sb(n, [P, 2, CHUNK, D]) for n in ("x", "x1", "proj"))
        z, zc, zq = (sb(n, [P, CHUNK, D]) for n in ("z", "zc", "zq"))
        rest = sb("rest", [P, 2, CHUNK, D + 1])
        sums = sb("sums", [P, 2, CHUNK, HROW + 1])
        factor = sb("factor", [P, 2, CHUNK])
        count = [sb(f"count{i}", [P, 2, CHUNK]) for i in range(2)]
        den = sb("den", [P, CHUNK, HEADS])
        agg = sb("agg", [P, 2, CHUNK, HEADS, HW])
        stat, root, rinv = sb("stat", [P, 2 * CHUNK]), sb("root", [P, CHUNK]), sb("rinv", [P, CHUNK])
        wp_a, wp_b = sb("wp_a", [P, D]), sb("wp_b", [D - P, D])
        wl_a, wl_b = sb("wl_a", [P, 2 * D]), sb("wl_b", [CV, 2 * D])
        t_a, t_b = sb("t_a", [P, 2, P]), sb("t_b", [CV, 2, P])
        o = sb("o", [P, 2, CHUNK, 2 * D])
        pt = [ctx.enter_context(nc.psum_tensor(f"m_pt{i}", [P, 512], F32)) for i in range(2)]
        po = [ctx.enter_context(nc.psum_tensor(f"m_po{i}", [P, 512], F32)) for i in range(2)]
        zeroed, weights, scaled, averaged, normed, completed = (
            sem(n) for n in ("zeroed", "weights", "scaled", "averaged", "normed", "completed"))
        rooted, turned, copied, multiplied, moved = (
            sem(n) for n in ("rooted", "turned", "copied", "multiplied", "moved"))
        sums_in, x_in, factor_in, stored = ([sem(f"{n}{r}") for r in range(2)]
                                            for n in ("sums_in", "x_in", "factor_in", "stored"))
        AVERAGE, NORM, COMPLETE = 4, 10, 2
        SPREAD = 8
        ROOT_AT = 4
        xv = xn.rearrange("(c b p) f -> c p b f", b=CHUNK, p=P)
        tv = table.rearrange("(c b p) f -> c p b f", b=CHUNK, p=P)
        rv = resid_d.rearrange("(c b p) f -> c p b f", b=CHUNK, p=P)
        sums_v = sums_d[0:chunks * CHUNK].rearrange("(c b) p f -> c p b f", b=CHUNK)
        placements = []

        def place(lo, hi, row0, col0, source):
            n, m = source.shape
            cut = max(0, min(n, P - row0))
            if cut:
                placements.append((lo[row0:row0 + cut, col0:col0 + m], source[0:cut, :]))
            if cut < n:
                at = row0 + cut - P
                placements.append((hi[at:at + n - cut, col0:col0 + m], source[cut:n, :]))

        for hd in range(HEADS):
            place(wp_a, wp_b, hd * HW, 0, w["Wps"][hd * AS:(hd + 1) * AS, :])
            for comp in range(3):
                place(wp_a, wp_b, hd * HW + AS + comp * AV, CS + comp * CV, w["Wpv"][hd * AV:(hd + 1) * AV, :])
        for side, (ws, wv) in enumerate((("Wl1_0", "Wl1_1"), ("Wsc0", "Wsc1"))):
            place(wl_a, wl_b, 0, side * D, w1[ws])
            for comp in range(3):
                place(wl_a, wl_b, CS + comp * CV, side * D + CS + comp * CV, w1[wv])

        def base(c):
            return 0 if isinstance(c, int) and c == 0 else c * (2 * CHUNK) - CHUNK

        def rows_base(c):
            return base(c + 1) + (0 if isinstance(c, int) and c == chunks - 1 else CHUNK)

        def present(c):
            return not isinstance(c, int) or c >= 0

        block = ctx.enter_context(nc.Block())

        @block.sync
        def _(sp):
            sp.wait_ge(zeroed, 4)
            for into, source in placements:
                sp.dma_start(into, source).then_inc(weights, 16)

            def store(c, r):
                if present(c):
                    sp.dma_start(tv[c], o[:, r, :, 0:D]).then_inc(stored[r], 16)
                    sp.dma_start(rv[c], rest[:, r]).then_inc(stored[r], 16)

            def body(c, r, j):
                wait(sp, averaged, (c - 1) * AVERAGE)
                sp.dma_start(sums[:, r], sums_v[c]).then_inc(sums_in[r], 16)
                wait(sp, normed, (c - 1) * NORM)
                sp.dma_start(x[:, r], xv[c]).then_inc(x_in[r], 16)
                wait(sp, completed, (c - 1) * COMPLETE)
                store(c - 2, r)
                sp.dma_start(factor[:, r], factor_d[c]).then_inc(factor_in[r], 16)

            in_pairs(sp, chunks, body)
            for r in range(2):
                sp.wait_ge(completed, (chunks - 1 + r) * COMPLETE)
                store(chunks - 2 + r, r)
            for r in range(2):
                sp.wait_ge(stored[r], 32 * (chunks // 2))

        @block.gpsimd
        def _(pool):
            for tile in (wp_a, wp_b, wl_a, wl_b):
                nc.gpsimd.memset(tile[:], 0.0).then_inc(zeroed, 1)

        @block.scalar
        def _(act):
            act.wait_ge(weights, 16 * len(placements))

            def roots(c):
                if present(c):
                    act.wait_ge(normed, c * NORM + SPREAD)
                    nc.scalar.activation(root[:], stat[:, 0:CHUNK], ACT.Sqrt).then_inc(rooted, 1)

            def blocks(first, move, between):
                for b in range(CHUNK + 1):
                    n = first + b
                    if b < CHUNK:
                        act.wait_ge(turned, n + 1)
                        wait(act, multiplied, n)
                        nc.scalar.activation(t_a[:, b % 2, :], pt[b % 2][:, 0:P], ACT.Copy)
                        nc.scalar.activation(t_b[:, b % 2, :], pt[b % 2][0:CV, P:2 * P], ACT.Copy).then_inc(copied, 1)
                    if b == ROOT_AT:
                        between()
                    if b >= 1:
                        act.wait_ge(multiplied, n)
                        move(b - 1, po[(b - 1) % 2]).then_inc(moved, 1)

            def averages(c, r):
                def move(b, bank):
                    if b == 0:
                        wait(act, normed, (c - 1) * NORM)
                    return nc.scalar.activation(proj[:, r, b, :], bank[:, 0:D], ACT.Copy)

                blocks(base(c), move, lambda: roots(c - 1))

            def rows(c, r, j):
                if not present(c):
                    return

                def move(b, bank):
                    if b == 0:
                        act.wait_ge(factor_in[r], (j + 1) * 16)
                        wait(act, stored[r], j * 32)
                    return nc.scalar.activation(o[:, r, b, :], bank[:, 0:2 * D], ACT.Copy, scale=factor[:, r, b:b + 1])

                blocks(rows_base(c), move, lambda: None)

            def body(c, r, j):
                averages(c, r)
                rows(c - 1, 1 - r, j if r else j - 1)

            in_pairs(act, chunks, body)
            roots(chunks - 1)
            rows(chunks - 1, 1, chunks // 2 - 1)

        @block.tensor
        def _(pe):
            pe.wait_ge(scaled, 3)

            def blocks(first, of, wa, wb, width):
                for b in range(CHUNK + 1):
                    if b < CHUNK:
                        nc.tensor.transpose(pt[b % 2][:, 0:P], of(b)[:, 0:P], ident[:])
                        nc.tensor.transpose(pt[b % 2][0:CV, P:2 * P], of(b)[:, P:D], ident[:]).then_inc(turned, 1)
                    if b >= 1:
                        n = first + (b - 1)
                        pe.wait_ge(copied, n + 1)
                        wait(pe, moved, n if b == 1 else n - 1)
                        into = po[(b - 1) % 2][:, 0:width]
                        nc.tensor.matmul(into, t_a[:, (b - 1) % 2, :], wa[:], start=True, stop=False)
                        nc.tensor.matmul(into, t_b[:, (b - 1) % 2, :], wb[:], start=False,
                                         stop=True).then_inc(multiplied, 1)

            def rows(c, r):
                if present(c):
                    pe.wait_ge(normed, (c + 1) * NORM)
                    blocks(rows_base(c), lambda b: x1[:, r, b, :], wl_a, wl_b, 2 * D)

            def body(c, r, j):
                pe.wait_ge(averaged, (c + 1) * AVERAGE)
                blocks(base(c), lambda b: agg[:, r, b].rearrange("p h k -> p (h k)"), wp_a, wp_b, D)
                rows(c - 1, 1 - r)

            in_pairs(pe, chunks, body)
            rows(chunks - 1, 1)

        @block.vector
        def _(dve):
            dve.wait_ge(weights, 16 * len(placements))
            inv8, inv32 = 1.0 / math.sqrt(CS), 1.0 / math.sqrt(CV)
            for tile, by in ((wl_a[0:CS], inv8), (wl_a[CS:P], inv32), (wl_b[:], inv32)):
                nc.vector.tensor_scalar(tile, tile, by, None, ALU.mult).then_inc(scaled, 1)

            def average(c, r, j):
                d = Count(averaged, c, AVERAGE)
                by_head = sums[:, r, :, 0:HROW].rearrange("p b (h k) -> p b h k", h=HEADS)
                dve.wait_ge(sums_in[r], (j + 1) * 16)
                wait(dve, averaged, c * AVERAGE)
                dve.wait_ge(averaged, d.up(nc.vector.tensor_scalar(den[:], by_head[:, :, :, HW], 1e-16, None,
                                                                   ALU.add)))
                k = d.up(nc.vector.reciprocal(den[:], den[:]))
                d.up(nc.vector.tensor_scalar(count[0][:, r], sums[:, r, :, HROW], 1.0, None, ALU.max))
                dve.wait_ge(averaged, k)
                d.up(nc.vector.tensor_tensor(agg[:, r], by_head[:, :, :, 0:HW], bc(den[:], 3, HW), ALU.mult))
                assert d.n == AVERAGE

            def normalise(c, r, j):
                if not present(c):
                    return
                d = Count(normed, c, NORM)
                dve.wait_ge(moved, base(c) + CHUNK)
                dve.wait_ge(x_in[r], (j + 1) * 16)
                dve.wait_ge(averaged, (c + 1) * AVERAGE)
                wait(dve, normed, c * NORM)
                wait(dve, completed, (c - 1) * COMPLETE)
                d.up(nc.vector.tensor_copy(count[1][:, r], count[0][:, r]))
                dve.wait_ge(normed, d.up(nc.vector.scalar_tensor_tensor(z[:], x[:, r], 2.0, proj[:, r], ALU.mult,
                                                                        ALU.add)))
                norm_steps(nc, dve, d, z[:], zc[:], zq[:], stat, root[:], rinv[:], rooted, c, x1[:, r])
                assert d.n == NORM

            def complete(c, r):
                if not present(c):
                    return
                d = Count(completed, c, COMPLETE)
                dve.wait_ge(moved, rows_base(c) + CHUNK)
                dve.wait_ge(normed, (c + 1) * NORM)
                d.up(nc.vector.tensor_tensor(rest[:, r, :, 0:D], x1[:, r], o[:, r, :, D:2 * D], ALU.add))
                d.up(nc.vector.tensor_copy(rest[:, r, :, D], count[1][:, r]))
                assert d.n == COMPLETE

            def body(c, r, j):
                average(c, r, j)
                normalise(c - 1, 1 - r, j if r else j - 1)
                complete(c - 2, r)

            in_pairs(dve, chunks, body)
            complete(chunks - 2, 0)
            normalise(chunks - 1, 1, chunks // 2 - 1)
            complete(chunks - 1, 1)


def edges1(nc, idx_d, y_d, rbf_d, table, unit_row, slot_row, b128, keep, w1, iota, sums_d):
    steps = b128.shape[1]
    groups = idx_d.shape[0]
    T = TILES
    with ExitStack() as ctx:
        def sb(n, shape, dt=F32):
            return ctx.enter_context(nc.sbuf_tensor(f"f_{n}", shape, dt))

        def sem(n):
            return ctx.enter_context(nc.semaphore(f"f_{n}"))

        def ring_sem(n, size):
            return [sem(f"{n}{r}") for r in range(size)]

        W0, W2, W1, W3 = 0, CS, CS + CV, 2 * CS + CV
        w_1, rest_1, w_2 = sb("w_1", [16, CS]), sb("rest_1", [16, CS]), sb("w_2", [CS, WE])
        parts_1, stack_1 = sb("parts_1", [16, 3, CS], BF16), sb("stack_1", [BASIS, CS], BF16)
        idx = sb("idx", [P, RING, 2 * T], I32)
        y, rbf = sb("y", [P, RING, T, 6]), sb("rbf", [BASIS, RING, GROUP], BF16)
        e = sb("e", [P, RING, T, D])
        hidden = sb("hidden", [CS, 2, GROUP])
        wy = sb("wy", [P, 2, T, MID])
        ey = sb("ey", [P, T, 3, CV])
        dot = sb("dot", [P, T, CV])
        we = sb("we", [P, T, CS])
        q = sb("q", [P, 2, T, ACC1])
        rel = sb("rel", [P, RING, T])
        onehot = sb("onehot", [P, RING, T, P])
        acc = sb("acc", [P, RING, ACC1])
        ps_h = [ctx.enter_context(nc.psum_tensor(f"f_ps_h{i}", [P, 512], F32)) for i in range(2)]
        ps_w = [ctx.enter_context(nc.psum_tensor(f"f_ps_w{i}", [P, 1024], F32)) for i in range(2)]
        ps_a = [ctx.enter_context(nc.psum_tensor(f"f_ps_a{i}", [P, 512], F32)) for i in range(2)]
        weights, scaled, parted, stacked = sem("weights"), sem("scaled"), sem("parted"), sem("stacked")
        idx_in, y_in, rbf_in, gathered, stored = (
            ring_sem(n, RING) for n in ("idx_in", "y_in", "rbf_in", "gathered", "stored"))
        hid, silu, radial, scalar_w, product, hot, multiplied, added, issued = (
            sem(n) for n in ("hid", "silu", "radial", "scalar_w", "product", "hot", "multiplied", "added", "issued"))
        HOT, PRODUCT = 2, 8

        def rounds(engine, body):
            for r in range(RING):
                body(r, r, 0)
            last = steps // RING - 1
            with engine.Fori(1, last) as i:
                for r in range(RING):
                    body(i * RING + r, r, i)
            for r in range(RING):
                body(last * RING + r, r, last)

        def present(s):
            return not isinstance(s, int) or 0 <= s < steps

        block = ctx.enter_context(nc.Block())

        @block.sync
        def _(sp):
            sp.dma_start(w_1[:], w1["Wfc1"]).then_inc(weights, 16)
            for at, source, n in ((W0, 0, CS), (W2, 2 * CS, CV), (W1, CS, CS), (W3, 2 * CS + CV, CV)):
                sp.dma_start(w_2[:, at:at + n], w1["Wfc2"][:, source:source + n]).then_inc(weights, 16)
            sp.wait_ge(parted, 5)
            stack_weight(sp, parts_1, stack_1, stacked)

            def body(s, r, i):
                unit = sp.value_load(unit_row[0:1, bass.ds(s, 1)], min_val=0, max_val=groups - 1)
                at = sp.snap(unit * GROUP)
                wait(sp, product, (s - (RING - 1)) * PRODUCT)
                sp.dma_start(idx[:, r, :], idx_d[unit]).then_inc(idx_in[r], 16)
                sp.dma_start(y[:, r], y_d[unit]).then_inc(y_in[r], 16)
                wait(sp, hid, s - (RING - 1))
                sp.dma_start(rbf[:, r, :], rbf_d[:, bass.ds(at, GROUP)]).then_inc(rbf_in[r], 16)

            rounds(sp, body)

        @block.gpsimd
        def _(pool):
            def gather(s, r, i):
                if not present(s):
                    return
                pool.wait_ge(idx_in[r], (i + 1) * 16)
                wait(pool, product, (s - (RING - 1)) * PRODUCT)
                pool.sem_inc(issued, 1)
                for t in range(T):
                    pool.indirect_dma_start(
                        out=e[:, r, t, :], out_offset=None, in_=table,
                        in_offset=bass.IndirectOffsetOnAxis(ap=idx[:, r, t:t + 1], axis=0),
                    ).then_inc(gathered[r], 16)

            rounds(pool, gather)

        @block.tensor
        def _(pe):
            pe.wait_ge(scaled, 1)
            pe.wait_ge(stacked, 16 * len(PAIRS))

            def hidden_layer(s, r, i):
                if not present(s):
                    return
                pe.wait_ge(rbf_in[r], (i + 1) * 16)
                wait(pe, silu, s - 1)
                nc.tensor.matmul(ps_h[r % 2][0:CS, :], stack_1[:], rbf[:, r, :],
                                 start=True, stop=True).then_inc(hid, 1)

            def radial_weights(s, r, i):
                if not present(s):
                    return
                pe.wait_ge(silu, s + 1)
                wait(pe, product, (s - 1) * PRODUCT)
                for t in range(T):
                    last = nc.tensor.matmul(ps_w[r % 2][:, t * 256:t * 256 + WE], hidden[:, r % 2, t * P:(t + 1) * P],
                                            w_2[:], start=True, stop=True)
                last.then_inc(radial, 1)

            def sums(s, r, i):
                slot = r % 2
                pe.wait_ge(hot, (s + 1) * HOT)
                pe.wait_ge(product, (s + 1) * PRODUCT)
                wait(pe, added, s - 1)
                for t in range(T):
                    last = nc.tensor.matmul(ps_a[slot][:, 0:ACC1], onehot[:, r, t, :], q[:, slot, t, :],
                                            start=t == 0, stop=t == T - 1)
                last.then_inc(multiplied, 1)

            def body(s, r, i):
                hidden_layer(s + 2, (r + 2) % RING, i + (r + 2) // RING)
                radial_weights(s + 1, (r + 1) % RING, i + (r + 1) // RING)
                sums(s, r, i)

            hidden_layer(0, 0, 0)
            hidden_layer(1, 1, 0)
            radial_weights(0, 0, 0)
            rounds(pe, body)

        @block.scalar
        def _(act):
            def activate(s, r, i):
                if not present(s):
                    return
                act.wait_ge(hid, s + 1)
                wait(act, radial, s - 1)
                nc.scalar.activation(hidden[:, r % 2, :], ps_h[r % 2][0:CS, :], ACT.Silu,
                                     scale=1.0 / math.sqrt(16.0)).then_inc(silu, 1)

            def with_scalar(s, r, i):
                if not present(s):
                    return
                act.wait_ge(radial, s + 1)
                act.wait_ge(y_in[r], (i + 1) * 16)
                wait(act, product, (s - 1) * PRODUCT)
                for t in range(T):
                    last = nc.scalar.activation(wy[:, r % 2, t, :], ps_w[r % 2][:, t * 256:t * 256 + MID], ACT.Copy,
                                                scale=y[:, r, t, 0:1])
                last.then_inc(scalar_w, 1)

            def store(s, r, i):
                if not present(s):
                    return
                slot = act.value_load(slot_row[0:1, bass.ds(s, 1)], min_val=0, max_val=sums_d.shape[0] - 1)
                act.wait_ge(added, s + 1)
                act.dma_start(sums_d[slot], acc[:, r, :]).then_inc(stored[r], 16)

            def body(s, r, i):
                activate(s + 2, (r + 2) % RING, i + (r + 2) // RING)
                with_scalar(s + 1, (r + 1) % RING, i + (r + 1) // RING)
                store(s - 2, (r - 2) % RING, None)

            activate(0, 0, 0)
            activate(1, 1, 0)
            with_scalar(0, 0, 0)
            rounds(act, body)
            store(steps - 2, RING - 2, None)
            store(steps - 1, RING - 1, None)
            for r in range(RING):
                act.wait_ge(stored[r], 16 * (steps // RING))

        @block.vector
        def _(dve):
            dve.wait_ge(weights, 16 * 5)
            nc.vector.tensor_scalar(w_2[:, 0:W3], w_2[:, 0:W3], 1.0 / math.sqrt(CS), None, ALU.mult)
            nc.vector.tensor_scalar(w_2[:, W3:WE], w_2[:, W3:WE], 1.0 / math.sqrt(3.0 * CS), None,
                                    ALU.mult).then_inc(scaled, 1)
            split_weight(nc, dve, w_1[:], rest_1[:], parts_1, parted)
            mult = lambda out, a, b: nc.vector.tensor_tensor(out, a, b, ALU.mult)
            plus = lambda out, a, b: nc.vector.tensor_tensor(out, a, b, ALU.add)

            def hots(s, r, i):
                if not present(s):
                    return
                d = Count(hot, s, HOT)
                dve.wait_ge(idx_in[r], (i + 1) * 16)
                k = d.up(nc.vector.tensor_tensor(rel[:, r, :], idx[:, r, T:2 * T],
                                                 b128[:, bass.ds(s, 1)].broadcast_to([P, T]), ALU.subtract))
                wait(dve, multiplied, s - (RING - 1))
                dve.wait_ge(hot, k)
                d.up(nc.vector.tensor_tensor(onehot[:, r], bc(iota[:], 1, T), bc(rel[:, r, :], 2, P),
                                             ALU.is_equal))
                assert d.n == HOT

            def products(s, r, i):
                d = Count(product, s, PRODUCT)
                slot = r % 2
                w = ps_w[slot][:].rearrange("p (t k) -> p t k", t=T)
                e0 = e[:, r, :, 0:CS]
                e1 = e[:, r, :, CS:D].rearrange("p t (x c) -> p t x c", x=3)
                yx = y[:, r, :, 1:4]
                vectors = q[:, slot, :, MID:ACC1].rearrange("p t (x c) -> p t x c", x=3)
                dve.wait_ge(gathered[r], (i + 1) * 16 * T)
                dve.wait_ge(y_in[r], (i + 1) * 16)
                k_ey = d.up(mult(ey[:], e1, bc(yx, 3, CV)))
                dve.wait_ge(scalar_w, s + 1)
                wait(dve, product, s * PRODUCT)
                k_we = d.up(mult(we[:], w[:, :, W1:W1 + CS], e0))
                dve.wait_ge(product, k_ey)
                k_dot = d.up(plus(dot[:], ey[:, :, 0, :], ey[:, :, 1, :]))
                wait(dve, multiplied, s - 1)
                d.up(mult(q[:, slot, :, 0:CS], wy[:, slot, :, 0:CS], e0))
                dve.wait_ge(product, k_dot)
                k_dot = d.up(plus(dot[:], dot[:], ey[:, :, 2, :]))
                d.up(mult(vectors[:, :, :, CS:MID], bc(wy[:, slot, :, CS:MID], 2, 3), e1))
                dve.wait_ge(product, k_dot)
                d.up(mult(q[:, slot, :, CS:MID], w[:, :, W3:W3 + CV], dot[:]))
                dve.wait_ge(product, k_we)
                d.up(mult(vectors[:, :, :, 0:CS], bc(we[:], 2, 3), bc(yx, 3, CS)))
                assert d.n == PRODUCT

            def add(s, r, i):
                if not present(s):
                    return
                slot = r % 2
                dve.wait_ge(multiplied, s + 1)
                wait(dve, stored[r], 16 * i)
                wait(dve, added, s)
                if isinstance(s, int) and s == 0:
                    nc.vector.tensor_copy(acc[:, 0, :], ps_a[0][:, 0:ACC1]).then_inc(added, 1)
                else:
                    nc.vector.scalar_tensor_tensor(acc[:, r, :], acc[:, (r - 1) % RING, :], keep[:, bass.ds(s, 1)],
                                                   ps_a[slot][:, 0:ACC1], ALU.mult, ALU.add).then_inc(added, 1)

            def body(s, r, i):
                hots(s + 1, (r + 1) % RING, i + (r + 1) // RING)
                products(s, r, i)
                add(s - 1, (r - 1) % RING, i + (r - 1) // RING)

            hots(0, 0, 0)
            rounds(dve, body)
            add(steps - 1, RING - 1, steps // RING - 1)
            dve.wait_ge(added, steps)


def final(nc, sums_d, factor_d, resid_d, out, w1, ident):
    blocks = resid_d.shape[0] // P
    chunks = blocks // CHUNK
    with ExitStack() as ctx:
        def sb(n, shape, dt=F32):
            return ctx.enter_context(nc.sbuf_tensor(f"l_{n}", shape, dt))

        def sem(n):
            return ctx.enter_context(nc.semaphore(f"l_{n}"))

        sums, means = sb("sums", [P, 2, CHUNK, ACC1]), sb("means", [P, 2, CHUNK, ACC1])
        share, factor = sb("share", [P, CHUNK]), sb("factor", [P, 2, CHUNK])
        square, gain = sb("square", [P, 2, CHUNK]), sb("gain", [P, CHUNK])
        resid = sb("resid", [P, 2, CHUNK, D + 1])
        conv = sb("conv", [P, 2, CHUNK, 1 + D])
        z, zc, zq, o = (sb("z", [P, CHUNK, D]), sb("zc", [P, CHUNK, D]), sb("zq", [P, CHUNK, D]),
                        sb("o", [P, 2, CHUNK, D]))
        stat, root, rinv = sb("stat", [P, 2 * CHUNK]), sb("root", [P, CHUNK]), sb("rinv", [P, CHUNK])
        w_s, w_v = sb("w_s", [MID, 1 + CS]), sb("w_v", [MID, CV])
        turned_rows = sb("turned_rows", [MID, 2, 512])
        pt = [ctx.enter_context(nc.psum_tensor(f"l_pt{i}", [P, 512], F32)) for i in range(2)]
        po = [ctx.enter_context(nc.psum_tensor(f"l_po{i}", [P, 512], F32)) for i in range(2)]
        weights, averaged, finished, rooted, turned, copied, multiplied, moved = (
            sem(n) for n in ("weights", "averaged", "finished", "rooted", "turned", "copied", "multiplied", "moved"))
        sums_in, rest_in, stored = ([sem(f"{n}{r}") for r in range(2)] for n in ("sums_in", "rest_in", "stored"))
        MEANS, FINISH = 4, 11
        SPREAD = 9
        ROOT_AT = 4
        block = ctx.enter_context(nc.Block())
        rv = resid_d.rearrange("(c b p) f -> c p b f", b=CHUNK, p=P)
        ov = out.rearrange("(c b p) f -> c p b f", b=CHUNK, p=P)
        sv = sums_d[0:blocks].rearrange("(c b) p f -> c p b f", b=CHUNK)

        def present(c):
            return not isinstance(c, int) or c >= 0

        @block.sync
        def _(sp):
            sp.dma_start(w_s[:, 0:1], w1["Wa"]).then_inc(weights, 16)
            sp.dma_start(w_s[:, 1:1 + CS], w1["Wl2_s"]).then_inc(weights, 16)
            sp.dma_start(w_v[:], w1["Wl2_v"]).then_inc(weights, 16)

            def store(c, r):
                if present(c):
                    sp.dma_start(ov[c], o[:, r]).then_inc(stored[r], 16)

            def body(c, r, j):
                wait(sp, averaged, (c - 1) * MEANS)
                sp.dma_start(sums[:, r], sv[c]).then_inc(sums_in[r], 16)
                wait(sp, finished, (c - 1) * FINISH)
                sp.dma_start(resid[:, r], rv[c]).then_inc(rest_in[r], 16)
                sp.dma_start(factor[:, r], factor_d[c]).then_inc(rest_in[r], 16)
                store(c - 2, r)

            in_pairs(sp, chunks, body)
            for r in range(2):
                sp.wait_ge(finished, (chunks - 1 + r) * FINISH)
                store(chunks - 2 + r, r)
            for r in range(2):
                sp.wait_ge(stored[r], 16 * (chunks // 2))

        @block.tensor
        def _(pe):
            pe.wait_ge(weights, 48)

            def product(n, slot, all_moved):
                pe.wait_ge(copied, n + 1)
                wait(pe, moved, n if all_moved else n - 1)
                rows, into = turned_rows[:, slot, :], po[slot]
                nc.tensor.matmul(into[:, 0:1 + CS], rows[:, 0:P], w_s[:], start=True, stop=True)
                for x in range(3):
                    at = 1 + CS + x * CV
                    last = nc.tensor.matmul(into[:, at:at + CV], rows[:, (1 + x) * P:(2 + x) * P], w_v[:],
                                            start=True, stop=True)
                last.then_inc(multiplied, 1)

            def body(c, r, j):
                pe.wait_ge(averaged, (c + 1) * MEANS)
                for b in range(CHUNK + 1):
                    if b < CHUNK:
                        for k in range(4):
                            last = nc.tensor.transpose(pt[b % 2][0:MID, k * P:(k + 1) * P],
                                                       means[:, r, b, k * MID:(k + 1) * MID], ident[:])
                        last.then_inc(turned, 1)
                    if b >= 1:
                        product(c * CHUNK + (b - 1), (b - 1) % 2, b == 1)

            in_pairs(pe, chunks, body)

        @block.scalar
        def _(act):
            def roots(c):
                if present(c):
                    act.wait_ge(finished, c * FINISH + SPREAD)
                    nc.scalar.activation(root[:], stat[:, 0:CHUNK], ACT.Sqrt).then_inc(rooted, 1)

            def body(c, r, j):
                for b in range(CHUNK + 1):
                    n = c * CHUNK + b
                    if b < CHUNK:
                        act.wait_ge(turned, n + 1)
                        wait(act, multiplied, n)
                        nc.scalar.activation(turned_rows[:, b % 2, :], pt[b % 2][0:MID, :],
                                             ACT.Copy).then_inc(copied, 1)
                    if b == ROOT_AT:
                        roots(c - 1)
                    if b >= 1:
                        act.wait_ge(multiplied, n)
                        if b == 1:
                            wait(act, finished, (c - 1) * FINISH)
                        nc.scalar.activation(conv[:, r, b - 1, :], po[(b - 1) % 2][:, 0:1 + D],
                                             ACT.Copy).then_inc(moved, 1)

            in_pairs(act, chunks, body)
            roots(chunks - 1)

        @block.vector
        def _(dve):
            def average(c, r, j):
                d = Count(averaged, c, MEANS)
                dve.wait_ge(rest_in[r], (j + 1) * 32)
                wait(dve, averaged, c * MEANS)
                k = d.up(nc.vector.tensor_tensor(square[:, r], factor[:, r], factor[:, r], ALU.mult))
                k2 = d.up(nc.vector.reciprocal(share[:], resid[:, r, :, D]))
                dve.wait_ge(averaged, k)
                d.up(nc.vector.tensor_scalar(square[:, r], square[:, r], 1.0 / MID, None, ALU.mult))
                dve.wait_ge(sums_in[r], (j + 1) * 16)
                wait(dve, turned, (c - 1) * CHUNK)
                dve.wait_ge(averaged, k2)
                d.up(nc.vector.tensor_tensor(means[:, r], sums[:, r], bc(share[:], 2, ACC1), ALU.mult))
                assert d.n == MEANS

            def finish(c, r, j):
                if not present(c):
                    return
                d = Count(finished, c, FINISH)
                dve.wait_ge(moved, (c + 1) * CHUNK)
                dve.wait_ge(averaged, (c + 1) * MEANS)
                wait(dve, finished, c * FINISH)
                dve.wait_ge(finished, d.up(nc.vector.tensor_tensor(gain[:], conv[:, r, :, 0], square[:, r],
                                                                   ALU.mult)))
                dve.wait_ge(finished, d.up(nc.vector.tensor_tensor(z[:], conv[:, r, :, 1:1 + D], bc(gain[:], 2, D),
                                                                   ALU.mult)))
                dve.wait_ge(finished, d.up(nc.vector.tensor_tensor(z[:], z[:], resid[:, r, :, 0:D], ALU.add)))
                wait(dve, stored[r], j * 16)
                norm_steps(nc, dve, d, z[:], zc[:], zq[:], stat, root[:], rinv[:], rooted, c, o[:, r])
                assert d.n == FINISH

            def body(c, r, j):
                average(c, r, j)
                finish(c - 1, 1 - r, j if r else j - 1)

            in_pairs(dve, chunks, body)
            finish(chunks - 1, 1, chunks // 2 - 1)


def message_passing(nc, xn, idx, harmonics, rbf, dst_windows, dst_tiles, first_dst, factor, w, w1, out):
    padded, groups = xn.shape[0], idx.shape[0]
    blocks = padded // P
    tiles = groups * TILES

    def dram(name, shape):
        return nc.dram_tensor(name, shape, F32, kind="Internal").ap()

    table_src, table_dst = dram("table_src", [padded, D]), dram("table_dst", [padded, D])
    h = dram("edge_values", [groups, P, TILES * HROW])
    sums0, sums1 = dram("sums0", [blocks + SPARE, P, HROW + 1]), dram("sums1", [blocks + SPARE, P, ACC1])
    table1, resid = dram("table1", [padded, D]), dram("resid", [padded, D + 1])

    basis = nc.dram_tensor("basis", [BASIS, rbf.shape[1]], BF16, kind="Internal").ap()

    with ExitStack() as ctx:
        ident = ctx.enter_context(nc.sbuf_tensor("ident", [P, P], F32))
        iota = ctx.enter_context(nc.sbuf_tensor("iota", [P, P], F32))
        constants(nc, ident, iota)

        splits(nc, rbf, basis)
        tables(nc, xn, table_src, table_dst, w, ident)
        steps = staircase_steps(groups, blocks)
        rows = (ctx.enter_context(nc.sbuf_tensor("unit_row", [1, steps], I32)),
                ctx.enter_context(nc.sbuf_tensor("slot_row", [1, steps], I32)),
                ctx.enter_context(nc.sbuf_tensor("b128", [P, steps], F32)),
                ctx.enter_context(nc.sbuf_tensor("keep", [P, steps], F32)))
        staircase(nc, "walk", first_dst, groups, blocks, *rows)
        with ExitStack() as inner:
            logits = inner.enter_context(nc.sbuf_tensor("logits", [P, tiles, HEADS], F32))
            edges(nc, idx, harmonics, basis, table_src, table_dst, h, w, ident, logits)
            softmax(nc, dst_windows, logits, ident)
            reduce_values(nc, h, *rows, dst_tiles, logits, sums0, iota)
        middle(nc, xn, sums0, factor, table1, resid, w, w1, ident)
        edges1(nc, idx, harmonics, basis, table1, *rows, w1, iota, sums1)
        final(nc, sums1, factor, resid, out, w1, ident)


_W0 = ["gamma_s", "beta_s", "gamma_v", "Ws_src", "Wv_src", "Ws_dst", "Wv_dst", "W_rbf", "W_alpha", "alpha_dot",
       "Ws_val", "Wv_val", "Wg", "w2_ss", "w2_sv", "w2_vs", "w2_vv0", "w2_vv1", "Ws_vlin", "Wv_vlin", "Wps", "Wpv"]
_W1 = ["Wfc1", "Wfc2", "Wsc0", "Wsc1", "Wl1_0", "Wl1_1", "Wl2_s", "Wl2_v", "Wa"]


def _layout(x, src, dst, edge_attr_16, edge_attr_4, node_vec1):
    n, n_edges = x.shape[0], src.shape[0]
    blocks = -(-n // (2 * P * CHUNK)) * 2 * CHUNK
    padded = blocks * P
    edges_p = -(-n_edges // (SEG_TILES * P)) * SEG_TILES * P

    def pad(a, size, fill=0):
        out = np.full((size,) + a.shape[1:], fill, a.dtype)
        out[:a.shape[0]] = a
        return out

    def tiled(a, tiles):
        return a.reshape((-1, tiles, P) + a.shape[1:]).swapaxes(1, 2)

    xp = pad(x, padded)
    by_component = xp[:, CS:].reshape(padded, CV, 3).transpose(0, 2, 1).reshape(padded, 3 * CV)
    s, d = pad(src, edges_p), pad(dst, edges_p, padded - 1)
    y = pad(edge_attr_4, edges_p)
    none = np.full(1, -1, d.dtype)
    window = np.concatenate([none, d, none])
    span = SEG_TILES * P

    def firsts(size):
        got = d[::size][1:]
        got = pad(got, -(-got.shape[0] // P) * P, 1 << 20)
        return got.reshape(-1, P).T

    return {
        "xn": np.concatenate([xp[:, :CS], by_component], 1),
        "idx": np.concatenate([tiled(s, TILES), tiled(d, TILES)], 2),
        "harmonics": tiled(y[:, [0, 1, 2, 3, 1, 2]], TILES),
        "rbf": pad(edge_attr_16, edges_p).T,
        "dst_windows": np.stack([window[q * span:q * span + span + 2] for q in range(edges_p // span)]),
        "dst_tiles": d.reshape(-1, P).T,
        "first_dst": firsts(GROUP),
        "factor": pad(node_vec1, padded).reshape(-1, CHUNK, P).swapaxes(1, 2),
    }


def kernel(**inputs):
    import concourse.bacc as _bacc
    from concourse import mybir as _mybir
    from concourse.bass_utils import run_bass_kernel_spmd as _run

    nc = _bacc.Bacc("TRN2", target_bir_lowering=False, num_devices=1)
    graph = [np.asarray(inputs[n]) for n in ("x", "src", "dst", "edge_attr_16", "edge_attr_4", "node_vec1")]
    n = graph[0].shape[0]
    arrays = {}

    def given(name, a):
        a = np.ascontiguousarray(a)
        arrays[name] = a
        return nc.dram_tensor(name, a.shape, _mybir.dt.from_np(a.dtype), kind="ExternalInput").ap()

    laid = [given(name, a) for name, a in _layout(*graph).items()]
    w = {k: given("w0_" + k, inputs["L0_gnn_" + k]) for k in _W0}
    w1 = {k: given("w1_" + k, inputs["L1_gnn_" + k]) for k in _W1}
    out = nc.dram_tensor("out", laid[0].shape, _mybir.dt.from_np(np.dtype("float32")), kind="ExternalOutput").ap()
    message_passing(nc, *laid, w, w1, out)
    got = _run(nc, [arrays], core_ids=[0]).results[0]["out"][:n]
    vectors = got[:, CS:].reshape(n, 3, CV).transpose(0, 2, 1).reshape(n, 3 * CV)
    return np.concatenate([got[:, :CS], vectors], 1)
```
